# Optimizing a Trainium2 kernel written in Bass

```python
import numpy as np
import jax
import jax.numpy as jnp

def _softmax(x, axis=-1):
    return jax.nn.softmax(x, axis=axis)

def _gelu(x):
    return jax.nn.gelu(x, approximate=True)

def _silu(x):
    return jax.nn.silu(x)

def _sigmoid(x):
    return jax.nn.sigmoid(x)

def _layernorm(x, axis=-1, eps=1e-05):
    m = jnp.mean(x, axis=axis, keepdims=True)
    v = jnp.var(x, axis=axis, keepdims=True)
    return (x - m) / jnp.sqrt(v + eps)

def _scatter_add(tgt, idx, src, axis=0):
    return tgt.at[idx].add(src)

def _segment_sum(src, seg, n):
    return jax.ops.segment_sum(src, seg, n)
kernel_name = 'mk_seq_preln_d2_jaxref_r4_d91c5f'

def setup_inputs(seed: int=0):
    np.random.seed(seed)
    _w = jnp.asarray

    def _L0_attn_setup():
        import jax, jax.numpy as jnp
        import numpy as np
        import math
        N_HEAD = 16
        V_HEAD = 32
        NOPE = 32
        ROPE_D = 64
        KEEP = 64
        EPS = 1e-06

        def _freqs(T, dim=ROPE_D, theta=10000.0):
            f = 1.0 / theta ** (jnp.arange(0, dim, 2, dtype=jnp.float32) / dim)
            t = jnp.arange(T, dtype=jnp.float32)
            a = jnp.outer(t, f)
            return (jnp.cos(a), jnp.sin(a))

        def _rope(x, cos, sin):
            S = x.shape[-2]
            c = cos[:S][None, None]
            s = sin[:S][None, None]
            x1, x2 = jnp.split(x, 2, axis=-1)
            return jnp.concatenate([x1 * c - x2 * s, x1 * s + x2 * c], axis=-1)

        def _rms(x, g, eps=EPS):
            return x * jax.lax.rsqrt(jnp.mean(x * x, axis=-1, keepdims=True) + eps) * g

        def _attn(q, k, v, causal):
            scale = 1.0 / math.sqrt(q.shape[-1])
            s = jnp.einsum('bhqd,bhkd->bhqk', q, k) * scale
            if causal:
                Tq, Tk = (s.shape[-2], s.shape[-1])
                mask = jnp.tril(jnp.ones((Tq, Tk), dtype=bool))
                s = jnp.where(mask, s, jnp.finfo(s.dtype).min)
            return jnp.einsum('bhqk,bhkd->bhqd', jax.nn.softmax(s, axis=-1), v)

        def _forward(x, w_cq, g_qnorm, w_dq_nope, w_dq_rope, w_ckv, g_kvnorm, w_dk_nope, w_dv, w_krope, w_imp, w_selk, w_selv, w_wink, w_winv, w_gate, w_proj):
            B, T, C = x.shape
            cos, sin = _freqs(T)
            nq = _rms(x @ w_cq, g_qnorm)
            q_nope = (nq @ w_dq_nope).reshape(B, T, N_HEAD, NOPE).transpose(0, 2, 1, 3)
            q_rope = (nq @ w_dq_rope).reshape(B, T, N_HEAD, ROPE_D).transpose(0, 2, 1, 3)
            q_rope = _rope(q_rope, cos, sin)
            q = jnp.concatenate([q_nope, q_rope], axis=-1)
            gate = jax.nn.softmax((x @ w_gate).mean(axis=1), axis=-1)
            ckv = _rms(x @ w_ckv, g_kvnorm)
            k_nope = (ckv @ w_dk_nope).reshape(B, T, N_HEAD, NOPE).transpose(0, 2, 1, 3)
            v1 = (ckv @ w_dv).reshape(B, T, N_HEAD, V_HEAD).transpose(0, 2, 1, 3)
            k_rope = (x @ w_krope).reshape(B, T, 1, ROPE_D).transpose(0, 2, 1, 3) / N_HEAD
            k_rope = _rope(k_rope, cos, sin)
            k1 = jnp.concatenate([k_nope, jnp.broadcast_to(k_rope, (B, N_HEAD, T, ROPE_D))], axis=-1)
            scores = (x @ w_imp)[..., 0]
            _, idx = jax.lax.top_k(scores, KEEP)
            idx = jnp.sort(idx, axis=1)
            sel = jnp.take_along_axis(x, idx[:, :, None], axis=1)
            ks = (sel @ w_selk).reshape(B, KEEP, N_HEAD, NOPE + ROPE_D).transpose(0, 2, 1, 3)
            vs = (sel @ w_selv).reshape(B, KEEP, N_HEAD, V_HEAD).transpose(0, 2, 1, 3)
            ks = jnp.concatenate([ks[..., :NOPE], _rope(ks[..., NOPE:], cos, sin)], axis=-1)
            kw = (x @ w_wink).reshape(B, T, N_HEAD, NOPE + ROPE_D).transpose(0, 2, 1, 3)
            vw = (x @ w_winv).reshape(B, T, N_HEAD, V_HEAD).transpose(0, 2, 1, 3)
            kw = jnp.concatenate([kw[..., :NOPE], _rope(kw[..., NOPE:], cos, sin)], axis=-1)
            a1 = _attn(q, k1, v1, causal=True)
            a2 = _attn(q, ks, vs, causal=False)
            a3 = _attn(q, kw, vw, causal=True)
            g = gate[:, :, None, None, None]
            out = g[:, 0] * a1 + g[:, 1] * a2 + g[:, 2] * a3
            out = out.transpose(0, 2, 1, 3).reshape(B, T, N_HEAD * V_HEAD)
            return out @ w_proj
        key = jax.random.key(seed)
        ks = jax.random.split(key, 20)
        B, T, C = (2, 256, 256)
        q_lora, kv_lora = (96, 32)
        std = 0.02

        def w(k, shape):
            return jax.random.normal(k, shape, dtype=jnp.float32) * std
        return {'x': jax.random.normal(ks[0], (B, T, C), dtype=jnp.float32), 'w_cq': w(ks[1], (C, q_lora)), 'g_qnorm': jnp.ones((q_lora,), jnp.float32), 'w_dq_nope': w(ks[2], (q_lora, N_HEAD * NOPE)), 'w_dq_rope': w(ks[3], (q_lora, N_HEAD * ROPE_D)), 'w_ckv': w(ks[4], (C, kv_lora)), 'g_kvnorm': jnp.ones((kv_lora,), jnp.float32), 'w_dk_nope': w(ks[5], (kv_lora, N_HEAD * NOPE)), 'w_dv': w(ks[6], (kv_lora, N_HEAD * V_HEAD)), 'w_krope': w(ks[7], (C, ROPE_D)), 'w_imp': w(ks[8], (C, 1)), 'w_selk': w(ks[9], (C, N_HEAD * (NOPE + ROPE_D))), 'w_selv': w(ks[10], (C, N_HEAD * V_HEAD)), 'w_wink': w(ks[11], (C, N_HEAD * (NOPE + ROPE_D))), 'w_winv': w(ks[12], (C, N_HEAD * V_HEAD)), 'w_gate': w(ks[13], (C, 3)), 'w_proj': w(ks[14], (N_HEAD * V_HEAD, C))}
    _L0_attn_in = _L0_attn_setup()

    def _L0_ffn_setup():
        import jax, jax.numpy as jnp
        import numpy as np
        import math
        BETA = 0.9
        THRESHOLD = 1.0
        NUM_STEPS = 5
        ALPHA = 2.0

        @jax.custom_vjp
        def spike_fn(u):
            return (u > 0).astype(u.dtype)

        def _spike_fwd(u):
            return (spike_fn(u), u)

        def _spike_bwd(u, g):
            s = jnp.pi / 2.0 * ALPHA * u
            return (g * (ALPHA / 2.0) / (1.0 + s * s),)
        spike_fn.defvjp(_spike_fwd, _spike_bwd)
        key = jax.random.key(seed)
        k1, k2, k3 = jax.random.split(key, 3)
        n_embd = 256
        x = jax.random.normal(k1, (4, 512, n_embd), dtype=jnp.float32)
        W_fc = jax.random.normal(k2, (4 * n_embd, n_embd), dtype=jnp.float32) / math.sqrt(n_embd)
        W_proj = jax.random.normal(k3, (n_embd, 4 * n_embd), dtype=jnp.float32) / math.sqrt(4 * n_embd)
        return {'x': x, 'W_fc': W_fc, 'W_proj': W_proj}
    _L0_ffn_in = _L0_ffn_setup()

    def _L1_attn_setup():
        import jax, jax.numpy as jnp
        import numpy as np
        D_MODEL = 256
        NUM_HEADS = 16
        D_K = D_MODEL // NUM_HEADS
        THETA = 10000.0

        def _rope(x, positions):
            d = x.shape[-1]
            inv_freq = THETA ** (-jnp.arange(0, d, 2, dtype=jnp.float32) / d)
            ang = positions[:, :, None].astype(jnp.float32) * inv_freq[None, None, :]
            cos = jnp.cos(ang)[:, None, :, :]
            sin = jnp.sin(ang)[:, None, :, :]
            x1 = x[..., 0::2]
            x2 = x[..., 1::2]
            r1 = x1 * cos - x2 * sin
            r2 = x1 * sin + x2 * cos
            out = jnp.stack([r1, r2], axis=-1).reshape(x.shape)
            return out
        key = jax.random.key(seed)
        k1, k2, k3 = jax.random.split(key, 3)
        B, S = (4, 512)
        x = jax.random.normal(k1, (B, S, D_MODEL), dtype=jnp.float32)
        W_qkv = jax.random.normal(k2, (3 * D_MODEL, D_MODEL), dtype=jnp.float32) * (1.0 / np.sqrt(D_MODEL))
        W_o = jax.random.normal(k3, (D_MODEL, D_MODEL), dtype=jnp.float32) * (1.0 / np.sqrt(D_MODEL))
        return {'x': x, 'W_qkv': W_qkv, 'W_o': W_o}
    _L1_attn_in = _L1_attn_setup()

    def _L1_ffn_setup():
        import jax, jax.numpy as jnp
        import numpy as np
        key = jax.random.key(seed)
        kx, kw = jax.random.split(key)
        x = jax.random.normal(kx, (32, 1024, 256), dtype=jnp.float32)
        weight = jax.random.normal(kw, (256, 256), dtype=jnp.float32) * 0.01
        return {'x': x, 'weight': weight}
    _L1_ffn_in = _L1_ffn_setup()
    _d = {'L0_attn_x': _L0_attn_in['x'], 'L0_attn_w_cq': _L0_attn_in['w_cq'], 'L0_attn_g_qnorm': _L0_attn_in['g_qnorm'], 'L0_attn_w_dq_nope': _L0_attn_in['w_dq_nope'], 'L0_attn_w_dq_rope': _L0_attn_in['w_dq_rope'], 'L0_attn_w_ckv': _L0_attn_in['w_ckv'], 'L0_attn_g_kvnorm': _L0_attn_in['g_kvnorm'], 'L0_attn_w_dk_nope': _L0_attn_in['w_dk_nope'], 'L0_attn_w_dv': _L0_attn_in['w_dv'], 'L0_attn_w_krope': _L0_attn_in['w_krope'], 'L0_attn_w_imp': _L0_attn_in['w_imp'], 'L0_attn_w_selk': _L0_attn_in['w_selk'], 'L0_attn_w_selv': _L0_attn_in['w_selv'], 'L0_attn_w_wink': _L0_attn_in['w_wink'], 'L0_attn_w_winv': _L0_attn_in['w_winv'], 'L0_attn_w_gate': _L0_attn_in['w_gate'], 'L0_attn_w_proj': _L0_attn_in['w_proj'], 'L0_ffn_W_fc': _L0_ffn_in['W_fc'], 'L0_ffn_W_proj': _L0_ffn_in['W_proj'], 'L1_attn_W_qkv': _L1_attn_in['W_qkv'], 'L1_attn_W_o': _L1_attn_in['W_o'], 'L1_ffn_weight': _L1_ffn_in['weight']}
    _x0 = _d['L0_attn_x']
    _d['L0_attn_x'] = jax.random.normal(jax.random.fold_in(jax.random.key(seed), 1), (8, 512, 256), dtype=_x0.dtype)
    del _x0
    return _d

def reference(L0_attn_x, L0_attn_w_cq, L0_attn_g_qnorm, L0_attn_w_dq_nope, L0_attn_w_dq_rope, L0_attn_w_ckv, L0_attn_g_kvnorm, L0_attn_w_dk_nope, L0_attn_w_dv, L0_attn_w_krope, L0_attn_w_imp, L0_attn_w_selk, L0_attn_w_selv, L0_attn_w_wink, L0_attn_w_winv, L0_attn_w_gate, L0_attn_w_proj, L0_ffn_W_fc, L0_ffn_W_proj, L1_attn_W_qkv, L1_attn_W_o, L1_ffn_weight):

    def _L0_attn_ref(x, w_cq, g_qnorm, w_dq_nope, w_dq_rope, w_ckv, g_kvnorm, w_dk_nope, w_dv, w_krope, w_imp, w_selk, w_selv, w_wink, w_winv, w_gate, w_proj):
        import jax, jax.numpy as jnp
        import numpy as np
        import math
        N_HEAD = 16
        V_HEAD = 32
        NOPE = 32
        ROPE_D = 64
        KEEP = 64
        EPS = 1e-06

        def _freqs(T, dim=ROPE_D, theta=10000.0):
            f = 1.0 / theta ** (jnp.arange(0, dim, 2, dtype=jnp.float32) / dim)
            t = jnp.arange(T, dtype=jnp.float32)
            a = jnp.outer(t, f)
            return (jnp.cos(a), jnp.sin(a))

        def _rope(x, cos, sin):
            S = x.shape[-2]
            c = cos[:S][None, None]
            s = sin[:S][None, None]
            x1, x2 = jnp.split(x, 2, axis=-1)
            return jnp.concatenate([x1 * c - x2 * s, x1 * s + x2 * c], axis=-1)

        def _rms(x, g, eps=EPS):
            return x * jax.lax.rsqrt(jnp.mean(x * x, axis=-1, keepdims=True) + eps) * g

        def _attn(q, k, v, causal):
            scale = 1.0 / math.sqrt(q.shape[-1])
            s = jnp.einsum('bhqd,bhkd->bhqk', q, k) * scale
            if causal:
                Tq, Tk = (s.shape[-2], s.shape[-1])
                mask = jnp.tril(jnp.ones((Tq, Tk), dtype=bool))
                s = jnp.where(mask, s, jnp.finfo(s.dtype).min)
            return jnp.einsum('bhqk,bhkd->bhqd', jax.nn.softmax(s, axis=-1), v)

        def _forward(x, w_cq, g_qnorm, w_dq_nope, w_dq_rope, w_ckv, g_kvnorm, w_dk_nope, w_dv, w_krope, w_imp, w_selk, w_selv, w_wink, w_winv, w_gate, w_proj):
            B, T, C = x.shape
            cos, sin = _freqs(T)
            nq = _rms(x @ w_cq, g_qnorm)
            q_nope = (nq @ w_dq_nope).reshape(B, T, N_HEAD, NOPE).transpose(0, 2, 1, 3)
            q_rope = (nq @ w_dq_rope).reshape(B, T, N_HEAD, ROPE_D).transpose(0, 2, 1, 3)
            q_rope = _rope(q_rope, cos, sin)
            q = jnp.concatenate([q_nope, q_rope], axis=-1)
            gate = jax.nn.softmax((x @ w_gate).mean(axis=1), axis=-1)
            ckv = _rms(x @ w_ckv, g_kvnorm)
            k_nope = (ckv @ w_dk_nope).reshape(B, T, N_HEAD, NOPE).transpose(0, 2, 1, 3)
            v1 = (ckv @ w_dv).reshape(B, T, N_HEAD, V_HEAD).transpose(0, 2, 1, 3)
            k_rope = (x @ w_krope).reshape(B, T, 1, ROPE_D).transpose(0, 2, 1, 3) / N_HEAD
            k_rope = _rope(k_rope, cos, sin)
            k1 = jnp.concatenate([k_nope, jnp.broadcast_to(k_rope, (B, N_HEAD, T, ROPE_D))], axis=-1)
            scores = (x @ w_imp)[..., 0]
            _, idx = jax.lax.top_k(scores, KEEP)
            idx = jnp.sort(idx, axis=1)
            sel = jnp.take_along_axis(x, idx[:, :, None], axis=1)
            ks = (sel @ w_selk).reshape(B, KEEP, N_HEAD, NOPE + ROPE_D).transpose(0, 2, 1, 3)
            vs = (sel @ w_selv).reshape(B, KEEP, N_HEAD, V_HEAD).transpose(0, 2, 1, 3)
            ks = jnp.concatenate([ks[..., :NOPE], _rope(ks[..., NOPE:], cos, sin)], axis=-1)
            kw = (x @ w_wink).reshape(B, T, N_HEAD, NOPE + ROPE_D).transpose(0, 2, 1, 3)
            vw = (x @ w_winv).reshape(B, T, N_HEAD, V_HEAD).transpose(0, 2, 1, 3)
            kw = jnp.concatenate([kw[..., :NOPE], _rope(kw[..., NOPE:], cos, sin)], axis=-1)
            a1 = _attn(q, k1, v1, causal=True)
            a2 = _attn(q, ks, vs, causal=False)
            a3 = _attn(q, kw, vw, causal=True)
            g = gate[:, :, None, None, None]
            out = g[:, 0] * a1 + g[:, 1] * a2 + g[:, 2] * a3
            out = out.transpose(0, 2, 1, 3).reshape(B, T, N_HEAD * V_HEAD)
            return out @ w_proj
        return _forward(x, w_cq, g_qnorm, w_dq_nope, w_dq_rope, w_ckv, g_kvnorm, w_dk_nope, w_dv, w_krope, w_imp, w_selk, w_selv, w_wink, w_winv, w_gate, w_proj)

    def _L0_ffn_ref(x, W_fc, W_proj):
        import jax, jax.numpy as jnp
        import numpy as np
        import math
        BETA = 0.9
        THRESHOLD = 1.0
        NUM_STEPS = 5
        ALPHA = 2.0

        @jax.custom_vjp
        def spike_fn(u):
            return (u > 0).astype(u.dtype)

        def _spike_fwd(u):
            return (spike_fn(u), u)

        def _spike_bwd(u, g):
            s = jnp.pi / 2.0 * ALPHA * u
            return (g * (ALPHA / 2.0) / (1.0 + s * s),)
        spike_fn.defvjp(_spike_fwd, _spike_bwd)
        h = jnp.square(jax.nn.relu(jnp.einsum('bsd,fd->bsf', x, W_fc)))
        y = jnp.einsum('bsf,df->bsd', h, W_proj)

        def step(mem, _):
            reset = jax.lax.stop_gradient(spike_fn(mem - THRESHOLD))
            mem_new = BETA * mem + y - reset * THRESHOLD
            spk = spike_fn(mem_new - THRESHOLD)
            return (mem_new, spk)
        mem0 = jnp.zeros_like(y)
        _, spks = jax.lax.scan(step, mem0, None, length=NUM_STEPS)
        return jnp.sum(spks, axis=0) / NUM_STEPS

    def _L1_attn_ref(x, W_qkv, W_o):
        import jax, jax.numpy as jnp
        import numpy as np
        D_MODEL = 256
        NUM_HEADS = 16
        D_K = D_MODEL // NUM_HEADS
        THETA = 10000.0

        def _rope(x, positions):
            d = x.shape[-1]
            inv_freq = THETA ** (-jnp.arange(0, d, 2, dtype=jnp.float32) / d)
            ang = positions[:, :, None].astype(jnp.float32) * inv_freq[None, None, :]
            cos = jnp.cos(ang)[:, None, :, :]
            sin = jnp.sin(ang)[:, None, :, :]
            x1 = x[..., 0::2]
            x2 = x[..., 1::2]
            r1 = x1 * cos - x2 * sin
            r2 = x1 * sin + x2 * cos
            out = jnp.stack([r1, r2], axis=-1).reshape(x.shape)
            return out
        B, S, _ = x.shape
        H, dk = (NUM_HEADS, D_K)
        qkv = jnp.einsum('bsd,ed->bse', x, W_qkv)
        qkv = qkv.reshape(B, S, 3, H, dk).transpose(2, 0, 3, 1, 4)
        q, k, v = (qkv[0], qkv[1], qkv[2])
        positions = jnp.broadcast_to(jnp.arange(S)[None, :], (B, S))
        q = _rope(q, positions)
        k = _rope(k, positions)
        scores = jnp.einsum('bhqd,bhkd->bhqk', q, k) / jnp.sqrt(jnp.float32(dk))
        causal = jnp.tril(jnp.ones((S, S), dtype=bool))
        scores = jnp.where(causal[None, None, :, :], scores, -jnp.inf)
        attn = jax.nn.softmax(scores, axis=-1)
        out = jnp.einsum('bhqk,bhkd->bhqd', attn, v)
        out = out.transpose(0, 2, 1, 3).reshape(B, S, H * dk)
        return jnp.einsum('bsd,ed->bse', out, W_o)

    def _L1_ffn_ref(x, weight):
        import jax, jax.numpy as jnp
        import numpy as np
        b_weight = jnp.sign(weight)
        return jnp.einsum('bsi,oi->bso', x, b_weight)
    x = L0_attn_x
    x = x + _L0_attn_ref(_layernorm(x, axis=-1), L0_attn_w_cq, L0_attn_g_qnorm, L0_attn_w_dq_nope, L0_attn_w_dq_rope, L0_attn_w_ckv, L0_attn_g_kvnorm, L0_attn_w_dk_nope, L0_attn_w_dv, L0_attn_w_krope, L0_attn_w_imp, L0_attn_w_selk, L0_attn_w_selv, L0_attn_w_wink, L0_attn_w_winv, L0_attn_w_gate, L0_attn_w_proj)
    x = x + _L0_ffn_ref(_layernorm(x, axis=-1), L0_ffn_W_fc, L0_ffn_W_proj)
    x = x + _L1_attn_ref(_layernorm(x, axis=-1), L1_attn_W_qkv, L1_attn_W_o)
    x = x + _L1_ffn_ref(_layernorm(x, axis=-1), L1_ffn_weight)
    return x

_drawn_inputs = setup_inputs


def setup_inputs(seed=0):
    import zlib

    import numpy as np

    out = dict(_drawn_inputs(seed))
    spreads = {'L0_attn_g_qnorm': (1.0, 0.6), 'L0_attn_g_kvnorm': (1.0, 0.6)}
    factors = {'L0_attn_w_cq': 8.0,
     'L0_attn_w_dq_nope': 8.0,
     'L0_attn_w_dq_rope': 8.0,
     'L0_attn_w_ckv': 7.661,
     'L0_attn_w_dk_nope': 8.0,
     'L0_attn_w_dv': 7.737,
     'L0_attn_w_krope': 8.0,
     'L0_attn_w_imp': 3.329,
     'L0_attn_w_selk': 8.0,
     'L0_attn_w_selv': 3.236,
     'L0_attn_w_wink': 8.0,
     'L0_attn_w_winv': 4.258,
     'L0_attn_w_gate': 8.0,
     'L0_attn_w_proj': 2.738}
    for name, (base, spread) in spreads.items():
        noise = np.random.default_rng([zlib.crc32(name.encode()), seed]).standard_normal(out[name].shape)
        drawn = base * np.exp(spread * noise) if base else spread * noise
        out[name] = jnp.asarray(drawn.astype(out[name].dtype))
    for name, factor in factors.items():
        out[name] = (out[name] * factor).astype(out[name].dtype)
    return out
```

```python
from contextlib import ExitStack

import numpy as np

import concourse.bass as bass
from concourse import mybir

F32 = mybir.dt.float32
BF16 = mybir.dt.bfloat16
ALU = mybir.AluOpType
ACT = mybir.ActivationFunctionType
AX = mybir.AxisListType

P = 128
B, T, C = 8, 512, 256
NT = T // P
NC = C // P
H = 16
HG = 4
NG = H // HG
QL, KVL = 96, 32
NOPE, ROPE, VD = 32, 64, 32
D0 = NOPE + ROPE
KEEP = 64
FF = 1024
NF = FF // P
SM_W = QL + KVL + ROPE + 3
D1 = 16
DP = 32
NEG = -1.0e30
Q_SCALE = float(D0) ** -0.5
LN_EPS, RMS_EPS = 1e-5, 1e-6

NWORK, NTR, NOUT = 4, 2, 2
NP = 8
TRANS_LAG = 5
PV_LAG = 2
PIECE_SLOT = 8
TR_PIECE_LAG = 2



def units_of_group0():
    out = []
    for kind in range(6):
        for h in range(HG):
            if kind == 0:
                u = dict(mm=[(h, "k1", 64, 512, 0, 3)], mask=[384], segs=[(0, 512)],
                         blocks=[(k * P, "v1", h, 3, k) for k in range(4)])
            elif kind == 1:
                u = dict(mm=[(h, "kw", 0, 512, 0, 3)], mask=[384], segs=[(0, 512)],
                         blocks=[(k * P, "vw", h, 3, k) for k in range(4)])
            elif kind == 2:
                u = dict(mm=[(h, "k1", 0, 448, 0, 2)], mask=[320], segs=[(0, 64), (64, 448)],
                         blocks=[(0, "vs", h, 2, 0)] + [(64 + k * P, "v1", h, 2, k) for k in range(3)])
            elif kind == 3:
                u = dict(mm=[(h, "k1", 0, 64, 0, 3), (h, "kw", 0, 384, 64, 2)], mask=[320],
                         segs=[(0, 64), (64, 448)],
                         blocks=[(0, "vs", h, 3, 0)] + [(64 + k * P, "vw", h, 2, k) for k in range(3)])
            elif kind == 4:
                u = dict(mm=[(h, "k1", 0, 320, 0, 1), (h, "kw", 0, 128, 320, 0)], mask=[192, 320],
                         segs=[(0, 64), (64, 320), (320, 448)],
                         blocks=[(0, "vs", h, 1, 0), (64, "v1", h, 1, 0), (192, "v1", h, 1, 1),
                                 (320, "vw", h, 0, 0)])
            else:
                u = dict(mm=[(h, "k1", 0, 192, 0, 0), (h, "kw", 0, 256, 192, 1)], mask=[64, 320],
                         segs=[(0, 64), (64, 192), (192, 448)],
                         blocks=[(0, "vs", h, 0, 0), (64, "v1", h, 0, 0), (192, "vw", h, 1, 0),
                                 (320, "vw", h, 1, 1)])
            u["kind"], u["slot"] = kind, h
            out.append(u)
    return out


def units_of_group1():
    out = []
    for h in range(HG):
        out.append(dict(kind=0, slot=h, mm=[(h, "k", 0, 512, 0, 3)], mask=[384], segs=[(0, 512)],
                        blocks=[(k * P, "v", h, 3, k) for k in range(4)]))
    for h in range(HG):
        out.append(dict(kind=1, slot=h, mm=[(h, "k", 0, 384, 0, 2), (h, "k", 0, 128, 384, 0)], mask=[256, 384],
                        segs=[(0, 384), (384, 512)],
                        blocks=[(k * P, "v", h, 2, k) for k in range(3)] + [(384, "v", h, 0, 0)]))
    for pair in range(2):
        a, b = 2 * pair, 2 * pair + 1
        out.append(dict(kind=2, slot=pair, mm=[(a, "k", 0, 256, 0, 1), (b, "k", 0, 256, 256, 1)], mask=[128, 384],
                        segs=[(0, 256), (256, 512)],
                        blocks=[(0, "v", a, 1, 0), (256, "v", b, 1, 0), (128, "v", a, 1, 1), (384, "v", b, 1, 1)]))
    return out


UNITS = [units_of_group0(), units_of_group1()]
NU = [len(u) for u in UNITS]
KINDS = [6, 3]
UNIT0 = [0, NG * NU[0]]
KIND0 = [0, NG * KINDS[0]]
GATES = [slice(1, 2), slice(2, 3), slice(0, 2), slice(0, 3, 2), slice(0, 3), slice(0, 3)]

PIECES = [(what, t) for t in range(NT) for what in ("q", "kw", "nv")] + [("sel", 0)]
NPIECE = len(PIECES)


def attention_steps(layer):
    n, steps = NG * NU[layer], []
    if layer == 0:
        for s in range(NPIECE + TR_PIECE_LAG):
            if s < NPIECE:
                steps.append(("piece", 0, s))
            if s >= TR_PIECE_LAG:
                steps.append(("piece_tr", 0, s - TR_PIECE_LAG))
    last = {}
    for j in range(n):
        last[(j // NU[layer], UNITS[layer][j % NU[layer]]["kind"])] = j
    for i in range(n + TRANS_LAG + PV_LAG):
        if i < n:
            steps.append(("scores", UNIT0[layer] + i))
            g, s = i // NU[0], i % NU[0] - PIECE_SLOT
            if layer == 0 and g + 1 < NG:
                if 0 <= s < NPIECE:
                    steps.append(("piece", g + 1, s))
                if 0 <= s - TR_PIECE_LAG < NPIECE:
                    steps.append(("piece_tr", g + 1, s - TR_PIECE_LAG))
        if 0 <= i - TRANS_LAG < n:
            steps.append(("trans", UNIT0[layer] + i - TRANS_LAG))
        for (g, kind), j in last.items():
            if j == i - TRANS_LAG - PV_LAG:
                steps.append(("pv", g, kind))
    return steps


STEPS = [attention_steps(0), attention_steps(1)]


def unit(j):
    layer = int(j >= UNIT0[1])
    i = j - UNIT0[layer]
    return layer, i // NU[layer], UNITS[layer][i % NU[layer]]


class Banks:

    def __init__(self, n):
        self.n, self.uses, self.of = n, 0, {}
        self.full, self.read = [0] * n, [0] * n

    def use(self, name, readers=1):
        k = self.uses % self.n
        self.uses += 1
        free_at = self.read[k]
        self.full[k] += 1
        self.read[k] += readers
        self.of[name] = (k, free_at, self.full[k], self.read[k])


def plan_banks():
    work, tr, outs = Banks(NWORK), Banks(NTR), Banks(NOUT)

    def ln(i):
        for c in range(NC):
            work.use(("hT", i, c))

    def attention(layer):
        for s in STEPS[layer]:
            if s[0] == "scores":
                work.use(("scores", s[1]))
            elif s[0] == "trans":
                tr.use(("trans", s[1]))
            elif s[0] == "piece":
                work.use(s, {"q": 3, "kw": 3, "nv": 2, "sel": 4}[PIECES[s[2]][0]])
            elif s[0] == "piece_tr":
                tr.use(s)
        for g in range(NG):
            outs.use((layer, g))

    ln(0)
    for i in range(2):
        work.use(("small", i))
    for name in ("imp", "score_cols", "gate", "nqT", "ckvT", "pos", "selT"):
        work.use(name)
    attention(0)
    for i in range(2):
        work.use(("proj", i))
    ln(1)
    for f in range(NF):
        work.use(("fc", f))
    for i in range(2):
        work.use(("y", i))
    ln(2)
    for t in range(NT):
        work.use(("qk", t), 2)
        if t % 2:
            work.use(("v", t // 2))
        tr.use(("qT", t), 4)
        tr.use(("kT", t))
    attention(1)
    for i in range(2):
        work.use(("o", i))
    ln(3)
    for i in range(2):
        work.use(("sign", i))
    return work, tr, outs


def constants():
    pos = np.arange(T, dtype=np.float32)

    def tab(dim):
        f = (1.0 / np.float32(10000.0) ** (np.arange(0, dim, 2, dtype=np.float32) / np.float32(dim))).astype(np.float32)
        a = np.outer(pos, f).astype(np.float32)
        tile = lambda m: np.ascontiguousarray(m.reshape(NT, P, -1).transpose(1, 0, 2))
        c, s = np.cos(a).astype(np.float32), np.sin(a).astype(np.float32)
        return tile(c), tile(np.concatenate([-s, s], 1))

    c0, s0 = tab(ROPE)
    c1, s1 = tab(D1)
    p = np.arange(P)
    f = np.float32
    return dict(
        cos0=c0, sin0=s0, cos1=c1, sin1=s1,
        ident=np.eye(P, dtype=f),
        causal=np.where(p[None, :] > p[:, None], f(NEG), f(0.0)).astype(f),
        before=(p[:, None] < p[None, :]).astype(f),
        earlier=((np.arange(7 * P)[None, :] - 3 * P) < p[:, None]).astype(f),
        ranks=np.broadcast_to(np.arange(KEEP, dtype=f), (P, KEEP)).copy(),
    )


CONST_NAMES = ["cos0", "sin0", "cos1", "sin1", "ident", "causal", "before", "earlier", "ranks"]
WEIGHT_NAMES = ["x", "w_small", "w_imp", "w_q", "w_nv", "w_kw", "w_sel", "w_proj", "g_q", "g_kv",
                "w_fc", "w_ffp", "w_qkv", "w_o", "w_sign"]


def build_program(nc, x, w_small, w_imp, w_q, w_nv, w_kw, w_sel, w_proj, g_q, g_kv,
                  w_fc, w_ffp, w_qkv, w_o, w_sign,
                  cos0, sin0, cos1, sin1, ident, causal, before, earlier, ranks, out):
    work, tr, outs = plan_banks()
    ctx = ExitStack()
    with ctx:
        def sb(name, shape, dt=F32):
            return ctx.enter_context(nc.sbuf_tensor(name, shape, dt))

        WS = sb("WS", [P, NC, SM_W])
        WIMP = sb("WIMP", [P, NC])
        WI = sb("WI", [P, NC, P])
        WQ = sb("WQ", [P, H * D0])
        WKW = sb("WKW", [P, 2, NC, 512])
        WSEL = sb("WSEL", [P, NC, 512])
        WP = sb("WP", [P, NG, C])
        GQ = sb("GQ", [P, QL])
        GK = sb("GK", [P, KVL])
        WFC = sb("WFC", [P, NC, FF])
        WFP = sb("WFP", [P, NF, C])
        WQKV = sb("WQKV", [P, NC, 3 * C])
        WO = sb("WO", [P, NG, C])
        WSG = sb("WSG", [P, NC, C])
        COS0, SIN0 = sb("COS0", [P, NT, 32]), sb("SIN0", [P, NT, 64])
        COS1, SIN1 = sb("COS1", [P, NT, 8]), sb("SIN1", [P, NT, 16])
        ID = sb("ID", [P, P])
        IDB = sb("IDB", [P, P], BF16)
        CAUSB = sb("CAUSB", [P, P], BF16)
        BEFB = sb("BEFB", [P, P], BF16)
        ONEB = sb("ONEB", [P, P], BF16)
        MEANW = sb("MEANW", [P, P])
        EARLY = sb("EARLY", [P, 7 * P])
        RANKS = sb("RANKS", [P, KEEP])
        MHALF = sb("MHALF", [P, 8])
        X0, X1, X2 = sb("X0", [P, NT, C]), sb("X1", [P, NT, C]), sb("X2", [P, NT, C])
        HN = sb("HN", [P, NT, C])
        HT = sb("HT", [P, NC, T])
        NQT = sb("NQT", [P, T])
        KR = sb("KR", [P, NT, ROPE])
        SMALL = sb("SMALL", [P, 2176])
        SM = SMALL[:, 0:4 * 196].rearrange("p (t c) -> p t c", t=NT)
        NCK = SMALL[:, 784:1296].rearrange("p (t c) -> p t c", t=NT)
        ROW = SMALL[:, 1296:1808]
        OH = SMALL[:, 1808:2064].rearrange("p (t c) -> p t c", t=NT)
        QK = SMALL[:, 0:2048].rearrange("p (n h d) -> p n h d", n=2, d=DP)
        SELT = sb("SELT", [P, NC, KEEP])
        BIG = sb("BIG", [P, 12800])
        o = 0
        QT, KW, K1 = [], [], []
        for par in range(2):
            QT.append(BIG[:, o:o + 2048].rearrange("p (h k) -> p h k", h=HG)); o += 2048
            KW.append(BIG[:, o:o + 2048].rearrange("p (h k) -> p h k", h=HG)); o += 2048
            K1.append(BIG[:, o:o + 2304].rearrange("p (h k) -> p h k", h=HG)); o += 2304
        QZ = BIG[:, 0:8192].rearrange("p (g h k) -> p g h k", g=NG, h=HG)
        KB = BIG[:, 8192:10240].rearrange("p (g k) -> p g k", g=NG)
        VP = BIG[:, 10240:12288].rearrange("p (t h d) -> p t h d", t=NT, d=DP)
        VV = sb("VV", [P, 2, NT, 256])
        VS = sb("VS", [KEEP, 2, P])
        TOK = sb("TOK", [P, 4, HG, D0])
        AB = sb("AB", [P, 2, 512])
        PR = sb("PR", [P, NP, 512])
        PT = sb("PT", [P, 2, HG, 512])
        OT = sb("OT", [P, NG, T])
        R2 = PT[:, :, :, :].rearrange("p a b c -> p (a b) c")
        STATE = PR[:, :, :].rearrange("p (n a) b -> p n (a b)", n=4)
        BN = sb("BN", [P, NT, 6]); MV = sb("MV", [P, NT, 2])
        VAR, YP, NA = sb("VAR", [P, 8]), sb("YP", [P, 8]), sb("NA", [P, 8])
        RSTD = sb("RSTD", [P, 8])
        SC, CG, CE = sb("SC", [P, NT]), sb("CG", [P, NT]), sb("CE", [P, NT])
        MF, MB, POS = sb("MF", [P, NT]), sb("MB", [P, NT], BF16), sb("POS", [P, NT])
        GS, GE, GG = sb("GS", [P, 3]), sb("GE", [P, 3]), sb("GG", [P, 3])
        GM, GD = sb("GM", [P, 1]), sb("GD", [P, 2])
        NM, RS = sb("NM", [P, NP, 4]), sb("RS", [P, NP, 4])
        RC, CF = sb("RC", [P, NP, 4]), sb("CF", [P, NP, 4])

        WB = [ctx.enter_context(nc.psum_tensor(f"work{k}", [P, 512], F32)) for k in range(NWORK)]
        TB = [ctx.enter_context(nc.psum_tensor(f"trans{k}", [P, 512], F32)) for k in range(NTR)]
        OB = [ctx.enter_context(nc.psum_tensor(f"outs{k}", [P, 512], F32)) for k in range(NOUT)]

        def sem(name):
            return ctx.enter_context(nc.semaphore(name))

        first_cleared = sem("work_full0")
        work_full = [first_cleared] + [sem(f"work_full{k}") for k in range(1, NWORK)]
        work_read = [sem(f"work_read{k}") for k in range(NWORK)]
        trans_full = [sem(f"trans_full{k}") for k in range(NTR)]
        trans_read = [sem(f"trans_read{k}") for k in range(NTR)]
        outs_read = [sem(f"outs_read{k}") for k in range(NOUT)]
        pv_done = sem("pv_done")
        var_ready = sem("var_ready")
        pow_done = sem("pow_done")
        h_ready = sem("h_ready")
        latents_ready = sem("latents_ready")
        kr_products = sem("kr_products")
        mask_ready = sem("mask_ready")
        onehot_ready = sem("onehot_ready")
        gate_in = sem("gate_in")
        gate_exp = sem("gate_exp")
        rope_products = sem("rope_products")
        tok_ready = sem("tok_ready")
        max_ready = sem("max_ready")
        coef_ready = sem("coef_ready")
        scaled = sem("scaled")
        squared = sem("squared")
        out_ready = sem("out_ready")
        zeroed = sem("zeroed")
        dve_step = sem("dve_step")
        kw_loaded = [sem("kw_loaded0"), sem("kw_loaded1")]
        sel_loaded = sem("sel_loaded")
        finished = sem("finished")
        cleared = range(first_cleared.num, finished.num + 1)
        next_sequence = sem("next_sequence")
        x_loaded = sem("x_loaded")
        x_stored = sem("x_stored")
        weights_loaded = sem("weights_loaded")
        set_up = sem("set_up")
        set_up_act = sem("set_up_act")

        block = ctx.enter_context(nc.Block())

        def full(e, use, bank):
            ring, sems, banks = bank
            k, _, f, _ = ring.of[use]
            e.wait_ge(sems[k], f)
            return banks[k]

        WORK, TRANS = (work, work_full, WB), (tr, trans_full, TB)

        def was_read(e, ring, sems, use):
            k, _, _, r = ring.of[use]
            e.wait_ge(sems[k], r)

        def evacuate_probabilities(e, copy, j):
            layer, g, u = unit(j)
            kind = KIND0[layer] + g * KINDS[layer] + u["kind"]
            if kind >= 2:
                e.wait_ge(pv_done, kind - 1)
            ps = full(e, ("trans", j), TRANS)
            copy(PT[:, kind % 2, u["slot"], :], ps[:, :]).then_inc(trans_read[tr.of[("trans", j)][0]], 1)

        loads = [(WS[:, :, :], w_small), (WIMP[:, :], w_imp), (WQ[0:QL, :], w_q), (WQ[QL:P, 0:1024], w_nv),
                 (GQ[:, :], g_q.partition_broadcast(P)), (GK[:, :], g_kv.partition_broadcast(P)),
                 (COS0[:, :, :], cos0), (SIN0[:, :, :], sin0), (COS1[:, :, :], cos1), (SIN1[:, :, :], sin1),
                 (ID[:, :], ident), (X2[:, 0, 0:P], causal), (X2[:, 1, 0:P], before),
                 (EARLY[:, :], earlier), (RANKS[:, :], ranks),
                 (WP[:, :, :], w_proj), (WFC[:, :, :], w_fc), (WFP[:, :, :], w_ffp), (WQKV[:, :, :], w_qkv),
                 (WO[:, :, :], w_o), (WSG[:, :, :], w_sign)]
        ALL_LOADED = 16 * len(loads)
        SET_UP = 10
        x_rows = x.rearrange("(n p) c -> p n c", p=P)
        out_rows = out.rearrange("(n p) c -> p n c", p=P)

        @block.sync
        def _(sp):
            sp.dma_start(X0[:, :, :], x_rows[:, 0:NT, :]).then_inc(x_loaded, 16)
            for dst, src in loads:
                sp.dma_start(dst, src).then_inc(weights_loaded, 16)
            with sp.Fori(0, B) as seq:
                for g in range(NG):
                    if g >= 2:
                        k, _, f, _ = work.of[("piece", g - 2, NPIECE - 2)]
                        sp.wait_ge(work_full[k], f)
                    sp.dma_start(WKW[:, g % 2, :, :], w_kw[g]).then_inc(kw_loaded[g % 2], 16)
                    if g >= 1:
                        k, _, f, _ = work.of[("piece", g - 1, NPIECE - 1)]
                        sp.wait_ge(work_full[k], f)
                    sp.dma_start(WSEL[:, :, :], w_sel[g]).then_inc(sel_loaded, 16)
                for i in range(2):
                    was_read(sp, work, work_read, ("proj", i))
                sp.dma_start(X0[:, :, :], x_rows[:, bass.ds(((seq + 1) % B) * NT, NT), :]).then_inc(x_loaded, 16)
                sp.wait_ge(out_ready, NT // 2)
                sp.dma_start(out_rows[:, bass.ds(seq * NT, NT), :], X2[:, :, :]).then_inc(x_stored, 16)
                sp.wait_ge(finished, 4)
                sp.sem_clear(cleared)
                sp.sem_inc(next_sequence, 1)
            sp.wait_ge(x_stored, 16 * (B + 1))
            sp.wait_ge(x_loaded, 16 * (B + 1))

        @block.tensor
        def _(pe):
            mm = nc.tensor.matmul

            def take(use, bank):
                ring, full_sems, banks, read_sems = bank
                k, free_at, _, _ = ring.of[use]
                if free_at > 0:
                    pe.wait_ge(read_sems[k], free_at)
                return banks[k], full_sems[k]

            W, R = (work, work_full, WB, work_read), (tr, trans_full, TB, trans_read)

            def transpose_rows(i):
                for c in range(NC):
                    ps, done = take(("hT", i, c), W)
                    for t in range(NT):
                        if c == 0:
                            pe.wait_ge(h_ready, NT * i + t + 1)
                        last = nc.tensor.transpose(ps[:, t * P:(t + 1) * P], HN[:, t, c * P:(c + 1) * P], ID[:, :])
                    last.then_inc(done, 1)

            def rows_transposed(i):
                for c in range(NC):
                    was_read(pe, work, work_read, ("hT", i, c))

            def piece(g, m):
                what, t = PIECES[m]
                ps, done = take(("piece", g, m), W)
                ht = lambda c: HT[:, c, t * P:(t + 1) * P]
                if what == "q":
                    last = mm(ps[:, 0:384], NQT[0:QL, t * P:(t + 1) * P], WQ[0:QL, g * 384:(g + 1) * 384],
                              start=True, stop=True)
                elif what == "kw":
                    if t == 0:
                        pe.wait_ge(kw_loaded[g % 2], 16 * (g // 2 + 1))
                    for c in range(NC):
                        last = mm(ps[:, 0:384], ht(c), WKW[:, g % 2, c, 0:384], start=(c == 0), stop=(c == NC - 1))
                elif what == "nv":
                    mm(ps[:, 0:256], NQT[QL:P, t * P:(t + 1) * P], WQ[QL:P, g * 256:(g + 1) * 256],
                       start=True, stop=True)
                    for c in range(NC):
                        last = mm(ps[:, 256:384], ht(c), WKW[:, g % 2, c, 384:512], start=(c == 0), stop=(c == NC - 1))
                else:
                    pe.wait_ge(sel_loaded, 16 * (g + 1))
                    for c in range(NC):
                        last = mm(ps[0:KEEP, 0:512], SELT[:, c, :], WSEL[:, c, :], start=(c == 0), stop=(c == NC - 1))
                last.then_inc(done, 1)

            def piece_transposes(g, m):
                what, t = PIECES[m]
                rows = KEEP if what == "sel" else P
                was_read(pe, work, work_read, ("piece", g, m))
                pe.wait_ge(tok_ready, 1 + g * NPIECE + m + 1)
                ps, done = take(("piece_tr", g, m), R)
                for h in range(HG):
                    last = nc.tensor.transpose(ps[0:D0, h * rows:(h + 1) * rows],
                                               TOK[0:rows, (g * NPIECE + m) % 4, h, :], ID[0:rows, 0:rows])
                last.then_inc(done, 1)

            def scores(j):
                layer, g, u = unit(j)
                ps, done = take(("scores", j), W)
                if layer == 0 and u["kind"] == 0 and u["slot"] == 0:
                    for m in range(NPIECE):
                        was_read(pe, tr, trans_read, ("piece_tr", g, m))
                for (h, src, k0, n, col, qt) in u["mm"]:
                    if layer == 0:
                        q = QT[g % 2][0:D0, h, qt * P:(qt + 1) * P]
                        k = (K1 if src == "k1" else KW)[g % 2][0:D0, h, k0:k0 + n]
                    else:
                        q = QZ[:, g, h, qt * P:(qt + 1) * P]
                        k = KB[:, g, k0:k0 + n]
                    masked = [c for c in u["mask"] if col <= c < col + n]
                    last = mm(ps[:, col:col + n], q, k, start=True, stop=not masked)
                    for c in masked:
                        last = mm(ps[:, c:c + P], IDB[:, :], CAUSB[:, :], start=False, stop=True)
                last.then_inc(done, 1)

            def transposes(j):
                layer, g, u = unit(j)
                pe.wait_ge(scaled, j + 1)
                ps, done = take(("trans", j), R)
                for b, blk in enumerate(u["blocks"]):
                    last = nc.tensor.transpose(ps[:, b * P:(b + 1) * P], PR[:, j % NP, blk[0]:blk[0] + P], ID[:, :])
                last.then_inc(done, 1)

            def values(layer, g, kind):
                group = [(i, u) for i, u in enumerate(UNITS[layer]) if u["kind"] == kind]
                for i, u in group:
                    was_read(pe, tr, trans_read, ("trans", UNIT0[layer] + g * NU[layer] + i))
                k, free_at, _, _ = outs.of[(layer, g)]
                if kind == 0 and free_at > 0:
                    pe.wait_ge(outs_read[k], free_at)
                last_kind = kind == KINDS[layer] - 1
                kpar = (KIND0[layer] + g * KINDS[layer] + kind) % 2
                for b in range(4):
                    for i, u in group:
                        _, src, h, qt, kt = u["blocks"][b]
                        rows = KEEP if src == "vs" else P
                        if src == "vs":
                            v = VS[:, g % 2, h * VD:(h + 1) * VD]
                        elif layer == 0:
                            off = 0 if src == "v1" else P
                            v = VV[:, g % 2, kt, off + h * VD:off + (h + 1) * VD]
                        else:
                            v = VP[:, kt, g * HG + h, :]
                        first = kind == 0 and b == 0
                        last = mm(OB[k][h * 32:(h + 1) * 32, qt * P:(qt + 1) * P], v,
                                  PT[0:rows, kpar, u["slot"], b * P:(b + 1) * P],
                                  start=first, stop=last_kind and b == 3, skip_group_check=True)
                last.then_inc(pv_done, 1)

            def attention(layer):
                for s in STEPS[layer]:
                    if s[0] == "piece":
                        piece(s[1], s[2])
                    elif s[0] == "piece_tr":
                        piece_transposes(s[1], s[2])
                    elif s[0] == "scores":
                        scores(s[1])
                    elif s[0] == "trans":
                        transposes(s[1])
                    else:
                        values(layer, s[1], s[2])

            def out_projection(name, layer, wt):
                for i in range(2):
                    ps, done = take((name, i), W)
                    for tt in range(2):
                        t = 2 * i + tt
                        for g in range(NG):
                            if i == 0 and tt == 0:
                                k, _, _, r = outs.of[(layer, g)]
                                pe.wait_ge(outs_read[k], r)
                            last = mm(ps[:, tt * C:(tt + 1) * C], OT[:, g, t * P:(t + 1) * P], wt[:, g, :],
                                      start=(g == 0), stop=(g == NG - 1))
                    last.then_inc(done, 1)

            pe.wait_ge(weights_loaded, ALL_LOADED)
            pe.wait_ge(set_up, SET_UP)
            pe.wait_ge(set_up_act, 1)
            with pe.Fori(0, B) as seq:
                transpose_rows(0)
                rows_transposed(0)
                for i in range(2):
                    ps, done = take(("small", i), W)
                    for tt in range(2):
                        t = 2 * i + tt
                        for c in range(NC):
                            last = mm(ps[:, tt * C:tt * C + SM_W], HT[:, c, t * P:(t + 1) * P], WS[:, c, :],
                                      start=(c == 0), stop=(c == NC - 1))
                    last.then_inc(done, 1)
                ps, done = take("imp", W)
                for c in range(NC):
                    last = mm(ps[:, :], WI[:, c, :], HT[:, c, :], start=(c == 0), stop=(c == NC - 1))
                last.then_inc(done, 1)
                ps, done = take("score_cols", W)
                was_read(pe, work, work_read, "imp")
                for t in range(NT):
                    last = nc.tensor.transpose(ps[:, t * P:(t + 1) * P], ROW[:, t * P:(t + 1) * P], ID[:, :])
                last.then_inc(done, 1)
                ps, done = take("gate", W)
                for i in range(2):
                    was_read(pe, work, work_read, ("small", i))
                for t in range(NT):
                    last = mm(ps[:, 0:3], MEANW[:, :], SM[:, t, SM_W - 3:SM_W], start=(t == 0), stop=(t == NT - 1))
                last.then_inc(done, 1)
                pe.wait_ge(latents_ready, 2 * NT)
                ps, done = take("nqT", W)
                for t in range(NT):
                    last = nc.tensor.transpose(ps[0:QL, t * P:(t + 1) * P], NCK[:, t, 0:QL], ID[:, :])
                last.then_inc(done, 1)
                ps, done = take("ckvT", W)
                for t in range(NT):
                    last = nc.tensor.transpose(ps[0:KVL, t * P:(t + 1) * P], NCK[:, t, QL:P], ID[:, :])
                last.then_inc(done, 1)
                ps, done = take("pos", W)
                pe.wait_ge(mask_ready, 1)
                for t in range(NT):
                    for s in range(t + 1):
                        last = mm(ps[:, t:t + 1], (BEFB if s == t else ONEB)[:, :], MB[:, s:s + 1],
                                  start=(s == 0), stop=(s == t))
                last.then_inc(done, 1)
                ps, done = take("selT", W)
                pe.wait_ge(onehot_ready, 1)
                for c in range(NC):
                    for t in range(NT):
                        last = mm(ps[:, c * KEEP:(c + 1) * KEEP], HN[:, t, c * P:(c + 1) * P], OH[:, t, :],
                                  start=(t == 0), stop=(t == NT - 1))
                last.then_inc(done, 1)
                was_read(pe, work, work_read, "nqT")
                was_read(pe, work, work_read, "ckvT")
                was_read(pe, work, work_read, "selT")
                attention(0)
                out_projection("proj", 0, WP)

                transpose_rows(1)
                rows_transposed(1)
                for f in range(NF):
                    ps, done = take(("fc", f), W)
                    for c in range(NC):
                        last = mm(ps[:, :], WFC[:, c, f * P:(f + 1) * P], HT[:, c, :], start=(c == 0), stop=(c == NC - 1))
                    last.then_inc(done, 1)
                for i in range(2):
                    ps, done = take(("y", i), W)
                    for tt in range(2):
                        t = 2 * i + tt
                        for f in range(NF):
                            if i == 0 and tt == 0:
                                pe.wait_ge(squared, f + 1)
                            last = mm(ps[:, tt * C:(tt + 1) * C], R2[:, f, t * P:(t + 1) * P], WFP[:, f, :],
                                      start=(f == 0), stop=(f == NF - 1))
                    last.then_inc(done, 1)

                transpose_rows(2)
                rows_transposed(2)
                for t in range(NT):
                    ps, done = take(("qk", t), W)
                    for c in range(NC):
                        last = mm(ps[:, :], HT[:, c, t * P:(t + 1) * P], WQKV[:, c, 0:2 * C],
                                  start=(c == 0), stop=(c == NC - 1))
                    last.then_inc(done, 1)
                    if t % 2:
                        ps, done = take(("v", t // 2), W)
                        for tt in range(2):
                            for c in range(NC):
                                last = mm(ps[:, tt * C:(tt + 1) * C], HT[:, c, (t - 1 + tt) * P:(t + tt) * P],
                                          WQKV[:, c, 2 * C:3 * C], start=(c == 0), stop=(c == NC - 1))
                        last.then_inc(done, 1)
                for t in range(NT):
                    pe.wait_ge(tok_ready, 1 + NG * NPIECE + t + 1)
                    for n, name in enumerate(("qT", "kT")):
                        ps, done = take((name, t), R)
                        for g in range(NG):
                            last = nc.tensor.transpose(
                                ps[:, g * P:(g + 1) * P],
                                QK[:, t % 2, n * H + g * HG:n * H + (g + 1) * HG, :].rearrange("p h d -> p (h d)"),
                                ID[:, :])
                        last.then_inc(done, 1)
                for t in range(NT):
                    was_read(pe, tr, trans_read, ("qT", t))
                    was_read(pe, tr, trans_read, ("kT", t))
                for i in range(2):
                    was_read(pe, work, work_read, ("v", i))
                attention(1)
                out_projection("o", 1, WO)

                transpose_rows(3)
                rows_transposed(3)
                for i in range(2):
                    ps, done = take(("sign", i), W)
                    for tt in range(2):
                        t = 2 * i + tt
                        for c in range(NC):
                            last = mm(ps[:, tt * C:(tt + 1) * C], HT[:, c, t * P:(t + 1) * P], WSG[:, c, :],
                                      start=(c == 0), stop=(c == NC - 1))
                    last.then_inc(done, 1)
                pe.drain().then_inc(finished, 1)
                pe.wait_ge(next_sequence, seq + 1)

        @block.vector
        def _(dve):
            v = nc.vector
            steps = [0]

            def then(ins):
                steps[0] += 1
                ins.then_inc(dve_step, 1)
                dve.wait_ge(dve_step, steps[0])

            def read_work(ins, use):
                ins.then_inc(work_read[work.of[use][0]], 1)

            def read_trans(ins, use):
                ins.then_inc(trans_read[tr.of[use][0]], 1)

            def rsqrt(i, n):
                dve.wait_ge(pow_done, i + 1)
                then(v.tensor_tensor(NA[:, 0:n], VAR[:, 0:n], YP[:, 0:n], ALU.mult))
                then(v.tensor_tensor(NA[:, 0:n], NA[:, 0:n], YP[:, 0:n], ALU.mult))
                then(v.tensor_scalar(NA[:, 0:n], NA[:, 0:n], -0.5, 1.5, ALU.mult, ALU.add))
                then(v.tensor_tensor(RSTD[:, 0:n], NA[:, 0:n], YP[:, 0:n], ALU.mult))

            def layernorm(i, pow_index, X):
                for t in range(NT):
                    ins = v.bn_stats(BN[:, t, :], X[:, t, :])
                then(ins)
                for t in range(NT):
                    ins = v.bn_aggr(MV[:, t, :], BN[:, t, :])
                then(ins)
                v.tensor_scalar(VAR[:, 0:NT], MV[:, :, 1], LN_EPS, None, ALU.add).then_inc(var_ready, 1)
                rsqrt(pow_index, NT)
                for t in range(NT):
                    v.tensor_scalar(HN[:, t, :], X[:, t, :], MV[:, t, 0:1], RSTD[:, t:t + 1],
                                    ALU.subtract, ALU.mult).then_inc(h_ready, 1)
                ps = full(dve, ("hT", i, 0), WORK)
                read_work(v.tensor_copy(HT[:, 0, :], ps[:, :]), ("hT", i, 0))

            def rope_products(ps4, cos, sin, a4, b4):
                one = v.tensor_tensor(a4, ps4, cos, ALU.mult)
                two = v.tensor_tensor(b4, ps4[:, :, ::-1, :], sin, ALU.mult)
                return one, two

            def ab(i, rows, heads, half):
                w = heads * 2 * half
                if w <= 256:
                    a, b = AB[0:rows, i % 2, 0:w], AB[0:rows, i % 2, 256:256 + w]
                else:
                    a, b = AB[0:rows, 0, 0:w], AB[0:rows, 1, 0:w]
                return [z.rearrange("p (h j d) -> p h j d", j=2, d=half) for z in (a, b)]

            ropes = [0]

            def piece(g, m):
                what, t = PIECES[m]
                if what == "nv":
                    return
                rows = KEEP if what == "sel" else P
                ps = full(dve, ("piece", g, m), WORK)
                i = ropes[0]
                ropes[0] += 1
                if i >= 2:
                    dve.wait_ge(tok_ready, 1 + rope_pool_index[i - 2])
                a4, b4 = ab(i, rows, HG, 32)
                src = ps[0:rows, 0:384].rearrange("p (h d) -> p h d", h=HG)[:, :, NOPE:D0]
                src = src.rearrange("p h (j d) -> p h j d", j=2)
                cos = COS0[0:rows, t:t + 1, :].unsqueeze(1).broadcast_to([rows, HG, 2, 32])
                sin = SIN0[0:rows, t:t + 1, :].rearrange("p a (j d) -> p a j d", j=2).broadcast_to([rows, HG, 2, 32])
                one, two = rope_products(src, cos, sin, a4, b4)
                read_work(one, ("piece", g, m))
                read_work(two, ("piece", g, m))

            rope_pool_index = [g * NPIECE + m + 1 for g in range(NG) for m in range(NPIECE) if PIECES[m][0] != "nv"]

            def piece_evac(g, m):
                what, t = PIECES[m]
                if what not in ("kw", "sel"):
                    return
                ps = full(dve, ("piece_tr", g, m), TRANS)
                if what == "kw":
                    ins = v.tensor_copy(KW[g % 2][0:D0, :, t * P:(t + 1) * P],
                                        ps[0:D0, :].rearrange("p (h k) -> p h k", h=HG))
                else:
                    ins = v.tensor_copy(K1[g % 2][0:D0, :, 0:KEEP],
                                        ps[0:D0, 0:HG * KEEP].rearrange("p (h k) -> p h k", h=HG))
                read_trans(ins, ("piece_tr", g, m))

            def maxima(j):
                _, _, u = unit(j)
                ps = full(dve, ("scores", j), WORK)
                for n, (a, b) in enumerate(u["segs"]):
                    last = v.tensor_reduce(NM[:, j % NP, n:n + 1], ps[:, a:b], AX.X, ALU.max, negate=True)
                last.then_inc(max_ready, 1)

            def coefficients(j):
                layer, _, u = unit(j)
                n = len(u["segs"])
                was_read(dve, work, work_read, ("scores", j))
                if layer == 0:
                    then(v.reciprocal(RC[:, j % NP, 0:n], RS[:, j % NP, 0:n]))
                    v.tensor_tensor(CF[:, j % NP, 0:n], RC[:, j % NP, 0:n], GG[:, GATES[u["kind"]]],
                                    ALU.mult).then_inc(coef_ready, 1)
                else:
                    v.reciprocal(CF[:, j % NP, 0:n], RS[:, j % NP, 0:n]).then_inc(coef_ready, 1)

            def attention(layer):
                n = NG * NU[layer]
                for s in STEPS[layer]:
                    if s[0] == "piece":
                        piece(s[1], s[2])
                    elif s[0] == "piece_tr":
                        piece_evac(s[1], s[2])
                    elif s[0] == "scores":
                        maxima(s[1])
                        if s[1] > UNIT0[layer]:
                            coefficients(s[1] - 1)
                        if s[1] == UNIT0[layer] + n - 1:
                            coefficients(s[1])
                    elif s[0] == "trans" and s[1] % 2 == 0:
                        evacuate_probabilities(dve, v.tensor_copy, s[1])

            def add_rows(name, src, dst):
                for i in range(2):
                    ps = full(dve, (name, i), WORK)
                    read_work(v.tensor_tensor(dst[:, 2 * i:2 * i + 2, :], src[:, 2 * i:2 * i + 2, :],
                                              ps[:, :].rearrange("p (t c) -> p t c", t=2), ALU.add), (name, i))
                for i in range(2):
                    was_read(dve, work, work_read, (name, i))

            dve.sem_inc(x_stored, 16)
            dve.wait_ge(weights_loaded, ALL_LOADED)
            v.tensor_copy(WI[:, :, :], WIMP[:, :].unsqueeze(2).broadcast_to([P, NC, P])).then_inc(set_up, 1)
            v.tensor_copy(IDB[:, :], ID[:, :]).then_inc(set_up, 1)
            v.tensor_copy(CAUSB[:, :], X2[:, 0, 0:P]).then_inc(set_up, 1)
            v.tensor_copy(BEFB[:, :], X2[:, 1, 0:P]).then_inc(set_up, 1)
            v.memset(ONEB[:, :], 1.0).then_inc(set_up, 1)
            v.memset(MEANW[:, :], 1.0 / T).then_inc(set_up, 1)
            v.memset(MHALF[:, :], -0.5).then_inc(set_up, 1)
            v.tensor_scalar(WS[:, :, P:P + ROPE], WS[:, :, P:P + ROPE], 1.0 / H, None, ALU.mult).then_inc(set_up, 1)
            v.tensor_scalar(WQKV[:, :, 0:C], WQKV[:, :, 0:C], float(D1) ** -0.5, None, ALU.mult).then_inc(set_up, 1)
            v.memset(NM[:, :, :], 0.0).then_inc(set_up, 1)
            dve.wait_ge(set_up, SET_UP)
            with dve.Fori(0, B) as seq:
                dve.wait_ge(x_loaded, 16 * seq + 16)
                layernorm(0, 0, X0)
                ps = full(dve, ("small", 0), WORK)
                read_work(v.tensor_copy(SM[:, 0:2, 0:SM_W], ps[:, :].rearrange("p (t c) -> p t c", t=2)[:, :, 0:SM_W]),
                          ("small", 0))
                was_read(dve, work, work_read, ("small", 0))
                was_read(dve, work, work_read, ("small", 1))
                sq = AB[:, 0, :].rearrange("p (t c) -> p t c", t=NT)
                then(v.tensor_tensor(sq, SM[:, :, 0:P], SM[:, :, 0:P], ALU.mult))
                v.tensor_reduce(NA[:, 0:NT], sq[:, :, 0:QL], AX.X, ALU.add)
                then(v.tensor_reduce(NA[:, NT:2 * NT], sq[:, :, QL:P], AX.X, ALU.add))
                then(v.tensor_scalar(VAR[:, 0:NT], NA[:, 0:NT], 1.0 / QL, RMS_EPS, ALU.mult, ALU.add))
                v.tensor_scalar(VAR[:, NT:2 * NT], NA[:, NT:2 * NT], 1.0 / KVL, RMS_EPS, ALU.mult,
                                ALU.add).then_inc(var_ready, 1)
                kr_ab = [AB[:, 1, 256 * k:256 * (k + 1)].rearrange("p (t j d) -> p t j d", t=NT, j=2) for k in range(2)]
                krs = SM[:, :, P:P + ROPE].rearrange("p t (j d) -> p t j d", j=2)
                v.tensor_tensor(kr_ab[0], krs, COS0[:, :, :].unsqueeze(2).broadcast_to([P, NT, 2, 32]), ALU.mult)
                v.tensor_tensor(kr_ab[1], krs[:, :, ::-1, :], SIN0[:, :, :].rearrange("p t (j d) -> p t j d", j=2),
                                ALU.mult).then_inc(kr_products, 1)
                ps = full(dve, "score_cols", WORK)
                read_work(v.tensor_copy(SC[:, :], ps[:, ::P]), "score_cols")
                rsqrt(1, 2 * NT)
                then(v.tensor_scalar(RSTD[:, 0:NT], RSTD[:, 0:NT], Q_SCALE, None, ALU.mult))
                for t in range(NT):
                    v.scalar_tensor_tensor(NCK[:, t, 0:QL], SM[:, t, 0:QL], RSTD[:, t:t + 1], GQ[:, :],
                                           ALU.mult, ALU.mult).then_inc(latents_ready, 1)
                    v.scalar_tensor_tensor(NCK[:, t, QL:P], SM[:, t, QL:P], RSTD[:, NT + t:NT + t + 1], GK[:, :],
                                           ALU.mult, ALU.mult).then_inc(latents_ready, 1)
                was_read(dve, work, work_read, "score_cols")
                was_read(dve, work, work_read, "imp")
                for t in range(NT):
                    then(v.tensor_scalar(AB[:, 0, :], ROW, SC[:, t:t + 1], None, ALU.is_gt, ALU.add,
                                         accum_out=CG[:, t:t + 1]))
                    then(v.scalar_tensor_tensor(AB[:, 0, :], ROW, SC[:, t:t + 1],
                                                EARLY[:, (3 - t) * P:(3 - t) * P + T], ALU.is_equal, ALU.mult,
                                                accum_out=CE[:, t:t + 1]))
                then(v.tensor_tensor(CG[:, :], CG[:, :], CE[:, :], ALU.add))
                then(v.tensor_scalar(MF[:, :], CG[:, :], KEEP - 0.5, None, ALU.is_lt))
                v.tensor_copy(MB[:, :], MF[:, :]).then_inc(mask_ready, 1)
                ps = full(dve, "gate", WORK)
                read_work(v.tensor_copy(GS[:, :], ps[:, 0:3]), "gate")
                was_read(dve, work, work_read, "gate")
                v.tensor_reduce(GM[:, :], GS[:, :], AX.X, ALU.max, negate=True).then_inc(gate_in, 1)
                ps = full(dve, "ckvT", WORK)
                read_work(v.tensor_copy(NQT[QL:P, :], ps[0:KVL, :]), "ckvT")
                ps = full(dve, "pos", WORK)
                read_work(v.tensor_copy(POS[:, :], ps[:, 0:NT]), "pos")
                was_read(dve, work, work_read, "pos")
                for t in range(NT):
                    last = v.tensor_scalar(OH[:, t, :], RANKS[:, :], POS[:, t:t + 1], MF[:, t:t + 1],
                                           ALU.is_equal, ALU.mult)
                last.then_inc(onehot_ready, 1)
                dve.wait_ge(gate_exp, 1)
                then(v.reciprocal(GD[:, 1:2], GD[:, 0:1]))
                then(v.tensor_scalar(GG[:, :], GE[:, :], GD[:, 1:2], None, ALU.mult))
                ps = full(dve, "selT", WORK)
                read_work(v.tensor_copy(SELT[:, :, :], ps[:, 0:2 * KEEP].rearrange("p (c k) -> p c k", c=NC)), "selT")
                dve.wait_ge(tok_ready, 1)
                attention(0)
                ropes[0] = 0
                add_rows("proj", X0, X1)

                layernorm(1, 2, X1)
                Y, MEM, SP, SUM = (STATE[:, n, :] for n in range(4))
                for i in range(2):
                    was_read(dve, work, work_read, ("y", i))
                then(v.tensor_scalar(SP, Y, 1.0, None, ALU.is_gt))
                v.tensor_copy(SUM, SP)
                for step in range(4):
                    then(v.scalar_tensor_tensor(MEM, MEM if step else Y, 0.9, Y, ALU.mult, ALU.add))
                    then(v.tensor_tensor(MEM, MEM, SP, ALU.subtract))
                    then(v.tensor_scalar(SP, MEM, 1.0, None, ALU.is_gt))
                    then(v.tensor_tensor(SUM, SUM, SP, ALU.add))
                dve.wait_ge(x_stored, 16 * seq + 16)
                then(v.scalar_tensor_tensor(X2[:, :, :].rearrange("p t c -> p (t c)"), SUM, 0.2,
                                            X1[:, :, :].rearrange("p t c -> p (t c)"), ALU.mult, ALU.add))

                layernorm(2, 3, X2)
                dve.wait_ge(zeroed, 1)
                for t in range(NT):
                    ps = full(dve, ("qk", t), WORK)
                    if t:
                        dve.wait_ge(tok_ready, 1 + NG * NPIECE + t)
                    a4, b4 = ab(0, P, 2 * H, 8)
                    cos = COS1[:, t:t + 1, :].unsqueeze(1).broadcast_to([P, 2 * H, 2, 8])
                    sin = SIN1[:, t:t + 1, :].rearrange("p a (j d) -> p a j d", j=2).broadcast_to([P, 2 * H, 2, 8])
                    one, two = rope_products(ps[:, :].rearrange("p (h j d) -> p h j d", j=2, d=8), cos, sin, a4, b4)
                    read_work(one, ("qk", t))
                    read_work(two, ("qk", t))
                for t in range(NT):
                    ps = full(dve, ("qT", t), TRANS)
                    for h in (0, 1):
                        ins = v.tensor_copy(QZ[32 * h:32 * h + 32, :, h, t * P:(t + 1) * P],
                                            ps[32 * h:32 * h + 32, :].rearrange("p (g k) -> p g k", g=NG))
                        read_trans(ins, ("qT", t))
                    ps = full(dve, ("kT", t), TRANS)
                    read_trans(v.tensor_copy(KB[:, :, t * P:(t + 1) * P],
                                             ps[:, :].rearrange("p (g k) -> p g k", g=NG)), ("kT", t))
                attention(1)
                add_rows("o", X2, X1)

                layernorm(3, 4, X1)
                for i in range(2):
                    ps = full(dve, ("sign", i), WORK)
                    v.tensor_tensor(X2[:, 2 * i:2 * i + 2, :], X1[:, 2 * i:2 * i + 2, :],
                                    ps[:, :].rearrange("p (t c) -> p t c", t=2), ALU.add).then_inc(out_ready, 1)
                dve.drain().then_inc(finished, 1)
                dve.wait_ge(next_sequence, seq + 1)

        @block.scalar
        def _(act):
            a = nc.scalar

            def copy(dst, src):
                return a.activation(dst, src, ACT.Copy)

            def read_work(ins, use):
                ins.then_inc(work_read[work.of[use][0]], 1)

            def read_trans(ins, use):
                ins.then_inc(trans_read[tr.of[use][0]], 1)

            def transpose_half(i):
                ps = full(act, ("hT", i, 1), WORK)
                read_work(copy(HT[:, 1, :], ps[:, :]), ("hT", i, 1))

            def piece(g, m):
                what, t = PIECES[m]
                rows = KEEP if what == "sel" else P
                use = ("piece", g, m)
                ps = full(act, use, WORK)
                k, _, _, r = work.of[use]
                if what != "nv":
                    act.wait_ge(work_read[k], r - (2 if what == "sel" else 1))
                i = g * NPIECE + m
                if i >= 4:
                    kk, _, f, _ = tr.of[("piece_tr", (i - 4) // NPIECE, (i - 4) % NPIECE)]
                    act.wait_ge(trans_full[kk], f)
                wide = P if what == "nv" else 384
                src = ps[0:rows, 0:wide].rearrange("p (h d) -> p h d", h=HG)[:, :, 0:NOPE]
                read_work(copy(TOK[0:rows, i % 4, :, 0:NOPE], src), use)
                if what == "nv":
                    if g >= 2 and t == 0:
                        act.wait_ge(pv_done, KINDS[0] * (g - 1))
                    read_work(copy(VV[:, g % 2, t, :], ps[:, P:384]), use)
                elif what == "sel":
                    read_work(copy(VS[:, g % 2, :], ps[0:KEEP, 384:512]), use)

            def piece_evac(g, m):
                what, t = PIECES[m]
                if what not in ("q", "nv"):
                    return
                ps = full(act, ("piece_tr", g, m), TRANS)
                src = ps[0:D0, :].rearrange("p (h k) -> p h k", h=HG)
                if what == "q":
                    dst = QT[g % 2][0:D0, :, t * P:(t + 1) * P]
                else:
                    dst = K1[g % 2][0:D0, :, KEEP + t * P:KEEP + (t + 1) * P]
                read_trans(copy(dst, src), ("piece_tr", g, m))

            def exponentials(j):
                _, _, u = unit(j)
                act.wait_ge(max_ready, j + 1)
                ps = full(act, ("scores", j), WORK)
                if j >= NP:
                    kk, _, f, _ = tr.of[("trans", j - NP)]
                    act.wait_ge(trans_full[kk], f)
                for n, (lo, hi) in enumerate(u["segs"]):
                    last = a.activation(PR[:, j % NP, lo:hi], ps[:, lo:hi], ACT.Exp, bias=NM[:, j % NP, n:n + 1],
                                        accum_out=RS[:, j % NP, n:n + 1])
                read_work(last, ("scores", j))

            def attention(layer):
                for s in STEPS[layer]:
                    if s[0] == "piece":
                        piece(s[1], s[2])
                    elif s[0] == "piece_tr":
                        piece_evac(s[1], s[2])
                    elif s[0] == "scores":
                        exponentials(s[1])
                    elif s[0] == "trans" and s[1] % 2 == 1:
                        evacuate_probabilities(act, copy, s[1])
                    elif s[0] == "pv" and s[2] == KINDS[layer] - 1:
                        g = s[1]
                        act.wait_ge(pv_done, KIND0[layer] + (g + 1) * KINDS[layer])
                        k = outs.of[(layer, g)][0]
                        copy(OT[:, g, :], OB[k][:, :]).then_inc(outs_read[k], 1)

            act.wait_ge(weights_loaded, ALL_LOADED)
            a.activation(WSG[:, :, :], WSG[:, :, :], ACT.Sign).then_inc(set_up_act, 1)
            with act.Fori(0, B) as seq:
                transpose_half(0)
                ps = full(act, ("small", 1), WORK)
                read_work(copy(SM[:, 2:4, 0:SM_W], ps[:, :].rearrange("p (t c) -> p t c", t=2)[:, :, 0:SM_W]),
                          ("small", 1))
                ps = full(act, "imp", WORK)
                read_work(copy(ROW, ps[:, :]), "imp")
                ps = full(act, "nqT", WORK)
                read_work(copy(NQT[0:QL, :], ps[0:QL, :]), "nqT")
                act.wait_ge(gate_in, 1)
                a.activation(GE[:, :], GS[:, :], ACT.Exp, bias=GM[:, 0:1], accum_out=GD[:, 0:1]).then_inc(gate_exp, 1)
                attention(0)
                transpose_half(1)
                for f in range(NF):
                    ps = full(act, ("fc", f), WORK)
                    if f >= 2:
                        act.wait_ge(squared, f - 1)
                    read_work(a.activation(AB[:, f % 2, :], ps[:, :], ACT.Relu), ("fc", f))
                for i in range(2):
                    ps = full(act, ("y", i), WORK)
                    read_work(copy(STATE[:, 0, i * 512:(i + 1) * 512], ps[:, :]), ("y", i))
                transpose_half(2)
                act.wait_ge(zeroed, 1)
                for i in range(2):
                    ps = full(act, ("v", i), WORK)
                    src = ps[:, :].rearrange("p (t h d) -> p t h d", t=2, d=D1)
                    read_work(copy(VP[:, 2 * i:2 * i + 2, :, 0:D1], src), ("v", i))
                for t in range(NT):
                    ps = full(act, ("qT", t), TRANS)
                    for h in (2, 3):
                        ins = copy(QZ[32 * h:32 * h + 32, :, h, t * P:(t + 1) * P],
                                   ps[32 * h:32 * h + 32, :].rearrange("p (g k) -> p g k", g=NG))
                        read_trans(ins, ("qT", t))
                attention(1)
                transpose_half(3)
                act.drain().then_inc(finished, 1)
                act.wait_ge(next_sequence, seq + 1)

        @block.gpsimd
        def _(pool):
            gp = nc.gpsimd

            def power(i, n):
                pool.wait_ge(var_ready, i + 1)
                gp.tensor_tensor(YP[:, 0:n], VAR[:, 0:n], MHALF[:, 0:n], ALU.pow).then_inc(pow_done, 1)

            def piece(g, m):
                what, t = PIECES[m]
                rows = KEEP if what == "sel" else P
                i = g * NPIECE + m
                if i >= 4:
                    kk, _, f, _ = tr.of[("piece_tr", (i - 4) // NPIECE, (i - 4) % NPIECE)]
                    pool.wait_ge(trans_full[kk], f)
                dst = TOK[0:rows, i % 4, :, NOPE:D0]
                if what == "nv":
                    gp.tensor_copy(dst, KR[:, t:t + 1, :].broadcast_to([P, HG, ROPE])).then_inc(tok_ready, 1)
                    return
                k, _, _, r = work.of[("piece", g, m)]
                pool.wait_ge(work_read[k], r - (2 if what == "sel" else 1))
                n = (g * (NPIECE - NT) + sum(1 for q in PIECES[:m] if q[0] != "nv")) % 2
                gp.tensor_tensor(dst, AB[0:rows, n, 0:256].rearrange("p (h d) -> p h d", h=HG),
                                 AB[0:rows, n, 256:512].rearrange("p (h d) -> p h d", h=HG),
                                 ALU.add).then_inc(tok_ready, 1)

            def scale(j):
                _, _, u = unit(j)
                pool.wait_ge(coef_ready, j + 1)
                for n, (lo, hi) in enumerate(u["segs"]):
                    last = gp.tensor_tensor(PR[:, j % NP, lo:hi], PR[:, j % NP, lo:hi],
                                            CF[:, j % NP, n:n + 1].broadcast_to([P, hi - lo]), ALU.mult)
                last.then_inc(scaled, 1)

            def attention(layer):
                for s in STEPS[layer]:
                    if s[0] == "piece":
                        piece(s[1], s[2])
                    elif s[0] == "scores":
                        scale(s[1])

            pool.wait_ge(set_up, SET_UP)
            with pool.Fori(0, B) as seq:
                power(0, NT)
                power(1, 2 * NT)
                pool.wait_ge(kr_products, 1)
                gp.tensor_tensor(KR[:, :, :], AB[:, 1, 0:256].rearrange("p (t d) -> p t d", t=NT),
                                 AB[:, 1, 256:512].rearrange("p (t d) -> p t d", t=NT), ALU.add).then_inc(tok_ready, 1)
                pool.wait_ge(tok_ready, 1)
                attention(0)
                power(2, NT)
                pool.wait_ge(pv_done, KIND0[1])
                gp.memset(QK, 0.0)
                gp.memset(QZ, 0.0)
                gp.memset(VP, 0.0).then_inc(zeroed, 1)
                for f in range(NF):
                    was_read(pool, work, work_read, ("fc", f))
                    gp.tensor_tensor(R2[:, f, :], AB[:, f % 2, :], AB[:, f % 2, :], ALU.mult).then_inc(squared, 1)
                power(3, NT)
                for t in range(NT):
                    k, _, _, r = work.of[("qk", t)]
                    pool.wait_ge(work_read[k], r)
                    if t >= 2:
                        kk, _, f, _ = tr.of[("kT", t - 2)]
                        pool.wait_ge(trans_full[kk], f)
                    gp.tensor_tensor(QK[:, t % 2, :, 0:D1], AB[:, 0, :].rearrange("p (h d) -> p h d", d=D1),
                                     AB[:, 1, :].rearrange("p (h d) -> p h d", d=D1), ALU.add).then_inc(tok_ready, 1)
                attention(1)
                power(4, NT)
                pool.drain().then_inc(finished, 1)
                pool.wait_ge(next_sequence, seq + 1)


def head_cols(w, perm):
    rows = w.shape[0]
    return w.reshape(rows, H, -1)[:, :, perm].reshape(rows, -1)


def kernel(**inputs):
    import concourse.bacc as bacc
    from concourse.bass_utils import run_bass_kernel_spmd

    a = {k: np.asarray(v) for k, v in inputs.items()}
    L = lambda name: a["L0_attn_" + name]

    def halves(w):
        return np.ascontiguousarray(w.reshape(-1, P, w.shape[1]).transpose(1, 0, 2))

    q = np.concatenate([L("w_dq_nope").reshape(QL, H, NOPE), L("w_dq_rope").reshape(QL, H, ROPE)], 2).reshape(QL, -1)
    nv = np.concatenate([L("w_dk_nope").reshape(KVL, NG, P), L("w_dv").reshape(KVL, NG, P)], 2).reshape(KVL, -1)

    def grouped(wk, wv):
        both = np.concatenate([wk.reshape(NC, P, NG, HG * D0), wv.reshape(NC, P, NG, HG * VD)], 3)
        return np.ascontiguousarray(both.transpose(2, 1, 0, 3))

    even_odd = np.concatenate([np.arange(0, D1, 2), np.arange(1, D1, 2)])
    wqkv = np.ascontiguousarray(a["L1_attn_W_qkv"].T)
    wqkv = np.concatenate([head_cols(wqkv[:, 0:C], even_odd), head_cols(wqkv[:, C:2 * C], even_odd), wqkv[:, 2 * C:]], 1)
    wo = np.zeros((H, DP, C), a["L1_attn_W_o"].dtype)
    wo[:, 0:D1, :] = a["L1_attn_W_o"].T.reshape(H, D1, C)
    arrays = dict(
        x=a["L0_attn_x"].reshape(B * T, C),
        w_small=halves(np.concatenate([L("w_cq"), L("w_ckv"), L("w_krope"), L("w_gate")[:, [1, 0, 2]]], 1)),
        w_imp=halves(L("w_imp"))[:, :, 0],
        w_q=q, w_nv=nv,
        w_kw=grouped(L("w_wink"), L("w_winv")), w_sel=grouped(L("w_selk"), L("w_selv")),
        w_proj=halves(L("w_proj")), g_q=L("g_qnorm"), g_kv=L("g_kvnorm"),
        w_fc=halves(a["L0_ffn_W_fc"].T), w_ffp=halves(a["L0_ffn_W_proj"].T),
        w_qkv=halves(wqkv), w_o=halves(wo.reshape(H * DP, C)), w_sign=halves(a["L1_ffn_weight"].T),
        **constants(),
    )
    nc = bacc.Bacc("TRN2", target_bir_lowering=False, num_devices=1)
    feed, args = {}, []
    for name in WEIGHT_NAMES + CONST_NAMES:
        arr = np.ascontiguousarray(arrays[name])
        feed[name + "_dram"] = arr
        args.append(nc.dram_tensor(name + "_dram", arr.shape, mybir.dt.from_np(arr.dtype), kind="ExternalInput").ap())
    args.append(nc.dram_tensor("out_dram", (B * T, C), F32, kind="ExternalOutput").ap())
    build_program(nc, *args)
    result = run_bass_kernel_spmd(nc, [feed], core_ids=[0])
    return result.results[0]["out_dram"].reshape(B, T, C)
```

```python
from contextlib import ExitStack

import numpy as np

import concourse.bass as bass
from concourse import mybir

F32 = mybir.dt.float32
BF16 = mybir.dt.bfloat16
F32R = mybir.dt.float32r
ALU = mybir.AluOpType
ACT = mybir.ActivationFunctionType
AX = mybir.AxisListType

P = 128
B, T, C = 8, 512, 256
NT = T // P
NC = C // P
H = 16
HG = 4
NG = H // HG
NPAIR = H // 2
QL, KVL = 96, 32
NOPE, ROPE, VD = 32, 64, 32
D0 = NOPE + ROPE
KEEP = 64
FF = 1024
NF = FF // P
SM_W = QL + KVL + ROPE + 3
D1 = 16
DP = 32
NEG = -1.0e30
Q_SCALE = float(D0) ** -0.5
LN_EPS, RMS_EPS = 1e-5, 1e-6

NWORK, NOUT = 5, 3
NP = 8
A1, A3, A2 = 0, 1, 2



def max_units0():
    out = []
    for h in range(2):
        out += [
            dict(mm=[(h, "k1", 0, 448, 0, 3)], mask=[], segs=[(0, 64, A2, h, 3), (64, 448, A1, h, 3)]),
            dict(mm=[(h, "k1", 448, 128, 0, 3), (h, "kw", 0, 384, 128, 2)], mask=[0, 384],
                 segs=[(0, 128, None, h, 3), (128, 512, A3, h, 2)]),
            dict(mm=[(h, "kw", 0, 512, 0, 3)], mask=[384], segs=[(0, 512, A3, h, 3)]),
            dict(mm=[(h, "k1", 0, 448, 0, 2)], mask=[320], segs=[(0, 64, A2, h, 2), (64, 448, A1, h, 2)]),
            dict(mm=[(h, "k1", 0, 320, 0, 1), (h, "kw", 0, 128, 320, 0)], mask=[192, 320],
                 segs=[(0, 64, A2, h, 1), (64, 320, A1, h, 1), (320, 448, A3, h, 0)]),
            dict(mm=[(h, "k1", 0, 192, 0, 0), (h, "kw", 0, 256, 192, 1)], mask=[64, 320],
                 segs=[(0, 64, A2, h, 0), (64, 192, A1, h, 0), (192, 448, A3, h, 1)]),
        ]
    return out


def max_units1():
    out = []
    for h in range(2):
        out += [dict(mm=[(h, "k", 0, 512, 0, 3)], mask=[384], segs=[(0, 512, 0, h, 3)]),
                dict(mm=[(h, "k", 0, 384, 0, 2), (h, "k", 0, 128, 384, 0)], mask=[256, 384],
                     segs=[(0, 384, 0, h, 2), (384, 512, 0, h, 0)])]
    out.append(dict(mm=[(h, "k", 0, 256, 256 * h, 1) for h in range(2)], mask=[128, 384],
                    segs=[(256 * h, 256 * h + 256, 0, h, 1) for h in range(2)]))
    return out


def units0():
    out = []
    for what in ([(A1, 0, 0)], [(A1, 1, 0), (A1, 3, 384)], [(A3, 0, 0)], [(A3, 1, 0), (A3, 3, 384)],
                 [(A1, 2, 0), (A3, 2, 256)], [(A2, 0, 0)]):
        for h in range(2):
            out.append([(a, h, j, col) for a, j, col in what])
    return out


def units1():
    out = []
    for what in ([(0, 0)], [(1, 0), (3, 384)]):
        for h in range(2):
            out.append([(0, h, j, col) for j, col in what])
    out.append([(0, 0, 2, 0), (0, 1, 2, 256)])
    return out


MAX_UNITS = [max_units0(), max_units1()]
UNITS = [units0(), units1()]
NU = [len(u) for u in UNITS]
PV = [[(2 * k, 2 * k + 1) for k in range(6)], [(0, 1), (2, 3), (4,)]]
NPV = [len(k) for k in PV]
UNIT0 = [0, NPAIR * NU[0]]
PV0 = [0, NPAIR * NPV[0]]
NCOL = [24, 8]
COMPLETE = [{4: [A1, A3], 5: [A2]}, {2: [0]}]

PIECES = [("qk", 0), ("qk", 1), ("nv", 0), ("qk", 2), ("qk", 3), ("nv", 1), ("sel", 0)]
NPIECE = len(PIECES)
ROPED = [m for m in range(NPIECE) if PIECES[m][0] != "nv"]


AFTER = [{'pv': 2.67, 'tr': 2.52, 'group': 1.98, 'piece': -2.58, 'gap': 0.66, 'piece_tr': 2.36, 'max': 5.25, 'max_gap': 0.32, 'mt': 1.86}, {'pv': 2.35, 'tr': 1.46, 'group': 2.49, 'max': -1.78, 'max_gap': 1.03, 'mt': 2.68, 'pro': 0.38, 'pro_gap': [4.02, 4.0, 3.0, 4.0, 6.5, 7.0, 3.0, 0.0]}]


def attention_steps(layer):
    n, at, o = NU[layer], [], AFTER[layer]
    for p in range(NPAIR):
        t0 = n * p
        for i in range(n):
            at.append((t0 + i, ("unit", p, i)))
        for k, units in enumerate(PV[layer]):
            t = t0 + units[-1] + o["pv"]
            at.append((t, ("pv", p, k)))
            for a in COMPLETE[layer].get(k, []):
                if layer == 0:
                    what, group = p, a == A2 and p % 2
                elif p % 2:
                    what, group = p // 2, True
                else:
                    continue
                t1 = t + 0.3 + o["tr"]
                at += [(t + 0.3, ("out", what, a)), (t1, ("out_tr", what, a)), (t1 + 0.1, ("norm", what, a))]
                if group:
                    at += [(t1 + o["group"], ("group", p // 2)), (t1 + o["group"] + 0.1, ("group_out", p // 2))]
        b = n * (p - (1 if layer == 0 else 2))
        if layer == 0:
            for m in range(NPIECE):
                at.append((b + o["gap"] * m + o["piece"], ("piece", p, m)))
                t = max(b + o["gap"] * m + o["piece"] + o["piece_tr"], n * (p - 1) - 0.9 + 0.01 * m)
                at.append((t, ("piece_tr", p, m)))
        for i in range(len(MAX_UNITS[layer])):
            at.append((b + o["max"] + o["max_gap"] * i, ("max", p, i)))
        t = b + o["max"] + o["max_gap"] * (len(MAX_UNITS[layer]) - 1) + o["mt"]
        at += [(t, ("mt", p)), (t + 0.4, ("mt_out", p))]
    if layer == 1:
        t = o["pro"]
        for j in range(8):
            at.append((t + 0.15, ("pro", j)))
            t += o["pro_gap"][j]
            if 1 <= j <= 6:
                at.append((t, ("pro_pe", j - 1)))
    return [s for _, s in sorted(at, key=lambda x: x[0])]


STEPS = [attention_steps(0), attention_steps(1)]


QKV_STEPS = [("half", 0), ("qk", 0), ("qk", 1), ("heads", 0), ("half", 1), ("qk", 2), ("heads", 1),
             ("qk", 3), ("heads", 2), ("heads", 3)]


class Banks:

    def __init__(self, n):
        self.n, self.uses, self.units, self.of = n, 0, 0, {}
        self.full, self.read, self.exp = [0] * n, [0] * n, [0] * n

    def use(self, name, readers=1):
        k = self.uses % self.n
        self.uses += 1
        free_at, exp_at = self.read[k], self.exp[k]
        self.full[k] += 1
        if readers:
            self.read[k] += readers
            self.exp[k] = 0
        else:
            self.units += 1
            self.exp[k] = self.units
        self.of[name] = (k, free_at, self.full[k], self.read[k], exp_at)


def plan_banks():
    work, first = Banks(NWORK), Banks(NWORK)

    def prologue(banks, tag, j):
        for name in (["hT0", "hT1"], ["small0", "small1", "imp"], ["score_cols", "gate"], ["nqT", "ckvT"],
                     ["pos"], ["selT"])[j]:
            banks.use((tag, name))

    def attention(layer):
        for s in STEPS[layer]:
            if s[0] == "mt" and layer == 0:
                for h in range(2):
                    work.use((0,) + s + (h,))
            elif s[0] in ("unit", "max", "mt", "out_tr", "group"):
                work.use((layer,) + s, {"unit": 0, "mt": 2}.get(s[0], 1))
            elif s[0] == "piece":
                work.use(s, {"qk": 4, "nv": 2, "sel": 4}[PIECES[s[2]][0]])
            elif s[0] == "piece_tr":
                work.use(s, 2)
            elif s[0] == "pro_pe":
                prologue(work, "next", s[1])

    for j in range(6):
        prologue(first, "first", j)
    work.of.update(first.of)
    attention(0)
    for i in range(2):
        work.use(("proj", i))
    for i in range(2):
        work.use(("hT", 1, i))
    for i in range(2):
        for f in range(NF // 2):
            work.use(("fc", i, f))
        work.use(("y", i))
    for what, n in QKV_STEPS:
        if what == "half":
            work.use(("hT", 2, n))
            work.use(("v", n))
        elif what == "qk":
            work.use(("qk1", n), 2)
        else:
            for k in range(4):
                work.use(("heads", n, k), 2 if k < 2 else 1)
    attention(1)
    for i in range(2):
        work.use(("o", i))
    for i in range(2):
        work.use(("hT", 3, i))
        work.use(("sign", i))
    return work


def constants():
    pos = np.arange(T, dtype=np.float32)

    def tab(dim):
        f = (1.0 / np.float32(10000.0) ** (np.arange(0, dim, 2, dtype=np.float32) / np.float32(dim))).astype(np.float32)
        a = np.outer(pos, f).astype(np.float32)
        tile = lambda m: np.ascontiguousarray(m.reshape(NT, P, -1).transpose(1, 0, 2))
        c, s = np.cos(a).astype(np.float32), np.sin(a).astype(np.float32)
        return tile(c), tile(np.concatenate([-s, s], 1))

    c0, s0 = tab(ROPE)
    c1, s1 = tab(D1)
    p = np.arange(P)
    f = np.float32
    return dict(
        cos0=c0, sin0=s0, cos1=c1, sin1=s1,
        ident=np.eye(P, dtype=f),
        causal=np.where(p[None, :] > p[:, None], f(NEG), f(0.0)).astype(f),
        causal_t=np.where(p[None, :] < p[:, None], f(NEG), f(0.0)).astype(f),
        before=(p[:, None] < p[None, :]).astype(f),
        earlier=((np.arange(7 * P)[None, :] - 3 * P) < p[:, None]).astype(f),
        ranks=np.broadcast_to(np.arange(KEEP, dtype=f), (P, KEEP)).copy(),
    )


CONST_NAMES = ["cos0", "sin0", "cos1", "sin1", "ident", "causal", "causal_t", "before", "earlier", "ranks"]
WEIGHT_NAMES = ["x", "w_small", "w_imp", "w_q", "w_nv", "w_kw", "w_sel", "w_proj", "g_q", "g_kv",
                "w_fc", "w_ffp", "w_qkv", "w_o", "w_sign"]


def build_program(nc, x, w_small, w_imp, w_q, w_nv, w_kw, w_sel, w_proj, g_q, g_kv,
                  w_fc, w_ffp, w_qkv, w_o, w_sign,
                  cos0, sin0, cos1, sin1, ident, causal, causal_t, before, earlier, ranks, out):
    work = plan_banks()
    ctx = ExitStack()
    with ctx:
        def sb(name, shape, dt=F32):
            return ctx.enter_context(nc.sbuf_tensor(name, shape, dt))

        WS = sb("WS", [P, NC, SM_W])
        WIMP = sb("WIMP", [P, NC])
        WI = sb("WI", [P, NC, P])
        WQ = sb("WQ", [P, H * D0])
        WKW = sb("WKW", [P, 2, NC, 256])
        WSEL = sb("WSEL", [P, 2, NC, 256])
        WP = sb("WP", [P, NG, C])
        GQ = sb("GQ", [P, QL])
        GK = sb("GK", [P, KVL])
        WFC = sb("WFC", [P, NC, FF])
        WFP = sb("WFP", [P, NF, C])
        WQKV = sb("WQKV", [P, NC, 3 * C])
        WO = sb("WO", [P, NG, C])
        WSG = sb("WSG", [P, NC, C])
        COS0, SIN0 = sb("COS0", [P, NT, 32]), sb("SIN0", [P, NT, 64])
        COS1, SIN1 = sb("COS1", [P, NT, 8]), sb("SIN1", [P, NT, 16])
        ID = sb("ID", [P, P])
        IDB = sb("IDB", [P, P], BF16)
        CAUSB = sb("CAUSB", [P, P], BF16)
        CAUTB = sb("CAUTB", [P, P], BF16)
        ONES = sb("ONES", [P, 32])
        BEFB = sb("BEFB", [P, P], BF16)
        ONEB = sb("ONEB", [P, P], BF16)
        MEANW = sb("MEANW", [P, P])
        EARLY = sb("EARLY", [P, 7 * P])
        RANKS = sb("RANKS", [P, KEEP])
        MHALF = sb("MHALF", [P, 8])
        HEAD = sb("HEAD", [P, 2])
        X0, X1, X2 = sb("X0", [P, NT, C]), sb("X1", [P, NT, C]), sb("X2", [P, NT, C])
        HN = sb("HN", [P, NT, C])
        HT = sb("HT", [P, NC, T])
        HT0 = sb("HT0", [P, NC, T])
        NQT = sb("NQT", [P, T])
        KR = sb("KR", [P, NT, ROPE])
        SMALL = sb("SMALL", [P, 2176])
        SM = SMALL[:, 0:4 * 196].rearrange("p (t c) -> p t c", t=NT)
        NCK = SMALL[:, 784:1296].rearrange("p (t c) -> p t c", t=NT)
        ROW = SMALL[:, 1296:1808]
        OH = SMALL[:, 1808:2064].rearrange("p (t c) -> p t c", t=NT)
        QS = SMALL[:, 0:1024].rearrange("p (h s d) -> p h s d", h=H, s=4)
        KS = SMALL[:, 1024:2048].rearrange("p (h s d) -> p h s d", h=H, s=4)
        SELT = sb("SELT", [P, NC, KEEP])
        BIG = sb("BIG", [P, 12800], F32R)
        QW, K1 = [], []
        for o in (0, 6400):
            QW.append([BIG[:, o + 2048 * n:o + 2048 * n + 2048].rearrange("p (s k) -> p s k", s=4) for n in range(2)])
            K1.append([BIG[:, o + 4096 + 1152 * n:o + 4096 + 1152 * n + 1152].rearrange("p (h k) -> p h k", h=2)
                       for n in range(2)])
        QZ = BIG[:, 0:8192].rearrange("p (g h k) -> p g h k", g=NPAIR, h=2)
        KB = BIG[:, 8192:12288].rearrange("p (g k) -> p g k", g=NPAIR)
        VV = sb("VV", [P, 3, NT, 2, 64])
        VS = sb("VS", [KEEP, 3, 64])
        TOK = sb("TOK", [P, 4, HG, D0])
        AB = sb("AB", [P, 2, 512])
        PR = sb("PR", [P, NP, 512])
        OT = sb("OT", [P, NG, T])
        NRM = sb("NRM", [P, 4096])
        OE = [NRM[:, 0:1536].rearrange("p (a k) -> p a k", a=3), NRM[:, 2048:3072].rearrange("p (a k) -> p a k", a=2)]
        OROWS = [NRM[:, o:o + 1024].rearrange("p (n t c) -> p n t c", n=2, t=NT) for o in (2304, 3072)]
        GATED = NRM[:, 1536:2304].rearrange("p (a t h d) -> p a t h d", a=3, t=NT, h=2)
        VP = NRM[:, 0:2048].rearrange("p (t h d) -> p t h d", t=NT, d=DP)
        ROPED1 = PR[:, 0:2, :].rearrange("p n (h d) -> p n h d", d=D1)
        STATE = NRM[:, :].rearrange("p (i n a) -> p i n a", i=2, n=4)
        R2 = PR
        NMX = sb("NMX", [P, 2, 24])
        NPART = sb("NPART", [P, 2])
        RSUM = sb("RSUM", [P, 3, NT, 4])
        BN = sb("BN", [P, NT, 6]); MV = sb("MV", [P, NT, 2])
        VAR, YP, NA = sb("VAR", [P, 8]), sb("YP", [P, 8]), sb("NA", [P, 8])
        RSTD = sb("RSTD", [P, 8])
        SC, CG, CE = sb("SC", [P, NT]), sb("CG", [P, NT]), sb("CE", [P, NT])
        MF, MB, POS = sb("MF", [P, NT]), sb("MB", [P, NT], BF16), sb("POS", [P, NT])
        GS, GE, GG = sb("GS", [P, 3]), sb("GE", [P, 3]), sb("GG", [P, 3])
        GM, GD = sb("GM", [P, 1]), sb("GD", [P, 3])

        WB = [ctx.enter_context(nc.psum_tensor(f"work{k}", [P, 512], F32)) for k in range(NWORK)]
        OB = [ctx.enter_context(nc.psum_tensor(f"outs{k}", [P, 512], F32)) for k in range(NOUT)]

        def sem(name):
            return ctx.enter_context(nc.semaphore(name))

        first_cleared = sem("work_full0")
        work_full = [first_cleared] + [sem(f"work_full{k}") for k in range(1, NWORK)]
        work_read = [sem(f"work_read{k}") for k in range(NWORK)]
        pv_done = sem("pv_done")
        var_ready = sem("var_ready")
        pow_done = sem("pow_done")
        h_ready = sem("h_ready")
        latents_ready = sem("latents_ready")
        kr_products = sem("kr_products")
        mask_ready = sem("mask_ready")
        onehot_ready = sem("onehot_ready")
        gate_in = sem("gate_in")
        gate_exp = sem("gate_exp")
        rope_products = sem("rope_products")
        tok_ready = sem("tok_ready")
        max_ready = sem("max_ready")
        exp_ready = sem("exp_ready")
        evacuated = sem("evacuated")
        summed = sem("summed")
        stacked = sem("stacked")
        stacked_hi = sem("stacked_hi")
        roped1 = sem("roped1")
        squared = sem("squared")
        out_ready = sem("out_ready")
        zeroed = sem("zeroed")
        values_set = sem("values_set")
        pool_step = sem("pool_step")
        dve_step = sem("dve_step")
        kw_loaded = [sem("kw_loaded0"), sem("kw_loaded1")]
        sel_loaded = [sem("sel_loaded0"), sem("sel_loaded1")]
        finished = sem("finished")
        cleared = range(first_cleared.num, finished.num + 1)
        next_sequence = sem("next_sequence")
        x_loaded = sem("x_loaded")
        x_stored = sem("x_stored")
        weights_loaded = sem("weights_loaded")
        set_up = sem("set_up")
        set_up_act = sem("set_up_act")

        block = ctx.enter_context(nc.Block())

        def full(e, use, bank):
            ring, sems, banks = bank
            k, _, f, _, _ = ring.of[use]
            e.wait_ge(sems[k], f)
            return banks[k]

        WORK = (work, work_full, WB)

        def maxima_uses(layer, p):
            return [(0, "mt", p, 0), (0, "mt", p, 1)] if layer == 0 else [(1, "mt", p)]

        def end_pass(e, n):
            e.drain().then_inc(finished, 1)
            e.wait_ge(next_sequence, n)

        LN_AT = {"first": 0, "next": 2, 1: 0, 2: 1, 3: 3}
        POW_AT = {"first": 0, "next": 4, 1: 0, 2: 2, 3: 6}

        def was_read(e, ring, sems, use):
            k, _, _, r, _ = ring.of[use]
            e.wait_ge(sems[k], r)

        def ab(i, rows, heads, half):
            w = heads * 2 * half
            if w <= 256:
                a, b = AB[0:rows, i % 2, 0:w], AB[0:rows, i % 2, 256:256 + w]
            else:
                a, b = AB[0:rows, 0, 0:w], AB[0:rows, 1, 0:w]
            return [z.rearrange("p (h j d) -> p h j d", j=2, d=half) for z in (a, b)]

        def transposed_heads(p, m, ps):
            what, t = PIECES[m]
            par = p % 2
            if what == "qk":
                return (ps[0:D0, :].rearrange("p (s k) -> p s k", s=4),
                        [QW[par][n][0:D0, :, t * P:(t + 1) * P] for n in range(2)])
            if what == "nv":
                return (ps[0:D0, :].rearrange("p (t h k) -> p t h k", t=2, h=2),
                        [K1[par][n][0:D0, :, KEEP + 2 * t * P:KEEP + 2 * (t + 1) * P]
                         .rearrange("p h (t k) -> p t h k", t=2) for n in range(2)])
            return (ps[0:D0, 0:2 * KEEP].rearrange("p (h k) -> p h k", h=2),
                    [K1[par][n][0:D0, :, 0:KEEP] for n in range(2)])

        def products_of(j):
            layer = int(j >= UNIT0[1])
            p, i = (j - UNIT0[layer]) // NU[layer], (j - UNIT0[layer]) % NU[layer]
            k = [i in units for units in PV[layer]].index(True)
            return PV0[layer] + p * NPV[layer] + k + 1

        loads = [(WS[:, :, :], w_small), (WIMP[:, :], w_imp), (WQ[0:QL, :], w_q), (WQ[QL:P, 0:1024], w_nv),
                 (GQ[:, :], g_q.partition_broadcast(P)), (GK[:, :], g_kv.partition_broadcast(P)),
                 (COS0[:, :, :], cos0), (SIN0[:, :, :], sin0), (COS1[:, :, :], cos1), (SIN1[:, :, :], sin1),
                 (ID[:, :], ident), (X2[:, 0, 0:P], causal), (X2[:, 1, 0:P], before), (X2[:, 2, 0:P], causal_t),
                 (EARLY[:, :], earlier), (RANKS[:, :], ranks),
                 (WP[:, :, :], w_proj), (WFC[:, :, :], w_fc), (WFP[:, :, :], w_ffp), (WQKV[:, :, :], w_qkv),
                 (WO[:, :, :], w_o), (WSG[:, :, :], w_sign)]
        ALL_LOADED = 16 * len(loads)
        SET_UP = 15
        x_rows = x.rearrange("(n p) c -> p n c", p=P)
        out_rows = out.rearrange("(n p) c -> p n c", p=P)

        @block.sync
        def _(sp):
            sp.dma_start(X0[:, :, :], x_rows[:, 0:NT, :]).then_inc(x_loaded, 16)
            for dst, src in loads:
                sp.dma_start(dst, src).then_inc(weights_loaded, 16)

            def next_pass():
                sp.wait_ge(finished, 4)
                sp.sem_clear(cleared)
                sp.sem_inc(next_sequence, 1)

            next_pass()
            with sp.Fori(0, B) as seq:
                def load_weights(p):
                    sp.dma_start(WKW[:, p % 2, :, :], w_kw[p]).then_inc(kw_loaded[p % 2], 16)
                    sp.dma_start(WSEL[:, p % 2, :, :], w_sel[p]).then_inc(sel_loaded[p % 2], 16)

                for p in range(2):
                    load_weights(p)
                for s in STEPS[0]:
                    if s[0] == "piece" and s[2] == NPIECE - 1 and s[1] + 2 < NPAIR:
                        full(sp, s, WORK)
                        load_weights(s[1] + 2)
                for i in range(2):
                    was_read(sp, work, work_read, ("proj", i))
                sp.dma_start(X0[:, :, :], x_rows[:, bass.ds(((seq + 1) % B) * NT, NT), :]).then_inc(x_loaded, 16)
                sp.wait_ge(out_ready, NT // 2)
                sp.dma_start(out_rows[:, bass.ds(seq * NT, NT), :], X2[:, :, :]).then_inc(x_stored, 16)
                next_pass()
            sp.wait_ge(x_stored, 16 * (B + 1))
            sp.wait_ge(x_loaded, 16 * (B + 1))

        @block.tensor
        def _(pe):
            mm = nc.tensor.matmul

            def take(use, bank):
                ring, full_sems, banks, read_sems = bank
                k, free_at, _, _, exp_at = ring.of[use]
                if exp_at > 0:
                    pe.wait_ge(exp_ready, exp_at)
                elif free_at > 0:
                    pe.wait_ge(read_sems[k], free_at)
                return banks[k], full_sems[k]

            W = (work, work_full, WB, work_read)

            def transpose_half(i, half):
                ps, done = take(("hT", i, half), W)
                for t in (2 * half, 2 * half + 1):
                    pe.wait_ge(h_ready, NT * LN_AT[i] + t + 1)
                    for c in range(NC):
                        last = nc.tensor.transpose(ps[:, (2 * c + t % 2) * P:(2 * c + t % 2 + 1) * P],
                                                   HN[:, t, c * P:(c + 1) * P], ID[:, :])
                last.then_inc(done, 1)

            def prologue(tag, j):
                def read(name):
                    was_read(pe, work, work_read, (tag, name))

                if j == 0:
                    for c in range(NC):
                        ps, done = take((tag, f"hT{c}"), W)
                        for t in range(NT):
                            if c == 0:
                                pe.wait_ge(h_ready, NT * LN_AT[tag] + t + 1)
                            last = nc.tensor.transpose(ps[:, t * P:(t + 1) * P], HN[:, t, c * P:(c + 1) * P], ID[:, :])
                        last.then_inc(done, 1)
                elif j == 1:
                    for c in range(NC):
                        read(f"hT{c}")
                    for i in range(2):
                        ps, done = take((tag, f"small{i}"), W)
                        for tt in range(2):
                            t = 2 * i + tt
                            for c in range(NC):
                                last = mm(ps[:, tt * C:tt * C + SM_W], HT0[:, c, t * P:(t + 1) * P], WS[:, c, :],
                                          start=(c == 0), stop=(c == NC - 1))
                        last.then_inc(done, 1)
                    ps, done = take((tag, "imp"), W)
                    for c in range(NC):
                        last = mm(ps[:, :], WI[:, c, :], HT0[:, c, :], start=(c == 0), stop=(c == NC - 1))
                    last.then_inc(done, 1)
                elif j == 2:
                    ps, done = take((tag, "score_cols"), W)
                    read("imp")
                    for t in range(NT):
                        last = nc.tensor.transpose(ps[:, t * P:(t + 1) * P], ROW[:, t * P:(t + 1) * P], ID[:, :])
                    last.then_inc(done, 1)
                    ps, done = take((tag, "gate"), W)
                    for i in range(2):
                        read(f"small{i}")
                    for t in range(NT):
                        last = mm(ps[:, 0:3], MEANW[:, :], SM[:, t, SM_W - 3:SM_W], start=(t == 0), stop=(t == NT - 1))
                    last.then_inc(done, 1)
                elif j == 3:
                    pe.wait_ge(latents_ready, 2 * NT)
                    for name, rows, c0 in (("nqT", QL, 0), ("ckvT", KVL, QL)):
                        ps, done = take((tag, name), W)
                        for t in range(NT):
                            last = nc.tensor.transpose(ps[0:rows, t * P:(t + 1) * P], NCK[:, t, c0:c0 + rows], ID[:, :])
                        last.then_inc(done, 1)
                elif j == 4:
                    ps, done = take((tag, "pos"), W)
                    pe.wait_ge(mask_ready, 1)
                    for t in range(NT):
                        for s in range(t + 1):
                            last = mm(ps[:, t:t + 1], (BEFB if s == t else ONEB)[:, :], MB[:, s:s + 1],
                                      start=(s == 0), stop=(s == t))
                    last.then_inc(done, 1)
                else:
                    ps, done = take((tag, "selT"), W)
                    pe.wait_ge(onehot_ready, 1)
                    for c in range(NC):
                        for t in range(NT):
                            last = mm(ps[:, c * KEEP:(c + 1) * KEEP], HN[:, t, c * P:(c + 1) * P], OH[:, t, :],
                                      start=(t == 0), stop=(t == NT - 1))
                    last.then_inc(done, 1)

            def piece(p, m):
                what, t = PIECES[m]
                ps, done = take(("piece", p, m), W)
                if what == "qk":
                    mm(ps[:, 0:192], NQT[0:QL, t * P:(t + 1) * P], WQ[0:QL, p * 192:(p + 1) * 192], start=True, stop=True)
                    if t == 0:
                        pe.wait_ge(kw_loaded[p % 2], 16 * (p // 2 + 1))
                    for c in range(NC):
                        last = mm(ps[:, 192:448], HT0[:, c, t * P:(t + 1) * P], WKW[:, p % 2, c, :],
                                  start=(c == 0), stop=(c == NC - 1))
                elif what == "nv":
                    for tt in range(2):
                        t2 = 2 * t + tt
                        last = mm(ps[:, tt * P:(tt + 1) * P], NQT[QL:P, t2 * P:(t2 + 1) * P],
                                  WQ[QL:P, p * P:(p + 1) * P], start=True, stop=True)
                else:
                    pe.wait_ge(sel_loaded[p % 2], 16 * (p // 2 + 1))
                    for c in range(NC):
                        last = mm(ps[0:KEEP, 0:256], SELT[:, c, :], WSEL[:, p % 2, c, :], start=(c == 0), stop=(c == NC - 1))
                last.then_inc(done, 1)

            def piece_transposes(p, m):
                what, t = PIECES[m]
                rows, heads = (KEEP, 2) if what == "sel" else (P, 4)
                was_read(pe, work, work_read, ("piece", p, m))
                pe.wait_ge(tok_ready, p * NPIECE + m + 1)
                ps, done = take(("piece_tr", p, m), W)
                for h in range(heads):
                    last = nc.tensor.transpose(ps[0:D0, h * rows:(h + 1) * rows],
                                               TOK[0:rows, (p * NPIECE + m) % 4, h, :], ID[0:rows, 0:rows])
                last.then_inc(done, 1)

            def max_scores(layer, p, i):
                u = MAX_UNITS[layer][i]
                if layer == 0 and i == 0:
                    for m in range(NPIECE):
                        was_read(pe, work, work_read, ("piece_tr", p, m))
                ps, done = take((layer, "max", p, i), W)
                for (h, src, k0, n, col, qt) in u["mm"]:
                    if layer == 0:
                        q = QW[p % 2][0][0:D0, h, qt * P:(qt + 1) * P]
                        k = K1[p % 2][0][0:D0, h, k0:k0 + n] if src == "k1" else QW[p % 2][0][0:D0, 2 + h, k0:k0 + n]
                    else:
                        q, k = QZ[:, p, h, qt * P:(qt + 1) * P], KB[:, p, k0:k0 + n]
                    masked = [c for c in u["mask"] if col <= c < col + n]
                    last = mm(ps[:, col:col + n], q, k, start=True, stop=not masked)
                    for c in masked:
                        last = mm(ps[:, c:c + P], IDB[:, :], CAUSB[:, :], start=False, stop=True)
                last.then_inc(done, 1)

            def transpose_maxima(layer, p):
                if layer == 0:
                    pe.wait_ge(max_ready, p + 1)
                    for h in range(2):
                        ps, done = take((0, "mt", p, h), W)
                        for t in range(NT):
                            c = h * NT + t
                            last = nc.tensor.transpose(ps[0:3, t * P:(t + 1) * P], NMX[:, p % 2, c:24:8], ID[:, :])
                        last.then_inc(done, 1)
                else:
                    was_read(pe, work, work_read, (1, "max", p, len(MAX_UNITS[1]) - 1))
                    ps, done = take((1, "mt", p), W)
                    for t in range(NT):
                        last = nc.tensor.transpose(ps[0:2, t * P:(t + 1) * P], NMX[:, p % 2, t:8:NT], ID[:, :])
                    last.then_inc(done, 1)

            def unit(layer, p, i):
                if i == 0:
                    for use in maxima_uses(layer, p):
                        was_read(pe, work, work_read, use)
                ps, done = take((layer, "unit", p, i), W)
                for (a, h, j, col) in UNITS[layer][i]:
                    q0, keys = j * P, (KEEP if layer == 0 and a == A2 else P)
                    out = ps[0:keys, col:col + T - q0]
                    causal_block = not (layer == 0 and a == A2)
                    if layer == 0:
                        q = [QW[p % 2][n][:, h, q0:T] for n in range(2)]
                        if a == A3:
                            k = [QW[p % 2][n][:, 2 + h, j * P:(j + 1) * P] for n in range(2)]
                        else:
                            k0 = 0 if a == A2 else KEEP + j * P
                            k = [K1[p % 2][n][:, h, k0:k0 + keys] for n in range(2)]
                        mm(out, k[0][0:D0 + 3], q[0][0:D0 + 3], start=True, stop=False)
                        mm(out, k[0][0:D0], q[1][0:D0], start=False, stop=False)
                        last = mm(out, k[1][0:D0], q[0][0:D0], start=False, stop=not causal_block)
                    else:
                        last = mm(out, KB[:, p, j * P:(j + 1) * P], QZ[:, p, h, q0:T], start=True, stop=False)
                    if causal_block:
                        last = mm(ps[:, col:col + P], IDB[:, :], CAUTB[:, :], start=False, stop=True)
                last.then_inc(done, 1)

            def values(layer, p, k):
                units = PV[layer][k]
                pe.wait_ge(exp_ready, UNIT0[layer] + p * NU[layer] + units[-1] + 1)
                if layer == 0 and p and k in (0, 2, 5):
                    pe.wait_ge(evacuated, 3 * (p - 1) + {0: A1, 2: A3, 5: A2}[k] + 1)
                elif layer and k == 0:
                    pe.wait_ge(evacuated, 3 * NPAIR + max(p // 2 - 2, 0))
                parts = [(i, part) for i in units for part in UNITS[layer][i]]
                parts.sort(key=lambda x: (x[1][0], x[1][2], x[1][1]))
                for n in range(0, len(parts), 2):
                    for side in range(2 - layer):
                        for i, (a, h, j, col) in parts[n:n + 2]:
                            rows = KEEP if layer == 0 and a == A2 else P
                            if side:
                                v = ONES[0:rows, :]
                            elif layer == 1:
                                v = VP[:, j, 2 * p + h, :]
                            elif a == A2:
                                v = VS[:, p % 3, h * VD:(h + 1) * VD]
                            else:
                                v = VV[:, p % 3, j, a, h * VD:(h + 1) * VD]
                            bank = OB[a if layer == 0 else p // 2 % 3]
                            row = 64 * (p % 2 if layer else side) + 32 * h
                            slot = (UNIT0[layer] + p * NU[layer] + i) % NP
                            last = mm(bank[row:row + 32, j * P:T], v, PR[0:rows, slot, col:col + T - j * P],
                                      start=(j == 0), stop=(j == 2 or a == A2), skip_group_check=True)
                last.then_inc(pv_done, 1)

            def transpose_tiles(use, src):
                ps, done = take(use, W)
                for t in range(NT):
                    last = nc.tensor.transpose(ps[:, t * P:(t + 1) * P], src(t), ID[:, :])
                last.then_inc(done, 1)

            def attention(layer):
                for s in STEPS[layer]:
                    if s[0] == "piece":
                        piece(s[1], s[2])
                    elif s[0] == "piece_tr":
                        piece_transposes(s[1], s[2])
                    elif s[0] == "max":
                        max_scores(layer, s[1], s[2])
                    elif s[0] == "mt":
                        transpose_maxima(layer, s[1])
                    elif s[0] == "unit":
                        unit(layer, s[1], s[2])
                    elif s[0] == "pv":
                        values(layer, s[1], s[2])
                    elif s[0] == "pro_pe":
                        prologue("next", s[1])
                    elif s[0] == "out_tr":
                        n = 3 * s[1] + s[2] if layer == 0 else 3 * NPAIR + s[1]
                        pe.wait_ge(evacuated, n + 1)
                        transpose_tiles((layer,) + s, lambda t: OE[layer][:, s[2] if layer == 0 else s[1] % 2, t * P:(t + 1) * P])
                    elif s[0] == "group":
                        if layer == 0:
                            pe.wait_ge(summed, 2 * s[1] + 2)
                        else:
                            was_read(pe, work, work_read, (1, "out_tr", s[1], 0))
                        transpose_tiles((layer,) + s, lambda t: OROWS[layer][:, s[1] % 2, t, :])

            def out_projection(name, layer, wt):
                for i in range(2):
                    ps, done = take((name, i), W)
                    for tt in range(2):
                        t = 2 * i + tt
                        for g in range(NG):
                            if i == 0 and tt == 0:
                                was_read(pe, work, work_read, (layer, "group", g))
                            last = mm(ps[:, tt * C:(tt + 1) * C], OT[:, g, t * P:(t + 1) * P], wt[:, g, :],
                                      start=(g == 0), stop=(g == NG - 1))
                    last.then_inc(done, 1)

            pe.wait_ge(weights_loaded, ALL_LOADED)
            pe.wait_ge(set_up, SET_UP)
            pe.wait_ge(set_up_act, 1)
            for j in range(6):
                prologue("first", j)
            end_pass(pe, 1)
            with pe.Fori(0, B) as seq:
                attention(0)
                out_projection("proj", 0, WP)

                for i in range(2):
                    transpose_half(1, i)
                for i in range(2):
                    was_read(pe, work, work_read, ("hT", 1, i))
                    for f2 in range(NF // 2):
                        ps, done = take(("fc", i, f2), W)
                        for side in range(2):
                            f = 2 * f2 + side
                            for c in range(NC):
                                last = mm(ps[:, side * 256:(side + 1) * 256], WFC[:, c, f * P:(f + 1) * P],
                                          HT[:, c, i * 256:(i + 1) * 256], start=(c == 0), stop=(c == NC - 1))
                        last.then_inc(done, 1)
                    ps, done = take(("y", i), W)
                    for tt in range(2):
                        for f in range(NF):
                            if tt == 0 and f % 2 == 0:
                                pe.wait_ge(squared, NF // 2 * i + f // 2 + 1)
                            hidden = R2[:, NF // 2 * i + f // 2, (f % 2) * 256 + tt * P:(f % 2) * 256 + (tt + 1) * P]
                            last = mm(ps[:, tt * C:(tt + 1) * C], hidden, WFP[:, f, :],
                                      start=(f == 0), stop=(f == NF - 1))
                    last.then_inc(done, 1)

                def values_of_half(i):
                    transpose_half(2, i)
                    was_read(pe, work, work_read, ("hT", 2, i))
                    ps, done = take(("v", i), W)
                    for tt in range(2):
                        t = 2 * i + tt
                        for c in range(NC):
                            last = mm(ps[:, tt * C:(tt + 1) * C], HT[:, c, t * P:(t + 1) * P],
                                      WQKV[:, c, 2 * C:3 * C], start=(c == 0), stop=(c == NC - 1))
                    last.then_inc(done, 1)

                def transpose_heads(t):
                    pe.wait_ge(stacked, 2 * (t + 1))
                    for n in range(4):
                        ps, done = take(("heads", t, n), W)
                        for g in range(4):
                            h = 2 * (4 * (n % 2) + g)
                            src = (QS if n < 2 else KS)[:, h:h + 2, :, :].rearrange("p h s d -> p (h s d)")
                            last = nc.tensor.transpose(ps[:, g * P:(g + 1) * P], src, ID[:, :])
                        last.then_inc(done, 1)

                for what, n in QKV_STEPS:
                    if what == "half":
                        values_of_half(n)
                    elif what == "heads":
                        transpose_heads(n)
                    else:
                        ps, done = take(("qk1", n), W)
                        for c in range(NC):
                            last = mm(ps[:, :], HT[:, c, n * P:(n + 1) * P], WQKV[:, c, 0:2 * C],
                                      start=(c == 0), stop=(c == NC - 1))
                        last.then_inc(done, 1)
                for t in range(NT):
                    for n in range(4):
                        was_read(pe, work, work_read, ("heads", t, n))
                for i in range(2):
                    was_read(pe, work, work_read, ("v", i))
                attention(1)
                out_projection("o", 1, WO)

                for i in range(2):
                    transpose_half(3, i)
                    was_read(pe, work, work_read, ("hT", 3, i))
                    ps, done = take(("sign", i), W)
                    for tt in range(2):
                        t = 2 * i + tt
                        for c in range(NC):
                            last = mm(ps[:, tt * C:(tt + 1) * C], HT[:, c, t * P:(t + 1) * P], WSG[:, c, :],
                                      start=(c == 0), stop=(c == NC - 1))
                    last.then_inc(done, 1)
                end_pass(pe, seq + 2)

        @block.vector
        def _(dve):
            v = nc.vector
            steps = [0]

            def then(ins):
                steps[0] += 1
                ins.then_inc(dve_step, 1)
                dve.wait_ge(dve_step, steps[0])

            def read_work(ins, use):
                ins.then_inc(work_read[work.of[use][0]], 1)

            def rsqrt(i, n, c0=0):
                dve.wait_ge(pow_done, i + 1)
                na, y, var, rstd = (z[:, c0:c0 + n] for z in (NA, YP, VAR, RSTD))
                then(v.tensor_tensor(na, var, y, ALU.mult))
                then(v.tensor_tensor(na, na, y, ALU.mult))
                then(v.tensor_scalar(na, na, -0.5, 1.5, ALU.mult, ALU.add))
                then(v.tensor_tensor(rstd, na, y, ALU.mult))

            def variances(X, t0=0, n=NT):
                for t in range(t0, t0 + n):
                    ins = v.bn_stats(BN[:, t, :], X[:, t, :])
                then(ins)
                for t in range(t0, t0 + n):
                    ins = v.bn_aggr(MV[:, t, :], BN[:, t, :])
                then(ins)
                v.tensor_scalar(VAR[:, t0:t0 + n], MV[:, t0:t0 + n, 1], LN_EPS, None, ALU.add).then_inc(var_ready, 1)

            def normalised_rows(pow_index, X, t0=0, n=NT):
                rsqrt(pow_index, n, t0)
                for t in range(t0, t0 + n):
                    v.tensor_scalar(HN[:, t, :], X[:, t, :], MV[:, t, 0:1], RSTD[:, t:t + 1],
                                    ALU.subtract, ALU.mult).then_inc(h_ready, 1)

            def rope_products(ps4, cos, sin, a4, b4):
                one = v.tensor_tensor(a4, ps4, cos, ALU.mult)
                two = v.tensor_tensor(b4, ps4[:, :, ::-1, :], sin, ALU.mult)
                return one, two

            def piece(p, m):
                what, t = PIECES[m]
                if what == "nv":
                    return
                rows, heads = (KEEP, 2) if what == "sel" else (P, 4)
                ps = full(dve, ("piece", p, m), WORK)
                i = p * len(ROPED) + ROPED.index(m)
                if i >= 2:
                    q = (i - 2) // len(ROPED) * NPIECE + ROPED[(i - 2) % len(ROPED)]
                    dve.wait_ge(tok_ready, q + 1)
                a4, b4 = ab(i, rows, heads, 32)
                src = ps[0:rows, 0:heads * D0].rearrange("p (h d) -> p h d", h=heads)[:, :, NOPE:D0]
                src = src.rearrange("p h (j d) -> p h j d", j=2)
                cos = COS0[0:rows, t:t + 1, :].unsqueeze(1).broadcast_to([rows, heads, 2, 32])
                sin = SIN0[0:rows, t:t + 1, :].rearrange("p a (j d) -> p a j d", j=2).broadcast_to([rows, heads, 2, 32])
                one, two = rope_products(src, cos, sin, a4, b4)
                read_work(one, ("piece", p, m))
                read_work(two, ("piece", p, m))

            def low_parts(p, m):
                use = ("piece_tr", p, m)
                k, _, _, r, _ = work.of[use]
                ps = full(dve, use, WORK)
                dve.wait_ge(work_read[k], r - 1)
                src, dst = transposed_heads(p, m, ps)
                read_work(v.tensor_tensor(dst[1], src, dst[0].bitcast(F32), ALU.subtract), use)

            def maxima(layer, p, i):
                u = MAX_UNITS[layer][i]
                ps = full(dve, (layer, "max", p, i), WORK)
                if i == 0 and layer * NPAIR + p >= 2:
                    full(dve, maxima_uses(*((layer, p - 2) if p >= 2 else (0, NPAIR - 2 + p)))[-1], WORK)
                for n, (lo, hi, att, h, qt) in enumerate(u["segs"]):
                    if att is None:
                        dst = NPART[:, h:h + 1]
                    else:
                        c = (att * 2 + h) * NT + qt
                        dst = NMX[:, p % 2, c:c + 1]
                    last = v.tensor_reduce(dst, ps[:, lo:hi], AX.X, ALU.max, negate=True)
                read_work(last, (layer, "max", p, i))
                if layer == 0 and i == len(MAX_UNITS[0]) - 1:
                    was_read(dve, work, work_read, (layer, "max", p, i))
                    c = NT - 1
                    dst = NMX[:, p % 2, c:c + NT + 1:NT]
                    v.tensor_tensor(dst, dst, NPART[:, :], ALU.min).then_inc(max_ready, 1)

            def normalise(layer, n, att):
                use = (layer, "out_tr", n, att)
                ps = full(dve, use, WORK)
                if layer == 0:
                    rows = ps[:, :].rearrange("p (t s h d) -> p t s h d", t=NT, s=2, h=2)
                    outputs, sums, heads, width = rows[:, :, 0, :, :], rows[:, :, 1, :, 0], 2, VD
                    dst = GATED[:, att, :, :, :]
                    if n and att == A1:
                        dve.wait_ge(summed, n)
                else:
                    outputs = ps[:, :].rearrange("p (t h d) -> p t h d", t=NT, d=DP)
                    sums, heads, width = outputs[:, :, :, D1], HG, DP
                    dst = OROWS[1][:, n % 2, :, :].rearrange("p t (h d) -> p t h d", h=HG)
                    if n >= 2:
                        full(dve, (1, "group", n - 2), WORK)
                rs = RSUM[:, att, :, 0:heads]
                then(v.reciprocal(rs, sums))
                if layer == 0:
                    g = 1 if att == A1 else 2 if att == A3 else 0
                    then(v.tensor_scalar(rs, rs, GG[:, g:g + 1], None, ALU.mult))
                read_work(v.tensor_tensor(dst, outputs, rs.unsqueeze(3).broadcast_to([P, NT, heads, width]), ALU.mult), use)

            def attention(layer, seq):
                for s in STEPS[layer]:
                    if s[0] == "piece":
                        piece(s[1], s[2])
                    elif s[0] == "piece_tr":
                        low_parts(s[1], s[2])
                    elif s[0] == "max":
                        maxima(layer, s[1], s[2])
                    elif s[0] == "norm":
                        normalise(layer, s[1], s[2])
                    elif s[0] == "pro":
                        prologue("next", s[1], 16 * seq + 32)

            def prologue(tag, j, loads):
                def filled(name):
                    return full(dve, (tag, name), WORK)

                def read(ins, name):
                    read_work(ins, (tag, name))

                def wait_read(name):
                    was_read(dve, work, work_read, (tag, name))

                if j == 0:
                    dve.wait_ge(x_loaded, loads)
                    variances(X0)
                elif j == 1:
                    normalised_rows(POW_AT[tag], X0)
                elif j == 3:
                    ps = filled("small0")
                    read(v.tensor_copy(SM[:, 0:2, 0:SM_W], ps[:, :].rearrange("p (t c) -> p t c", t=2)[:, :, 0:SM_W]),
                         "small0")
                    wait_read("small0")
                    wait_read("small1")
                    sq = AB[:, 0, :].rearrange("p (t c) -> p t c", t=NT)
                    then(v.tensor_tensor(sq, SM[:, :, 0:P], SM[:, :, 0:P], ALU.mult))
                    v.tensor_reduce(NA[:, 0:NT], sq[:, :, 0:QL], AX.X, ALU.add)
                    then(v.tensor_reduce(NA[:, NT:2 * NT], sq[:, :, QL:P], AX.X, ALU.add))
                    then(v.tensor_scalar(VAR[:, 0:NT], NA[:, 0:NT], 1.0 / QL, RMS_EPS, ALU.mult, ALU.add))
                    v.tensor_scalar(VAR[:, NT:2 * NT], NA[:, NT:2 * NT], 1.0 / KVL, RMS_EPS, ALU.mult,
                                    ALU.add).then_inc(var_ready, 1)
                    kr_ab = [AB[:, 1, 256 * k:256 * (k + 1)].rearrange("p (t j d) -> p t j d", t=NT, j=2) for k in range(2)]
                    krs = SM[:, :, P:P + ROPE].rearrange("p t (j d) -> p t j d", j=2)
                    v.tensor_tensor(kr_ab[0], krs, COS0[:, :, :].unsqueeze(2).broadcast_to([P, NT, 2, 32]), ALU.mult)
                    v.tensor_tensor(kr_ab[1], krs[:, :, ::-1, :], SIN0[:, :, :].rearrange("p t (j d) -> p t j d", j=2),
                                    ALU.mult).then_inc(kr_products, 1)
                elif j == 4:
                    ps = filled("score_cols")
                    read(v.tensor_copy(SC[:, :], ps[:, ::P]), "score_cols")
                    ps = filled("gate")
                    read(v.tensor_copy(GS[:, :], ps[:, 0:3]), "gate")
                    rsqrt(POW_AT[tag] + 1, 2 * NT)
                    then(v.tensor_scalar(RSTD[:, 0:NT], RSTD[:, 0:NT], Q_SCALE, None, ALU.mult))
                    for t in range(NT):
                        v.scalar_tensor_tensor(NCK[:, t, 0:QL], SM[:, t, 0:QL], RSTD[:, t:t + 1], GQ[:, :],
                                               ALU.mult, ALU.mult).then_inc(latents_ready, 1)
                        v.scalar_tensor_tensor(NCK[:, t, QL:P], SM[:, t, QL:P], RSTD[:, NT + t:NT + t + 1], GK[:, :],
                                               ALU.mult, ALU.mult).then_inc(latents_ready, 1)
                elif j == 5:
                    ps = filled("ckvT")
                    read(v.tensor_copy(NQT[QL:P, :], ps[0:KVL, :]), "ckvT")
                    wait_read("gate")
                    v.tensor_reduce(GM[:, :], GS[:, :], AX.X, ALU.max, negate=True).then_inc(gate_in, 1)
                    wait_read("score_cols")
                    wait_read("imp")
                    for t in range(NT):
                        then(v.tensor_scalar(AB[:, 0, :], ROW, SC[:, t:t + 1], None, ALU.is_gt, ALU.add,
                                             accum_out=CG[:, t:t + 1]))
                        then(v.scalar_tensor_tensor(AB[:, 0, :], ROW, SC[:, t:t + 1],
                                                    EARLY[:, (3 - t) * P:(3 - t) * P + T], ALU.is_equal, ALU.mult,
                                                    accum_out=CE[:, t:t + 1]))
                    then(v.tensor_tensor(CG[:, :], CG[:, :], CE[:, :], ALU.add))
                    then(v.tensor_scalar(MF[:, :], CG[:, :], KEEP - 0.5, None, ALU.is_lt))
                    v.tensor_copy(MB[:, :], MF[:, :]).then_inc(mask_ready, 1)
                elif j == 6:
                    ps = filled("pos")
                    read(v.tensor_copy(POS[:, :], ps[:, 0:NT]), "pos")
                    wait_read("pos")
                    for t in range(NT):
                        last = v.tensor_scalar(OH[:, t, :], RANKS[:, :], POS[:, t:t + 1], MF[:, t:t + 1],
                                               ALU.is_equal, ALU.mult)
                    last.then_inc(onehot_ready, 1)
                elif j == 7:
                    dve.wait_ge(gate_exp, 1)
                    then(v.reciprocal(GD[:, 1:2], GD[:, 0:1]))
                    then(v.tensor_scalar(GG[:, :], GE[:, :], GD[:, 1:2], None, ALU.mult))
                    ps = filled("selT")
                    read(v.tensor_copy(SELT[:, :, :], ps[:, 0:2 * KEEP].rearrange("p (c k) -> p c k", c=NC)), "selT")

            def add_half(name, i, src, dst):
                ps = full(dve, (name, i), WORK)
                half = slice(2 * i, 2 * i + 2)
                read_work(v.tensor_tensor(dst[:, half, :], src[:, half, :],
                                          ps[:, :].rearrange("p (t c) -> p t c", t=2), ALU.add), (name, i))
                was_read(dve, work, work_read, (name, i))
                variances(dst, 2 * i, 2)

            dve.sem_inc(x_stored, 16)
            dve.wait_ge(weights_loaded, ALL_LOADED)
            v.tensor_copy(WI[:, :, :], WIMP[:, :].unsqueeze(2).broadcast_to([P, NC, P])).then_inc(set_up, 1)
            v.tensor_copy(IDB[:, :], ID[:, :]).then_inc(set_up, 1)
            v.tensor_copy(CAUSB[:, :], X2[:, 0, 0:P]).then_inc(set_up, 1)
            v.tensor_copy(BEFB[:, :], X2[:, 1, 0:P]).then_inc(set_up, 1)
            v.tensor_copy(CAUTB[:, :], X2[:, 2, 0:P]).then_inc(set_up, 1)
            v.memset(ONEB[:, :], 1.0).then_inc(set_up, 1)
            v.memset(MEANW[:, :], 1.0 / T).then_inc(set_up, 1)
            v.memset(MHALF[:, :], -0.5).then_inc(set_up, 1)
            v.tensor_scalar(WS[:, :, P:P + ROPE], WS[:, :, P:P + ROPE], 1.0 / H, None, ALU.mult).then_inc(set_up, 1)
            v.tensor_scalar(WQKV[:, :, 0:C], WQKV[:, :, 0:C], float(D1) ** -0.5, None, ALU.mult).then_inc(set_up, 1)
            v.memset(ONES[:, :], 1.0).then_inc(set_up, 1)
            for h in range(2):
                for n in range(2):
                    v.memset(HEAD[64 * n:64 * n + 64, h:h + 1], float(n == h)).then_inc(set_up, 1)
            dve.wait_ge(set_up, SET_UP)
            for j in range(8):
                prologue("first", j, 16)
            end_pass(dve, 1)
            steps[0] = 0
            with dve.Fori(0, B) as seq:
                attention(0, seq)
                for i in range(2):
                    add_half("proj", i, X0, X1)
                for i in range(2):
                    normalised_rows(POW_AT[1] + i, X1, 2 * i, 2)

                def keys_out(t):
                    for n in (2, 3):
                        ps = full(dve, ("heads", t, n), WORK)
                        read_work(v.tensor_copy(KB[:, 4 * (n - 2):4 * (n - 1), t * P:(t + 1) * P],
                                                ps[:, :].rearrange("p (g k) -> p g k", g=4)), ("heads", t, n))

                def rope(t):
                    ps = full(dve, ("qk1", t), WORK)
                    if t:
                        dve.wait_ge(roped1, t)
                    a4, b4 = ab(0, P, 2 * H, 8)
                    cos = COS1[:, t:t + 1, :].unsqueeze(1).broadcast_to([P, 2 * H, 2, 8])
                    sin = SIN1[:, t:t + 1, :].rearrange("p a (j d) -> p a j d", j=2).broadcast_to([P, 2 * H, 2, 8])
                    one, two = rope_products(ps[:, :].rearrange("p (h j d) -> p h j d", j=2, d=8), cos, sin, a4, b4)
                    read_work(one, ("qk1", t))
                    read_work(two, ("qk1", t))

                def stack_low(t):
                    dve.wait_ge(stacked_hi, 2 * (t + 1))
                    v.tensor_tensor(QS[:, :, 1, :].bitcast(F32R), ROPED1[:, t % 2, 0:H, :], QS[:, :, 0, :],
                                    ALU.subtract).then_inc(stacked, 1)
                    v.tensor_tensor(KS[:, :, 3, :].bitcast(F32R), ROPED1[:, t % 2, H:2 * H, :], KS[:, :, 0, :],
                                    ALU.subtract).then_inc(stacked, 1)

                def spikes(i, between={}):
                    Y, NEGM, DRIVEN, SUM = (STATE[:, i, n, :] for n in range(4))
                    was_read(dve, work, work_read, ("y", i))
                    v.tensor_scalar(SUM, Y, 1.0, None, ALU.is_gt)
                    then(v.scalar_tensor_tensor(DRIVEN, Y, 0.9, Y, ALU.mult, ALU.add))
                    then(v.scalar_tensor_tensor(NEGM, Y, 1.0, DRIVEN, ALU.is_gt, ALU.subtract))
                    for step in range(3):
                        v.scalar_tensor_tensor(SUM, NEGM, -1.0, SUM, ALU.is_lt, ALU.add)
                        then(v.scalar_tensor_tensor(DRIVEN, NEGM, -0.9, Y, ALU.mult, ALU.add))
                        then(v.scalar_tensor_tensor(NEGM, NEGM, -1.0, DRIVEN, ALU.is_lt, ALU.subtract))
                        if step in between:
                            between[step]()
                    then(v.scalar_tensor_tensor(SUM, NEGM, -1.0, SUM, ALU.is_lt, ALU.add))
                    if i == 0:
                        dve.wait_ge(x_stored, 16 * seq + 16)
                    half = slice(2 * i, 2 * i + 2)
                    then(v.scalar_tensor_tensor(X2[:, half, :].rearrange("p t c -> p (t c)"), SUM, 0.2,
                                                X1[:, half, :].rearrange("p t c -> p (t c)"), ALU.mult, ALU.add))
                    variances(X2, 2 * i, 2)

                spikes(0)
                normalised_rows(POW_AT[2], X2, 0, 2)
                spikes(1, {0: lambda: rope(0), 1: lambda: rope(1), 2: lambda: stack_low(0)})
                normalised_rows(POW_AT[2] + 1, X2, 2, 2)
                keys_out(0)
                stack_low(1)
                rope(2)
                keys_out(1)
                stack_low(2)
                rope(3)
                keys_out(2)
                stack_low(3)
                keys_out(3)
                attention(1, seq)
                for i in range(2):
                    add_half("o", i, X2, X1)
                for i in range(2):
                    normalised_rows(POW_AT[3] + i, X1, 2 * i, 2)
                for i in range(2):
                    ps = full(dve, ("sign", i), WORK)
                    v.tensor_tensor(X2[:, 2 * i:2 * i + 2, :], X1[:, 2 * i:2 * i + 2, :],
                                    ps[:, :].rearrange("p (t c) -> p t c", t=2), ALU.add).then_inc(out_ready, 1)
                end_pass(dve, seq + 2)

        @block.scalar
        def _(act):
            a = nc.scalar

            def copy(dst, src):
                return a.activation(dst, src, ACT.Copy)

            def read_work(ins, use):
                ins.then_inc(work_read[work.of[use][0]], 1)

            def selecting_rows(par):
                for row, dst in ((A3, QW[par][0][D0:D0 + 3, 2:4, :]), (A2, K1[par][0][D0:D0 + 3, :, 0:KEEP]),
                                 (A1, K1[par][0][D0:D0 + 3, :, KEEP:])):
                    one = ID[D0:D0 + 3, D0 + row:D0 + row + 1].unsqueeze(2).broadcast_to(list(dst.shape))
                    copy(dst, one)

            def half_out(i, half):
                ps = full(act, ("hT", i, half), WORK)
                read_work(copy(HT[:, :, half * 256:(half + 1) * 256], ps[:, :].rearrange("p (c k) -> p c k", c=NC)),
                          ("hT", i, half))

            def prologue(tag, j):
                copies = {2: [("hT0", HT0[:, 0, :], lambda ps: ps[:, :]), ("hT1", HT0[:, 1, :], lambda ps: ps[:, :])],
                          3: [("small1", SM[:, 2:4, 0:SM_W],
                               lambda ps: ps[:, :].rearrange("p (t c) -> p t c", t=2)[:, :, 0:SM_W]),
                              ("imp", ROW, lambda ps: ps[:, :])],
                          5: [("nqT", NQT[0:QL, :], lambda ps: ps[0:QL, :])]}
                for name, dst, src in copies.get(j, []):
                    ps = full(act, (tag, name), WORK)
                    read_work(copy(dst, src(ps)), (tag, name))
                if j == 6:
                    act.wait_ge(gate_in, 1)
                    a.activation(GE[:, :], GS[:, :], ACT.Exp, bias=GM[:, 0:1], accum_out=GD[:, 0:1]).then_inc(gate_exp, 1)

            def piece(p, m):
                what, t = PIECES[m]
                rows, heads = (KEEP, 2) if what == "sel" else (P, 4)
                use = ("piece", p, m)
                ps = full(act, use, WORK)
                k, _, _, r, _ = work.of[use]
                if what != "nv":
                    act.wait_ge(work_read[k], r - 2)
                i = p * NPIECE + m
                if i >= 4:
                    full(act, ("piece_tr", (i - 4) // NPIECE, (i - 4) % NPIECE), WORK)
                if what == "nv":
                    both = ps[:, 0:2 * P].rearrange("p (t n) -> p t n", t=2)
                    src = both[:, :, 0:64].rearrange("p t (h d) -> p t h d", h=2)
                    dst = TOK[:, i % 4, :, 0:NOPE].rearrange("p (t h) d -> p t h d", t=2)
                    read_work(copy(dst, src), use)
                    read_work(copy(VV[:, p % 3, 2 * t:2 * t + 2, A1, :], both[:, :, 64:P]), use)
                else:
                    src = ps[0:rows, 0:heads * D0].rearrange("p (h d) -> p h d", h=heads)[:, :, 0:NOPE]
                    read_work(copy(TOK[0:rows, i % 4, 0:heads, 0:NOPE], src), use)
                    if what == "qk":
                        read_work(copy(VV[:, p % 3, t, A3, :], ps[:, 384:448]), use)
                    else:
                        read_work(copy(VS[:, p % 3, :], ps[0:KEEP, 192:256]), use)

            def high_parts(p, m):
                ps = full(act, ("piece_tr", p, m), WORK)
                src, dst = transposed_heads(p, m, ps)
                read_work(copy(dst[0], src), ("piece_tr", p, m))

            def maxima_out(layer, p):
                for h in range(2):
                    if layer == 0:
                        ps = full(act, (0, "mt", p, h), WORK)
                        read_work(copy(QW[p % 2][0][D0:D0 + 3, h, :], ps[0:3, :]), (0, "mt", p, h))
                    else:
                        ps = full(act, (1, "mt", p), WORK)
                        read_work(a.activation(QZ[2 * D1:2 * D1 + 2, p, h, :], ps[0:2, :], ACT.Copy,
                                               scale=ID[0:2, h:h + 1]), (1, "mt", p))

            def outputs(layer, n, att):
                if layer == 0:
                    act.wait_ge(pv_done, PV0[0] + n * NPV[0] + (6 if att == A2 else 5))
                    if n:
                        full(act, (0, "out_tr", n - 1, att), WORK)
                    copy(OE[0][:, att, :], OB[att][:, :]).then_inc(evacuated, 1)
                else:
                    act.wait_ge(pv_done, PV0[1] + 2 * (n + 1) * NPV[1])
                    if n >= 2:
                        full(act, (1, "out_tr", n - 2, 0), WORK)
                    copy(OE[1][:, n % 2, :], OB[n % 3][:, :]).then_inc(evacuated, 1)

            def group_out(layer, g):
                ps = full(act, (layer, "group", g), WORK)
                read_work(copy(OT[:, g, :], ps[:, :]), (layer, "group", g))

            def exponentials(layer, p, i):
                j = UNIT0[layer] + p * NU[layer] + i
                ps = full(act, (layer, "unit", p, i), WORK)
                if j >= NP:
                    act.wait_ge(pv_done, products_of(j - NP))
                rows = KEEP if layer == 0 and UNITS[0][i][0][0] == A2 else P
                a.activation(PR[0:rows, j % NP, :], ps[0:rows, :], ACT.Exp).then_inc(exp_ready, 1)

            def attention(layer):
                for s in STEPS[layer]:
                    if s[0] == "piece":
                        piece(s[1], s[2])
                    elif s[0] == "piece_tr":
                        high_parts(s[1], s[2])
                    elif s[0] == "mt_out":
                        maxima_out(layer, s[1])
                    elif s[0] == "unit":
                        exponentials(layer, s[1], s[2])
                    elif s[0] == "out":
                        outputs(layer, s[1], s[2])
                    elif s[0] == "group_out":
                        group_out(layer, s[1])
                    elif s[0] == "pro":
                        prologue("next", s[1])

            act.wait_ge(weights_loaded, ALL_LOADED)
            act.wait_ge(set_up, SET_UP)
            a.activation(WSG[:, :, :], WSG[:, :, :], ACT.Sign).then_inc(set_up_act, 1)
            for par in range(2):
                selecting_rows(par)
            for j in range(8):
                prologue("first", j)
            end_pass(act, 1)
            with act.Fori(0, B) as seq:
                attention(0)
                for i in range(2):
                    half_out(1, i)
                for i in range(2):
                    for f2 in range(NF // 2):
                        ps = full(act, ("fc", i, f2), WORK)
                        f = NF // 2 * i + f2
                        if f >= 2:
                            act.wait_ge(squared, f - 1)
                        read_work(a.activation(AB[:, f % 2, :], ps[:, :], ACT.Relu), ("fc", i, f2))
                    ps = full(act, ("y", i), WORK)
                    read_work(copy(STATE[:, i, 0, :], ps[:, :]), ("y", i))

                def values_of_half(i):
                    half_out(2, i)
                    if i == 0:
                        act.wait_ge(values_set, 1)
                    ps = full(act, ("v", i), WORK)
                    src = ps[:, :].rearrange("p (t h d) -> p t h d", t=2, d=D1)
                    read_work(copy(VP[:, 2 * i:2 * i + 2, :, 0:D1], src), ("v", i))

                def queries_out(t):
                    for n in range(2):
                        ps = full(act, ("heads", t, n), WORK)
                        for h in range(2):
                            read_work(a.activation(QZ[:, 4 * n:4 * n + 4, h, t * P:(t + 1) * P],
                                                   ps[:, :].rearrange("p (g k) -> p g k", g=4), ACT.Copy,
                                                   scale=HEAD[:, h:h + 1]), ("heads", t, n))

                def stack_high(t):
                    act.wait_ge(roped1, t + 1)
                    if t:
                        for n in range(4):
                            full(act, ("heads", t - 1, n), WORK)
                    q = ROPED1[:, t % 2, 0:H, :].unsqueeze(2).broadcast_to([P, H, 2, D1])
                    k = ROPED1[:, t % 2, H:2 * H, :].unsqueeze(2).broadcast_to([P, H, 2, D1])
                    copy(QS[:, :, 0:4:3, :].bitcast(F32R), q).then_inc(stacked_hi, 1)
                    copy(KS[:, :, 0:2, :].bitcast(F32R), k).then_inc(stacked_hi, 1)

                values_of_half(0)
                act.wait_ge(zeroed, 1)
                stack_high(0)
                stack_high(1)
                queries_out(0)
                values_of_half(1)
                for t in range(2, NT):
                    stack_high(t)
                    queries_out(t - 1)
                queries_out(NT - 1)
                attention(1)
                full(act, ("o", 0), WORK)
                selecting_rows(0)
                for i in range(2):
                    half_out(3, i)
                selecting_rows(1)
                end_pass(act, seq + 2)

        @block.gpsimd
        def _(pool):
            gp = nc.gpsimd

            def power(i, n, c0=0):
                pool.wait_ge(var_ready, i + 1)
                gp.tensor_tensor(YP[:, c0:c0 + n], VAR[:, c0:c0 + n], MHALF[:, c0:c0 + n], ALU.pow).then_inc(pow_done, 1)

            def piece(p, m):
                what, t = PIECES[m]
                rows, heads = (KEEP, 2) if what == "sel" else (P, 4)
                i = p * NPIECE + m
                if i >= 4:
                    full(pool, ("piece_tr", (i - 4) // NPIECE, (i - 4) % NPIECE), WORK)
                dst = TOK[0:rows, i % 4, 0:heads, NOPE:D0]
                if what == "nv":
                    gp.tensor_copy(dst.rearrange("p (t h) d -> p t h d", t=2),
                                   KR[:, 2 * t:2 * t + 2, :].unsqueeze(2).broadcast_to([P, 2, 2, ROPE])).then_inc(tok_ready, 1)
                    return
                k, _, _, r, _ = work.of[("piece", p, m)]
                pool.wait_ge(work_read[k], r - 2)
                a4, b4 = ab(p * len(ROPED) + ROPED.index(m), rows, heads, 32)
                merge = "p h j d -> p h (j d)"
                gp.tensor_tensor(dst, a4.rearrange(merge), b4.rearrange(merge), ALU.add).then_inc(tok_ready, 1)

            def sum_attentions(p):
                was_read(pool, work, work_read, (0, "out_tr", p, A2))
                if p >= 4 and p % 2 == 0:
                    full(pool, (0, "group", p // 2 - 2), WORK)
                flat = [GATED[:, a, :, :, :].rearrange("p t h d -> p t (h d)") for a in range(3)]
                gp.tensor_tensor(flat[A1], flat[A1], flat[A3], ALU.add).then_inc(pool_step, 1)
                pool.wait_ge(pool_step, p + 1)
                gp.tensor_tensor(OROWS[0][:, p // 2 % 2, :, 64 * (p % 2):64 * (p % 2) + 64], flat[A1], flat[A2],
                                 ALU.add).then_inc(summed, 1)

            def prologue(tag):
                power(POW_AT[tag], NT)
                power(POW_AT[tag] + 1, 2 * NT)
                pool.wait_ge(kr_products, 1)
                gp.tensor_tensor(KR[:, :, :], AB[:, 1, 0:256].rearrange("p (t d) -> p t d", t=NT),
                                 AB[:, 1, 256:512].rearrange("p (t d) -> p t d", t=NT), ALU.add)

            def attention0():
                for s in STEPS[0]:
                    if s[0] == "piece":
                        piece(s[1], s[2])
                    elif s[0] == "norm" and s[2] == A2:
                        sum_attentions(s[1])

            pool.wait_ge(set_up, SET_UP)
            prologue("first")
            end_pass(pool, 1)
            with pool.Fori(0, B) as seq:
                attention0()
                for i in range(2):
                    power(POW_AT[1] + i, 2, 2 * i)
                for i in range(2):
                    for f2 in range(NF // 2):
                        was_read(pool, work, work_read, ("fc", i, f2))
                        f = NF // 2 * i + f2
                        gp.tensor_tensor(R2[:, f, :], AB[:, f % 2, :], AB[:, f % 2, :], ALU.mult).then_inc(squared, 1)
                    if i == 0:
                        gp.memset(SMALL[:, 0:2048], 0.0).then_inc(pool_step, 1)
                pool.wait_ge(pool_step, NPAIR + 1)
                gp.memset(KS[:, :, 2, 0:2], 1.0).then_inc(zeroed, 1)
                power(POW_AT[2], 2)
                gp.memset(VP, 1.0).then_inc(values_set, 1)
                for t in range(NT):
                    if t == 2:
                        power(POW_AT[2] + 1, 2, 2)
                    was_read(pool, work, work_read, ("qk1", t))
                    if t >= 2:
                        pool.wait_ge(stacked, 2 * (t - 1))
                    gp.tensor_tensor(ROPED1[:, t % 2, :, :], AB[:, 0, :].rearrange("p (h d) -> p h d", d=D1),
                                     AB[:, 1, :].rearrange("p (h d) -> p h d", d=D1), ALU.add).then_inc(roped1, 1)
                prologue("next")
                for i in range(2):
                    power(POW_AT[3] + i, 2, 2 * i)
                end_pass(pool, seq + 2)


def head_cols(w, perm):
    rows = w.shape[0]
    return w.reshape(rows, H, -1)[:, :, perm].reshape(rows, -1)


def kernel(**inputs):
    import concourse.bacc as bacc
    from concourse.bass_utils import run_bass_kernel_spmd

    a = {k: np.asarray(v) for k, v in inputs.items()}
    L = lambda name: a["L0_attn_" + name]

    def halves(w):
        return np.ascontiguousarray(w.reshape(-1, P, w.shape[1]).transpose(1, 0, 2))

    q = np.concatenate([L("w_dq_nope").reshape(QL, H, NOPE), L("w_dq_rope").reshape(QL, H, ROPE)], 2).reshape(QL, -1)
    nv = np.concatenate([L("w_dk_nope").reshape(KVL, NPAIR, 64), L("w_dv").reshape(KVL, NPAIR, 64)], 2).reshape(KVL, -1)

    def paired(wk, wv):
        both = np.concatenate([wk.reshape(NC, P, NPAIR, 2 * D0), wv.reshape(NC, P, NPAIR, 2 * VD)], 3)
        return np.ascontiguousarray(both.transpose(2, 1, 0, 3))

    even_odd = np.concatenate([np.arange(0, D1, 2), np.arange(1, D1, 2)])
    wqkv = np.ascontiguousarray(a["L1_attn_W_qkv"].T)
    wqkv = np.concatenate([head_cols(wqkv[:, 0:C], even_odd), head_cols(wqkv[:, C:2 * C], even_odd), wqkv[:, 2 * C:]], 1)
    wo = np.zeros((H, DP, C), a["L1_attn_W_o"].dtype)
    wo[:, 0:D1, :] = a["L1_attn_W_o"].T.reshape(H, D1, C)
    arrays = dict(
        x=a["L0_attn_x"].reshape(B * T, C),
        w_small=halves(np.concatenate([L("w_cq"), L("w_ckv"), L("w_krope"), L("w_gate")[:, [1, 0, 2]]], 1)),
        w_imp=halves(L("w_imp"))[:, :, 0],
        w_q=q, w_nv=nv,
        w_kw=paired(L("w_wink"), L("w_winv")), w_sel=paired(L("w_selk"), L("w_selv")),
        w_proj=halves(L("w_proj")), g_q=L("g_qnorm"), g_kv=L("g_kvnorm"),
        w_fc=halves(a["L0_ffn_W_fc"].T), w_ffp=halves(a["L0_ffn_W_proj"].T),
        w_qkv=halves(wqkv), w_o=halves(wo.reshape(H * DP, C)), w_sign=halves(a["L1_ffn_weight"].T),
        **constants(),
    )
    nc = bacc.Bacc("TRN2", target_bir_lowering=False, num_devices=1)
    feed, args = {}, []
    for name in WEIGHT_NAMES + CONST_NAMES:
        arr = np.ascontiguousarray(arrays[name])
        feed[name + "_dram"] = arr
        args.append(nc.dram_tensor(name + "_dram", arr.shape, mybir.dt.from_np(arr.dtype), kind="ExternalInput").ap())
    args.append(nc.dram_tensor("out_dram", (B * T, C), F32, kind="ExternalOutput").ap())
    build_program(nc, *args)
    result = run_bass_kernel_spmd(nc, [feed], core_ids=[0])
    return result.results[0]["out_dram"].reshape(B, T, C)
```

```python
from contextlib import ExitStack

import numpy as np

import concourse.bass as bass
from concourse import mybir

F32 = mybir.dt.float32
BF16 = mybir.dt.bfloat16
F32R = mybir.dt.float32r
ALU = mybir.AluOpType
ACT = mybir.ActivationFunctionType
AX = mybir.AxisListType

P = 128
B, T, C = 8, 512, 256
NT = T // P
NC = C // P
H = 16
HG = 4
NG = H // HG
NPAIR = H // 2
QL, KVL = 96, 32
NOPE, ROPE, VD = 32, 64, 32
D0 = NOPE + ROPE
KEEP = 64
FF = 1024
NF = FF // P
SM_W = QL + KVL + ROPE + 3
D1 = 16
DP = 32
NEG = -1.0e30
Q_SCALE = float(D0) ** -0.5
LN_EPS, RMS_EPS = 1e-5, 1e-6

NWORK, NOUT = 5, 3
NP = 8
A1, A3, A2 = 0, 1, 2



def max_units0():
    out = []
    for h in range(2):
        out += [
            dict(mm=[(h, "k1", 0, 448, 0, 3)], mask=[], segs=[(0, 64, A2, h, 3), (64, 448, A1, h, 3)]),
            dict(mm=[(h, "k1", 448, 128, 0, 3), (h, "kw", 0, 384, 128, 2)], mask=[0, 384],
                 segs=[(0, 128, None, h, 3), (128, 512, A3, h, 2)]),
            dict(mm=[(h, "kw", 0, 512, 0, 3)], mask=[384], segs=[(0, 512, A3, h, 3)]),
            dict(mm=[(h, "k1", 0, 448, 0, 2)], mask=[320], segs=[(0, 64, A2, h, 2), (64, 448, A1, h, 2)]),
            dict(mm=[(h, "k1", 0, 320, 0, 1), (h, "kw", 0, 128, 320, 0)], mask=[192, 320],
                 segs=[(0, 64, A2, h, 1), (64, 320, A1, h, 1), (320, 448, A3, h, 0)]),
            dict(mm=[(h, "k1", 0, 192, 0, 0), (h, "kw", 0, 256, 192, 1)], mask=[64, 320],
                 segs=[(0, 64, A2, h, 0), (64, 192, A1, h, 0), (192, 448, A3, h, 1)]),
        ]
    return out


def max_units1():
    out = []
    for h in range(2):
        out += [dict(mm=[(h, "k", 0, 512, 0, 3)], mask=[384], segs=[(0, 512, 0, h, 3)]),
                dict(mm=[(h, "k", 0, 384, 0, 2), (h, "k", 0, 128, 384, 0)], mask=[256, 384],
                     segs=[(0, 384, 0, h, 2), (384, 512, 0, h, 0)])]
    out.append(dict(mm=[(h, "k", 0, 256, 256 * h, 1) for h in range(2)], mask=[128, 384],
                    segs=[(256 * h, 256 * h + 256, 0, h, 1) for h in range(2)]))
    return out


def units0():
    out = []
    for what in ([(A1, 0, 0)], [(A1, 1, 0), (A1, 3, 384)], [(A3, 0, 0)], [(A3, 1, 0), (A3, 3, 384)],
                 [(A1, 2, 0), (A3, 2, 256)], [(A2, 0, 0)]):
        for h in range(2):
            out.append([(a, h, j, col) for a, j, col in what])
    return out


def units1():
    out = []
    for what in ([(0, 0)], [(1, 0), (3, 384)]):
        for h in range(2):
            out.append([(0, h, j, col) for j, col in what])
    out.append([(0, 0, 2, 0), (0, 1, 2, 256)])
    return out


MAX_UNITS = [max_units0(), max_units1()]
UNITS = [units0(), units1()]
NU = [len(u) for u in UNITS]
PV = [[(2 * k, 2 * k + 1) for k in range(6)], [(0, 1), (2, 3), (4,)]]
NPV = [len(k) for k in PV]
UNIT0 = [0, NPAIR * NU[0]]
PV0 = [0, NPAIR * NPV[0]]
COMPLETE = [{4: [A1, A3], 5: [A2]}, {2: [0]}]

PIECES = [("qk", 0), ("qk", 1), ("nv", 0), ("qk", 2), ("qk", 3), ("nv", 1), ("sel", 0)]
NPIECE = len(PIECES)
ROPED = [m for m in range(NPIECE) if PIECES[m][0] != "nv"]


def nth(p):
    return max(p - 1, 0)


def piece_before(p, m, n, among=tuple(range(NPIECE))):
    k = among.index(m) - n
    if k >= 0:
        return p, among[k]
    return (p - 1, among[k + len(among)]) if p >= 2 else None


AFTER = [dict(pv=2.67, tr=1.82, group=1.98, piece=-2.58, gap=0.66, piece_tr=2.36, max=4.9, max_gap=0.31,
              mt=2.12, rows=-5.38, tail=[(-6.6, -6.5), (-4.0, -5.2), (-2.4, -3.9), (-1.5, -2.3)]),
         dict(pv=3.09, tr=1.9, group=2.19, max=-0.3, max_gap=1.03, mt=2.68, pro=-0.08,
              pro_gap=[2.57, 3.09, 1.5, 3.0, 3.0, 0.0], piece=32.74, gap=1.07, piece_tr=1.41)]


NPRO, PRO_PE = 12, [1, 2, 3, 4, 9, 10]


def attention_steps(layer):
    n, at, o = NU[layer], [], AFTER[layer]
    for p in range(NPAIR):
        t0 = n * p
        for i in range(n):
            at.append((t0 + i, ("unit", p, i)))
        for k, units in enumerate(PV[layer]):
            t = t0 + units[-1] + o["pv"]
            at.append((t, ("pv", p, k)))
            for a in COMPLETE[layer].get(k, []):
                if layer == 0:
                    what, group = p, a == A2 and p % 2
                elif p % 2:
                    what, group = p // 2, True
                else:
                    continue
                t1 = t + 0.3 + o["tr"]
                at += [(t + 0.3, ("out", what, a)), (t1, ("out_tr", what, a)), (t1 + 0.1, ("norm", what, a))]
                if group and layer == 0 and p == NPAIR - 1:
                    at.append((t1 + o["group"] - 0.01, ("projection",)))
                if group:
                    at += [(t1 + o["group"], ("group", p // 2)), (t1 + o["group"] + 0.1, ("group_out", p // 2))]
        b = n * (p - (1 if layer == 0 else 2))
        if layer == 0:
            for m in range(NPIECE if p else 0):
                at.append((b + o["gap"] * m + o["piece"], ("piece", p, m)))
                t = max(b + o["gap"] * m + o["piece"] + o["piece_tr"], n * (p - 1) - 0.9 + 0.01 * m)
                at.append((t, ("piece_tr", p, m)))
        for i in range(len(MAX_UNITS[layer])):
            at.append((b + o["max"] + o["max_gap"] * i, ("max", p, i)))
        t = b + o["max"] + o["max_gap"] * (len(MAX_UNITS[layer]) - 1) + o["mt"]
        at += [(t, ("mt", p)), (t + 0.4, ("mt_out", p))]
    if layer == 0:
        for j, (t_pe, t) in enumerate(o["tail"]):
            at += [(t_pe, ("tail_pe", j)), (t, ("tail", j))]
        at += [(o["rows"], ("rows", 0)), (o["rows"] + n, ("rows", 1))]
    if layer == 1:
        for m in range(NPIECE):
            t = max(o["piece"] + o["gap"] * m + o["piece_tr"], n * (NPAIR - 1) - 0.9 + 0.01 * m)
            at += [(o["piece"] + o["gap"] * m, ("piece", NPAIR, m)), (t, ("piece_tr", NPAIR, m))]
        t = o["pro"]
        for j in range(6, NPRO):
            at.append((t + 0.15, ("pro", j)))
            t += o["pro_gap"][j - 6]
            if j in PRO_PE:
                at.append((t, ("pro_pe", PRO_PE.index(j))))
    return [s for _, s in sorted(at, key=lambda x: x[0])]


STEPS = [attention_steps(0), attention_steps(1)]


QKV_STEPS = [("half", 0), ("qk", 0), ("qk", 1), ("v", 0), ("heads", 0), ("half", 1), ("qk", 2), ("qk", 3), ("v", 1),
             ("heads", 1), ("heads", 2), ("heads", 3)]


FFN_STEPS = [("fc", 0, 0), ("fc", 0, 1), ("pro_pe", 0), ("pro", 2), ("fc", 0, 2), ("fc", 0, 3), ("y", 0),
             ("pro_pe", 1), ("pro", 3), ("fc", 1, 0), ("fc", 1, 1), ("fc", 1, 2), ("fc", 1, 3), ("pro_pe", 2),
             ("y", 1), ("pro_pe", 3), ("pro", 5)]


class Banks:

    def __init__(self, n):
        self.n, self.uses, self.units, self.of = n, 0, 0, {}
        self.full, self.read, self.exp = [0] * n, [0] * n, [0] * n

    def use(self, name, readers=1):
        k = self.uses % self.n
        self.uses += 1
        free_at, exp_at = self.read[k], self.exp[k]
        self.full[k] += 1
        if readers:
            self.read[k] += readers
            self.exp[k] = 0
        else:
            self.units += 1
            self.exp[k] = self.units
        self.of[name] = (k, free_at, self.full[k], self.read[k], exp_at)


def plan_banks():
    work, first, last = Banks(NWORK), Banks(NWORK), Banks(NWORK)

    def piece(banks, s):
        banks.use(s, 2 if s[0] == "piece_tr" or PIECES[s[2]][0] == "nv" else 4)

    def tail(banks, tag, j):
        for name in (["o0", "o1"], ["hT0", "hT1"], ["sign0", "sign1"], [])[j]:
            banks.use((tag, name))

    def prologue(banks, tag, j):
        for name in (["hT0", "hT1"], ["small0", "small1", "imp"], ["score_cols", "gate"], ["nqT", "ckvT"],
                     ["pos"], ["selT"])[j]:
            banks.use((tag, name))

    def attention(layer):
        for s in STEPS[layer]:
            if s[0] == "mt" and layer == 0:
                for h in range(2):
                    work.use((0,) + s + (h,))
            elif s[0] in ("unit", "max", "mt", "out_tr", "group"):
                work.use((layer,) + s, {"unit": 0, "mt": 2}.get(s[0], 1))
            elif s[0] in ("piece", "piece_tr"):
                piece(work, s)
            elif s[0] == "projection":
                for i in range(2):
                    work.use(("proj", i))
            elif s[0] == "pro_pe":
                prologue(work, "next", s[1])
            elif s[0] == "tail_pe":
                tail(work, "before", s[1])

    for j in range(6):
        prologue(first, "first", j)
    for m in range(NPIECE):
        piece(first, ("piece", 0, m))
        piece(first, ("piece_tr", 0, m))
    for j in range(4):
        tail(last, "last", j)
    work.of.update(first.of)
    work.of.update(last.of)
    attention(0)
    for i in range(2):
        work.use(("hT", 1, i))
    for s in FFN_STEPS:
        if s[0] == "pro_pe":
            prologue(work, "next", s[1])
        elif s[0] != "pro":
            work.use(s)
    for what, n in QKV_STEPS:
        if what == "half":
            work.use(("hT", 2, n))
        elif what == "v":
            work.use(("v", n))
        elif what == "qk":
            work.use(("qk1", n), 2)
        else:
            for k in range(4):
                work.use(("heads", n, k), 2 if k < 2 else 1)
    attention(1)
    return work


def constants():
    pos = np.arange(T, dtype=np.float32)

    def tab(dim):
        f = (1.0 / np.float32(10000.0) ** (np.arange(0, dim, 2, dtype=np.float32) / np.float32(dim))).astype(np.float32)
        a = np.outer(pos, f).astype(np.float32)
        tile = lambda m: np.ascontiguousarray(m.reshape(NT, P, -1).transpose(1, 0, 2))
        c, s = np.cos(a).astype(np.float32), np.sin(a).astype(np.float32)
        return tile(c), tile(np.concatenate([-s, s], 1))

    c0, s0 = tab(ROPE)
    c1, s1 = tab(D1)
    p = np.arange(P)
    f = np.float32
    return dict(
        cos0=c0, sin0=s0, cos1=c1, sin1=s1,
        ident=np.eye(P, dtype=f),
        causal=np.where(p[None, :] > p[:, None], f(NEG), f(0.0)).astype(f),
        causal_t=np.where(p[None, :] < p[:, None], f(NEG), f(0.0)).astype(f),
        before=(p[:, None] < p[None, :]).astype(f),
        earlier=((np.arange(7 * P)[None, :] - 3 * P) < p[:, None]).astype(f),
        ranks=np.broadcast_to(np.arange(KEEP, dtype=f), (P, KEEP)).copy(),
    )


CONST_NAMES = ["cos0", "sin0", "cos1", "sin1", "ident", "causal", "causal_t", "before", "earlier", "ranks"]
WEIGHT_NAMES = ["x", "w_small", "w_imp", "w_q", "w_nv", "w_kw", "w_sel", "w_proj", "g_q", "g_kv",
                "w_fc", "w_ffp", "w_qkv", "w_o", "w_sign"]


def build_program(nc, x, w_small, w_imp, w_q, w_nv, w_kw, w_sel, w_proj, g_q, g_kv,
                  w_fc, w_ffp, w_qkv, w_o, w_sign,
                  cos0, sin0, cos1, sin1, ident, causal, causal_t, before, earlier, ranks, out):
    work = plan_banks()
    ctx = ExitStack()
    with ctx:
        def sb(name, shape, dt=F32):
            return ctx.enter_context(nc.sbuf_tensor(name, shape, dt))

        WS = sb("WS", [P, NC, SM_W])
        WIMP = sb("WIMP", [P, NC])
        WI = sb("WI", [P, NC, P])
        WQ = sb("WQ", [P, H * D0])
        WKW = sb("WKW", [P, 2, NC, 256])
        WSEL = sb("WSEL", [P, 2, NC, 256])
        WP = sb("WP", [P, NG, C])
        GQ = sb("GQ", [P, QL])
        GK = sb("GK", [P, KVL])
        WFC = sb("WFC", [P, NC, FF])
        WFP = sb("WFP", [P, NF, C])
        WQKV = sb("WQKV", [P, NC, 3 * C])
        WO = sb("WO", [P, NG, C])
        WSG = sb("WSG", [P, NC, C])
        COS0, SIN0 = sb("COS0", [P, NT, 32]), sb("SIN0", [P, NT, 64])
        COS1, SIN1 = sb("COS1", [P, NT, 8]), sb("SIN1", [P, NT, 16])
        ID = sb("ID", [P, P])
        IDB = sb("IDB", [P, P], BF16)
        CAUSB = sb("CAUSB", [P, P], BF16)
        CAUTB = sb("CAUTB", [P, P], BF16)
        ONES = sb("ONES", [P, 32])
        BEFB = sb("BEFB", [P, P], BF16)
        ONEB = sb("ONEB", [P, P], BF16)
        MEANW = sb("MEANW", [P, P])
        EARLY = sb("EARLY", [P, 7 * P])
        RANKS = sb("RANKS", [P, KEEP])
        MHALF = sb("MHALF", [P, 8])
        HEAD = sb("HEAD", [P, 2])
        X0, X1, X2 = sb("X0", [P, NT, C]), sb("X1", [P, NT, C]), sb("X2", [P, NT, C])
        HN = sb("HN", [P, NT, C])
        HN0 = sb("HN0", [P, NT, C])
        HT = sb("HT", [P, NC, T])
        HT0 = sb("HT0", [P, NC, T])
        NQT = sb("NQT", [P, T])
        KR = sb("KR", [P, NT, ROPE])
        SMALL = sb("SMALL", [P, 2048])
        SM = SMALL[:, 0:4 * 196].rearrange("p (t c) -> p t c", t=NT)
        NCK = SMALL[:, 784:1296].rearrange("p (t c) -> p t c", t=NT)
        ROW = sb("ROW", [P, T])[:, :]
        SELT = sb("SELT", [P, NC, KEEP])
        BIG = sb("BIG", [P, 12800], F32R)
        QW, K1 = [], []
        for o in (0, 6400):
            QW.append([BIG[:, o + 2048 * n:o + 2048 * n + 2048].rearrange("p (s k) -> p s k", s=4) for n in range(2)])
            K1.append([BIG[:, o + 4096 + 1152 * n:o + 4096 + 1152 * n + 1152].rearrange("p (h k) -> p h k", h=2)
                       for n in range(2)])
        QZ = BIG[:, 0:8192].rearrange("p (g h k) -> p g h k", g=NPAIR, h=2)
        KB = BIG[:, 8192:12288].rearrange("p (g k) -> p g k", g=NPAIR)
        VV = sb("VV", [P, 3, NT, 2, 64])
        VS = sb("VS", [KEEP, 3, 64])
        TOK = sb("TOK", [P, 4, HG, D0])
        AB = sb("AB", [P, 2, 512])
        OH = AB[:, 1, 0:NT * KEEP].rearrange("p (t c) -> p t c", t=NT)
        PR = sb("PR", [P, NP, 512])
        STACKS = [[z[:, o:o + 1024].rearrange("p (h s d) -> p h s d", h=H, s=4) for o in (0, 1024)]
                  for z in (SMALL, PR[:, 4:8, :].rearrange("p n k -> p (n k)"))]
        OT = sb("OT", [P, NG, T])
        NRM = sb("NRM", [P, 4096])
        OE = [NRM[:, 0:1536].rearrange("p (a k) -> p a k", a=3), NRM[:, 2048:3072].rearrange("p (a k) -> p a k", a=2)]
        OROWS = [NRM[:, o:o + 1024].rearrange("p (n t c) -> p n t c", n=2, t=NT) for o in (2304, 3072)]
        GATED = NRM[:, 1536:2304].rearrange("p (a t h d) -> p a t h d", a=3, t=NT, h=2)
        VP = NRM[:, 0:2048].rearrange("p (t h d) -> p t h d", t=NT, d=DP)
        ROPED1 = PR[:, 0:2, :].rearrange("p n (h d) -> p n h d", d=D1)
        STATE = NRM[:, :].rearrange("p (i n a) -> p i n a", i=2, n=4)
        R2 = PR
        NMX = sb("NMX", [P, 2, 24])
        NPART = sb("NPART", [P, 2])
        RSUM = sb("RSUM", [P, 3, NT, 4])
        BN = sb("BN", [P, NT, 6]); MV = sb("MV", [P, NT, 2])
        VAR, YP, NA = sb("VAR", [P, 8]), sb("YP", [P, 8]), sb("NA", [P, 8])
        RSTD = sb("RSTD", [P, 8])
        SC, CG, CE = sb("SC", [P, NT]), sb("CG", [P, NT]), sb("CE", [P, NT])
        MF, MB, POS = sb("MF", [P, NT]), sb("MB", [P, NT], BF16), sb("POS", [P, NT])
        GS, GE, GG = sb("GS", [P, 3]), sb("GE", [P, 3]), sb("GG", [P, 3])
        GM, GD = sb("GM", [P, 1]), sb("GD", [P, 3])

        WB = [ctx.enter_context(nc.psum_tensor(f"work{k}", [P, 512], F32)) for k in range(NWORK)]
        OB = [ctx.enter_context(nc.psum_tensor(f"outs{k}", [P, 512], F32)) for k in range(NOUT)]

        def sem(name):
            return ctx.enter_context(nc.semaphore(name))

        first_cleared = sem("work_full0")
        work_full = [first_cleared] + [sem(f"work_full{k}") for k in range(1, NWORK)]
        work_read = [sem(f"work_read{k}") for k in range(NWORK)]
        pv_done = sem("pv_done")
        var_ready = sem("var_ready")
        pow_done = sem("pow_done")
        h_ready = sem("h_ready")
        latents_ready = sem("latents_ready")
        kr_products = sem("kr_products")
        mask_ready = sem("mask_ready")
        onehot_ready = sem("onehot_ready")
        gate_in = sem("gate_in")
        gate_exp = sem("gate_exp")
        kr_ready = sem("kr_ready")
        tok_ready = sem("tok_ready")
        max_ready = sem("max_ready")
        exp_ready = sem("exp_ready")
        evacuated = sem("evacuated")
        summed = sem("summed")
        stacked = sem("stacked")
        stacked_hi = sem("stacked_hi")
        roped1 = sem("roped1")
        squared = sem("squared")
        values_set = sem("values_set")
        pool_step = sem("pool_step")
        dve_step = sem("dve_step")
        kw_loaded = [sem("kw_loaded0"), sem("kw_loaded1")]
        sel_loaded = [sem("sel_loaded0"), sem("sel_loaded1")]
        finished = sem("finished")
        cleared = range(first_cleared.num, finished.num + 1)
        next_sequence = sem("next_sequence")
        x_loaded = sem("x_loaded")
        x_stored = sem("x_stored")
        early_loaded, late_loaded = sem("early_loaded"), sem("late_loaded")
        set_up = sem("set_up")

        block = ctx.enter_context(nc.Block())

        def full(e, use, bank):
            ring, sems, banks = bank
            k, _, f, _, _ = ring.of[use]
            e.wait_ge(sems[k], f)
            return banks[k]

        WORK = (work, work_full, WB)

        def maxima_uses(layer, p):
            return [(0, "mt", p, 0), (0, "mt", p, 1)] if layer == 0 else [(1, "mt", p)]

        def end_pass(e, n):
            e.drain().then_inc(finished, 1)
            e.wait_ge(next_sequence, n)

        LN_AT = {"first": 0, 3: 0, 1: 1, "next": 2, 2: 3}
        POW_AT = {"first": (0, 1), 3: (0, 1), 1: (2, 3), "next": (4, 6), 2: (5, 7)}

        def was_read(e, ring, sems, use):
            k, _, _, r, _ = ring.of[use]
            e.wait_ge(sems[k], r)

        def ab(i, rows, heads, half):
            w = heads * 2 * half
            if w <= 256:
                a, b = AB[0:rows, i % 2, 0:w], AB[0:rows, i % 2, 256:256 + w]
            else:
                a, b = AB[0:rows, 0, 0:w], AB[0:rows, 1, 0:w]
            return [z.rearrange("p (h j d) -> p h j d", j=2, d=half) for z in (a, b)]

        def transposed_heads(p, m, ps):
            what, t = PIECES[m]
            par = p % 2
            if what == "qk":
                return (ps[0:D0, :].rearrange("p (s k) -> p s k", s=4),
                        [QW[par][n][0:D0, :, t * P:(t + 1) * P] for n in range(2)])
            if what == "nv":
                return (ps[0:D0, :].rearrange("p (t h k) -> p t h k", t=2, h=2),
                        [K1[par][n][0:D0, :, KEEP + 2 * t * P:KEEP + 2 * (t + 1) * P]
                         .rearrange("p h (t k) -> p t h k", t=2) for n in range(2)])
            return (ps[0:D0, 0:2 * KEEP].rearrange("p (h k) -> p h k", h=2),
                    [K1[par][n][0:D0, :, 0:KEEP] for n in range(2)])

        def products_of(j):
            layer = int(j >= UNIT0[1])
            p, i = (j - UNIT0[layer]) // NU[layer], (j - UNIT0[layer]) % NU[layer]
            k = [i in units for units in PV[layer]].index(True)
            return PV0[layer] + p * NPV[layer] + k + 1

        early_loads = [(WS[:, :, :], w_small), (WIMP[:, :], w_imp), (ID[:, :], ident),
                       (X2[:, 0, 0:P], causal), (X2[:, 1, 0:P], before), (X2[:, 2, 0:P], causal_t),
                       (GQ[:, :], g_q.partition_broadcast(P)), (GK[:, :], g_kv.partition_broadcast(P)),
                       (COS0[:, :, :], cos0), (SIN0[:, :, :], sin0), (EARLY[:, :], earlier), (RANKS[:, :], ranks)]
        late_loads = [(WQ[0:QL, :], w_q), (WQ[QL:P, 0:1024], w_nv), (COS1[:, :, :], cos1), (SIN1[:, :, :], sin1),
                      (WP[:, :, :], w_proj), (WFC[:, :, :], w_fc), (WFP[:, :, :], w_ffp), (WQKV[:, :, :], w_qkv),
                      (WO[:, :, :], w_o), (WSG[:, :, :], w_sign)]
        EARLY_LOADED, LATE_LOADED = 16 * len(early_loads), 16 * len(late_loads)
        SET_UP = 14
        x_rows = x.rearrange("(n p) c -> p n c", p=P)
        out_rows = out.rearrange("(n p) c -> p n c", p=P)

        @block.sync
        def _(sp):
            sp.dma_start(X0[:, :, :], x_rows[:, 0:NT, :]).then_inc(x_loaded, 16)
            for dst, src in early_loads:
                sp.dma_start(dst, src).then_inc(early_loaded, 16)

            def next_pass():
                sp.wait_ge(finished, 4)
                sp.sem_clear(cleared)
                sp.sem_inc(next_sequence, 1)

            def store(tag, row_tile):
                for i in range(2):
                    was_read(sp, work, work_read, (tag, f"sign{i}"))
                sp.dma_start(out_rows[:, bass.ds(row_tile, NT), :], X2[:, :, :]).then_inc(x_stored, 16)

            def load_weights(p):
                sp.dma_start(WKW[:, p % 2, :, :], w_kw[p % NPAIR]).then_inc(kw_loaded[p % 2], 16)
                sp.dma_start(WSEL[:, p % 2, :, :], w_sel[p % NPAIR]).then_inc(sel_loaded[p % 2], 16)

            load_weights(0)
            for dst, src in late_loads:
                sp.dma_start(dst, src).then_inc(late_loaded, 16)
            next_pass()
            with sp.Fori(0, B) as seq:
                for p in (1, 2):
                    load_weights(p)
                for s in STEPS[0]:
                    if s[0] == "piece" and s[2] == NPIECE - 1 and s[1] + 2 <= NPAIR:
                        full(sp, s, WORK)
                        load_weights(s[1] + 2)
                    elif s == ("tail", 3):
                        store("before", ((seq + (B - 1)) % B) * NT)
                for i in range(2):
                    was_read(sp, work, work_read, ("proj", i))
                sp.dma_start(X0[:, :, :], x_rows[:, bass.ds(((seq + 1) % B) * NT, NT), :]).then_inc(x_loaded, 16)
                next_pass()
            store("last", (B - 1) * NT)
            sp.wait_ge(x_stored, 16 * (B + 1))
            sp.wait_ge(x_loaded, 16 * (B + 1))

        @block.tensor
        def _(pe):
            mm = nc.tensor.matmul

            def take(use, bank):
                ring, full_sems, banks, read_sems = bank
                k, free_at, _, _, exp_at = ring.of[use]
                if exp_at > 0:
                    pe.wait_ge(exp_ready, exp_at)
                elif free_at > 0:
                    pe.wait_ge(read_sems[k], free_at)
                return banks[k], full_sems[k]

            W = (work, work_full, WB, work_read)

            def transpose_half(i, half, use=None):
                ps, done = take(use or ("hT", i, half), W)
                for t in (2 * half, 2 * half + 1):
                    pe.wait_ge(h_ready, NT * LN_AT[i] + t + 1)
                    for c in range(NC):
                        last = nc.tensor.transpose(ps[:, (2 * c + t % 2) * P:(2 * c + t % 2 + 1) * P],
                                                   HN[:, t, c * P:(c + 1) * P], ID[:, :])
                last.then_inc(done, 1)

            def out_projection(use, i, wt):
                ps, done = take(use, W)
                for tt in range(2):
                    t = 2 * i + tt
                    for g in range(NG):
                        last = mm(ps[:, tt * C:(tt + 1) * C], OT[:, g, t * P:(t + 1) * P], wt[:, g, :],
                                  start=(g == 0), stop=(g == NG - 1))
                last.then_inc(done, 1)

            def tail(tag, j):
                if j == 0:
                    for i in range(2):
                        out_projection((tag, f"o{i}"), i, WO)
                elif j == 1:
                    for i in range(2):
                        transpose_half(3, i, (tag, f"hT{i}"))
                elif j == 2:
                    for i in range(2):
                        was_read(pe, work, work_read, (tag, f"hT{i}"))
                        ps, done = take((tag, f"sign{i}"), W)
                        for tt in range(2):
                            t = 2 * i + tt
                            for c in range(NC):
                                last = mm(ps[:, tt * C:(tt + 1) * C], HT[:, c, t * P:(t + 1) * P], WSG[:, c, :],
                                          start=(c == 0), stop=(c == NC - 1))
                        last.then_inc(done, 1)

            def prologue(tag, j):
                def read(name):
                    was_read(pe, work, work_read, (tag, name))

                if j == 0:
                    for c in range(NC):
                        ps, done = take((tag, f"hT{c}"), W)
                        for t in range(NT):
                            if c == 0:
                                pe.wait_ge(h_ready, NT * LN_AT[tag] + t + 1)
                            last = nc.tensor.transpose(ps[:, t * P:(t + 1) * P], HN0[:, t, c * P:(c + 1) * P], ID[:, :])
                        last.then_inc(done, 1)
                elif j == 1:
                    for c in range(NC):
                        read(f"hT{c}")
                    for i in range(2):
                        ps, done = take((tag, f"small{i}"), W)
                        for tt in range(2):
                            t = 2 * i + tt
                            for c in range(NC):
                                last = mm(ps[:, tt * C:tt * C + SM_W], HT0[:, c, t * P:(t + 1) * P], WS[:, c, :],
                                          start=(c == 0), stop=(c == NC - 1))
                        last.then_inc(done, 1)
                    ps, done = take((tag, "imp"), W)
                    for c in range(NC):
                        last = mm(ps[:, :], WI[:, c, :], HT0[:, c, :], start=(c == 0), stop=(c == NC - 1))
                    last.then_inc(done, 1)
                elif j == 2:
                    ps, done = take((tag, "score_cols"), W)
                    read("imp")
                    for t in range(NT):
                        last = nc.tensor.transpose(ps[:, t * P:(t + 1) * P], ROW[:, t * P:(t + 1) * P], ID[:, :])
                    last.then_inc(done, 1)
                    ps, done = take((tag, "gate"), W)
                    for i in range(2):
                        read(f"small{i}")
                    for t in range(NT):
                        last = mm(ps[:, 0:3], MEANW[:, :], SM[:, t, SM_W - 3:SM_W], start=(t == 0), stop=(t == NT - 1))
                    last.then_inc(done, 1)
                elif j == 3:
                    pe.wait_ge(latents_ready, 2 * NT)
                    for name, rows, c0 in (("nqT", QL, 0), ("ckvT", KVL, QL)):
                        ps, done = take((tag, name), W)
                        for t in range(NT):
                            last = nc.tensor.transpose(ps[0:rows, t * P:(t + 1) * P], NCK[:, t, c0:c0 + rows], ID[:, :])
                        last.then_inc(done, 1)
                elif j == 4:
                    ps, done = take((tag, "pos"), W)
                    pe.wait_ge(mask_ready, 1)
                    for t in range(NT):
                        for s in range(t + 1):
                            last = mm(ps[:, t:t + 1], (BEFB if s == t else ONEB)[:, :], MB[:, s:s + 1],
                                      start=(s == 0), stop=(s == t))
                    last.then_inc(done, 1)
                else:
                    ps, done = take((tag, "selT"), W)
                    pe.wait_ge(onehot_ready, 1)
                    for c in range(NC):
                        for t in range(NT):
                            last = mm(ps[:, c * KEEP:(c + 1) * KEEP], HN0[:, t, c * P:(c + 1) * P], OH[:, t, :],
                                      start=(t == 0), stop=(t == NT - 1))
                    last.then_inc(done, 1)

            def piece(p, m):
                what, t = PIECES[m]
                w = p % NPAIR
                if w == 0:
                    for name in {0: ("nqT", "ckvT"), NPIECE - 1: ("selT",)}.get(m, ()):
                        was_read(pe, work, work_read, ("next" if p else "first", name))
                ps, done = take(("piece", p, m), W)
                if what == "qk":
                    mm(ps[:, 0:192], NQT[0:QL, t * P:(t + 1) * P], WQ[0:QL, w * 192:(w + 1) * 192], start=True, stop=True)
                    if t == 0:
                        pe.wait_ge(kw_loaded[p % 2], 16 * (nth(p) // 2 + 1))
                    for c in range(NC):
                        last = mm(ps[:, 192:448], HT0[:, c, t * P:(t + 1) * P], WKW[:, p % 2, c, :],
                                  start=(c == 0), stop=(c == NC - 1))
                elif what == "nv":
                    for tt in range(2):
                        t2 = 2 * t + tt
                        last = mm(ps[:, tt * P:(tt + 1) * P], NQT[QL:P, t2 * P:(t2 + 1) * P],
                                  WQ[QL:P, w * P:(w + 1) * P], start=True, stop=True)
                else:
                    pe.wait_ge(sel_loaded[p % 2], 16 * (nth(p) // 2 + 1))
                    for c in range(NC):
                        last = mm(ps[0:KEEP, 0:256], SELT[:, c, :], WSEL[:, p % 2, c, :], start=(c == 0), stop=(c == NC - 1))
                last.then_inc(done, 1)

            def piece_transposes(p, m):
                what, t = PIECES[m]
                rows, heads = (KEEP, 2) if what == "sel" else (P, 4)
                was_read(pe, work, work_read, ("piece", p, m))
                pe.wait_ge(tok_ready, nth(p) * NPIECE + m + 1)
                ps, done = take(("piece_tr", p, m), W)
                for h in range(heads):
                    last = nc.tensor.transpose(ps[0:D0, h * rows:(h + 1) * rows],
                                               TOK[0:rows, (nth(p) * NPIECE + m) % 4, h, :], ID[0:rows, 0:rows])
                last.then_inc(done, 1)

            def add_masks(ps, cols, mask):
                blocks = ps[:, cols[0]:cols[-1] + P].rearrange("p (n k) -> p n k", k=P)
                blocks = blocks[:, 0::max(blocks.shape[1] - 1, 1), :]
                return mm(blocks, IDB[:, :], mask[:, :].unsqueeze(1).broadcast_to([P, len(cols), P]),
                          start=False, stop=True)

            def max_scores(layer, p, i):
                u = MAX_UNITS[layer][i]
                if layer == 0 and p and i == 0:
                    for m in range(NPIECE):
                        was_read(pe, work, work_read, ("piece_tr", p, m))
                ps, done = take((layer, "max", p, i), W)
                for i_mm, (h, src, k0, n, col, qt) in enumerate(u["mm"]):
                    if layer == 0:
                        q = QW[p % 2][0][0:D0, h, qt * P:(qt + 1) * P]
                        k = K1[p % 2][0][0:D0, h, k0:k0 + n] if src == "k1" else QW[p % 2][0][0:D0, 2 + h, k0:k0 + n]
                    else:
                        q, k = QZ[:, p, h, qt * P:(qt + 1) * P], KB[:, p, k0:k0 + n]
                    last = mm(ps[:, col:col + n], q, k, start=(i_mm == 0),
                              stop=(not u["mask"] and i_mm == len(u["mm"]) - 1))
                if u["mask"]:
                    last = add_masks(ps, u["mask"], CAUSB)
                last.then_inc(done, 1)

            def transpose_maxima(layer, p):
                if layer == 0:
                    pe.wait_ge(max_ready, p + 1)
                    for h in range(2):
                        ps, done = take((0, "mt", p, h), W)
                        for t in range(NT):
                            c = h * NT + t
                            last = nc.tensor.transpose(ps[0:3, t * P:(t + 1) * P], NMX[:, p % 2, c:24:8], ID[:, :])
                        last.then_inc(done, 1)
                else:
                    was_read(pe, work, work_read, (1, "max", p, len(MAX_UNITS[1]) - 1))
                    ps, done = take((1, "mt", p), W)
                    for t in range(NT):
                        last = nc.tensor.transpose(ps[0:2, t * P:(t + 1) * P], NMX[:, p % 2, t:8:NT], ID[:, :])
                    last.then_inc(done, 1)

            def unit(layer, p, i):
                if i == 0:
                    for use in maxima_uses(layer, p):
                        was_read(pe, work, work_read, use)
                ps, done = take((layer, "unit", p, i), W)
                diagonal = []
                for (a, h, j, col) in UNITS[layer][i]:
                    q0, keys = j * P, (KEEP if layer == 0 and a == A2 else P)
                    out = ps[0:keys, col:col + T - q0]
                    causal_block = not (layer == 0 and a == A2)
                    if causal_block:
                        diagonal.append(col)
                    if layer == 0:
                        q = [QW[p % 2][n][:, h, q0:T] for n in range(2)]
                        if a == A3:
                            k = [QW[p % 2][n][:, 2 + h, j * P:(j + 1) * P] for n in range(2)]
                        else:
                            k0 = 0 if a == A2 else KEEP + j * P
                            k = [K1[p % 2][n][:, h, k0:k0 + keys] for n in range(2)]
                        mm(out, k[0][0:D0 + 3], q[0][0:D0 + 3], start=(col == 0), stop=False)
                        mm(out, k[0][0:D0], q[1][0:D0], start=False, stop=False)
                        last = mm(out, k[1][0:D0], q[0][0:D0], start=False, stop=not causal_block)
                    else:
                        last = mm(out, KB[:, p, j * P:(j + 1) * P], QZ[:, p, h, q0:T], start=(col == 0), stop=False)
                if diagonal:
                    last = add_masks(ps, diagonal, CAUTB)
                last.then_inc(done, 1)

            def values(layer, p, k):
                units = PV[layer][k]
                pe.wait_ge(exp_ready, UNIT0[layer] + p * NU[layer] + units[-1] + 1)
                if layer == 0 and p and k in (0, 2, 5):
                    pe.wait_ge(evacuated, 3 * (p - 1) + {0: A1, 2: A3, 5: A2}[k] + 1)
                elif layer and k == 0:
                    pe.wait_ge(evacuated, 3 * NPAIR + max(p // 2 - 2, 0))
                parts = [(i, part) for i in units for part in UNITS[layer][i]]
                parts.sort(key=lambda x: (x[1][0], x[1][2], x[1][1]))
                for n in range(0, len(parts), 2):
                    for side in range(2 - layer):
                        for i, (a, h, j, col) in parts[n:n + 2]:
                            rows = KEEP if layer == 0 and a == A2 else P
                            if side:
                                v = ONES[0:rows, :]
                            elif layer == 1:
                                v = VP[:, j, 2 * p + h, :]
                            elif a == A2:
                                v = VS[:, p % 3, h * VD:(h + 1) * VD]
                            else:
                                v = VV[:, p % 3, j, a, h * VD:(h + 1) * VD]
                            bank = OB[a if layer == 0 else p // 2 % 3]
                            row = 64 * (p % 2 if layer else side) + 32 * h
                            slot = (UNIT0[layer] + p * NU[layer] + i) % NP
                            last = mm(bank[row:row + 32, j * P:T], v, PR[0:rows, slot, col:col + T - j * P],
                                      start=(j == 0), stop=(j == 2 or a == A2), skip_group_check=True)
                last.then_inc(pv_done, 1)

            def transpose_tiles(use, src):
                ps, done = take(use, W)
                for t in range(NT):
                    last = nc.tensor.transpose(ps[:, t * P:(t + 1) * P], src(t), ID[:, :])
                last.then_inc(done, 1)

            proj_banks = []

            def add_group(ps, i, g):
                for tt in range(2):
                    t = 2 * i + tt
                    last = mm(ps[:, tt * C:(tt + 1) * C], OT[:, g, t * P:(t + 1) * P], WP[:, g, :],
                              start=(g == 0 and tt == 0), stop=(g == NG - 1 and tt == 1))
                return last

            def attention(layer):
                for s in STEPS[layer]:
                    if s[0] == "piece":
                        piece(s[1], s[2])
                    elif s[0] == "projection":
                        for i in range(2):
                            proj_banks.append(take(("proj", i), W))
                        for g in range(NG - 1):
                            was_read(pe, work, work_read, (0, "group", g))
                            for i in range(2):
                                add_group(proj_banks[i][0], i, g)
                    elif s[0] == "piece_tr":
                        piece_transposes(s[1], s[2])
                    elif s[0] == "max":
                        max_scores(layer, s[1], s[2])
                    elif s[0] == "mt":
                        transpose_maxima(layer, s[1])
                    elif s[0] == "unit":
                        unit(layer, s[1], s[2])
                    elif s[0] == "pv":
                        values(layer, s[1], s[2])
                    elif s[0] == "pro_pe":
                        prologue("next", s[1])
                    elif s[0] == "tail_pe":
                        tail("before", s[1])
                    elif s[0] == "out_tr":
                        n = 3 * s[1] + s[2] if layer == 0 else 3 * NPAIR + s[1]
                        pe.wait_ge(evacuated, n + 1)
                        transpose_tiles((layer,) + s, lambda t: OE[layer][:, s[2] if layer == 0 else s[1] % 2, t * P:(t + 1) * P])
                    elif s[0] == "group":
                        if layer == 0:
                            pe.wait_ge(summed, 2 * s[1] + 2)
                        else:
                            was_read(pe, work, work_read, (1, "out_tr", s[1], 0))
                        transpose_tiles((layer,) + s, lambda t: OROWS[layer][:, s[1] % 2, t, :])

            pe.wait_ge(early_loaded, EARLY_LOADED)
            pe.wait_ge(set_up, SET_UP)
            for j in range(6):
                prologue("first", j)
            pe.wait_ge(late_loaded, LATE_LOADED)
            for m in range(NPIECE):
                piece(0, m)
                piece_transposes(0, m)
            end_pass(pe, 1)
            with pe.Fori(0, B) as seq:
                attention(0)
                was_read(pe, work, work_read, (0, "group", NG - 1))
                for i, (ps, done) in enumerate(proj_banks):
                    add_group(ps, i, NG - 1).then_inc(done, 1)

                for i in range(2):
                    transpose_half(1, i)
                for s in FFN_STEPS:
                    if s[0] == "fc":
                        _, i, f2 = s
                        if f2 == 0:
                            was_read(pe, work, work_read, ("hT", 1, i))
                        ps, done = take(s, W)
                        for side in range(2):
                            f = 2 * f2 + side
                            for c in range(NC):
                                last = mm(ps[:, side * 256:(side + 1) * 256], WFC[:, c, f * P:(f + 1) * P],
                                          HT[:, c, i * 256:(i + 1) * 256], start=(c == 0), stop=(c == NC - 1))
                        last.then_inc(done, 1)
                    elif s[0] == "y":
                        i = s[1]
                        ps, done = take(s, W)
                        for tt in range(2):
                            for f in range(NF):
                                if tt == 0 and f % 2 == 0:
                                    pe.wait_ge(squared, NF // 2 * i + f // 2 + 1)
                                hidden = R2[:, NF // 2 * i + f // 2, (f % 2) * 256 + tt * P:(f % 2) * 256 + (tt + 1) * P]
                                last = mm(ps[:, tt * C:(tt + 1) * C], hidden, WFP[:, f, :],
                                          start=(f == 0), stop=(f == NF - 1))
                        last.then_inc(done, 1)
                    elif s[0] == "pro_pe":
                        prologue("next", s[1])

                def values_of_half(i):
                    ps, done = take(("v", i), W)
                    for tt in range(2):
                        t = 2 * i + tt
                        for c in range(NC):
                            last = mm(ps[:, tt * C:(tt + 1) * C], HT[:, c, t * P:(t + 1) * P],
                                      WQKV[:, c, 2 * C:3 * C], start=(c == 0), stop=(c == NC - 1))
                    last.then_inc(done, 1)

                def transpose_heads(t):
                    pe.wait_ge(stacked, 2 * (t + 1))
                    for n in range(4):
                        ps, done = take(("heads", t, n), W)
                        for g in range(4):
                            h = 2 * (4 * (n % 2) + g)
                            src = STACKS[t % 2][n // 2][:, h:h + 2, :, :].rearrange("p h s d -> p (h s d)")
                            last = nc.tensor.transpose(ps[:, g * P:(g + 1) * P], src, ID[:, :])
                        last.then_inc(done, 1)

                for what, n in QKV_STEPS:
                    if what == "half":
                        transpose_half(2, n)
                        was_read(pe, work, work_read, ("hT", 2, n))
                    elif what == "v":
                        values_of_half(n)
                    elif what == "heads":
                        transpose_heads(n)
                    else:
                        ps, done = take(("qk1", n), W)
                        for c in range(NC):
                            last = mm(ps[:, :], HT[:, c, n * P:(n + 1) * P], WQKV[:, c, 0:2 * C],
                                      start=(c == 0), stop=(c == NC - 1))
                        last.then_inc(done, 1)
                for t in range(NT):
                    for n in range(4):
                        was_read(pe, work, work_read, ("heads", t, n))
                for i in range(2):
                    was_read(pe, work, work_read, ("v", i))
                attention(1)
                end_pass(pe, seq + 2)
            for j in range(4):
                tail("last", j)

        @block.vector
        def _(dve):
            v = nc.vector
            steps = [0]

            def then(ins):
                steps[0] += 1
                ins.then_inc(dve_step, 1)
                dve.wait_ge(dve_step, steps[0])

            def read_work(ins, use):
                ins.then_inc(work_read[work.of[use][0]], 1)

            def rsqrt(i, n, c0=0):
                dve.wait_ge(pow_done, i + 1)
                na, y, var, rstd = (z[:, c0:c0 + n] for z in (NA, YP, VAR, RSTD))
                then(v.tensor_tensor(na, var, y, ALU.mult))
                then(v.tensor_tensor(na, na, y, ALU.mult))
                then(v.tensor_scalar(na, na, -0.5, 1.5, ALU.mult, ALU.add))
                then(v.tensor_tensor(rstd, na, y, ALU.mult))

            def variances(X, t0=0, n=NT):
                for t in range(t0, t0 + n):
                    ins = v.bn_stats(BN[:, t, :], X[:, t, :])
                then(ins)
                for t in range(t0, t0 + n):
                    ins = v.bn_aggr(MV[:, t, :], BN[:, t, :])
                then(ins)
                v.tensor_scalar(VAR[:, t0:t0 + n], MV[:, t0:t0 + n, 1], LN_EPS, None, ALU.add).then_inc(var_ready, 1)

            def normalised_rows(pow_index, X, t0=0, n=NT, dst=HN):
                rsqrt(pow_index, n, t0)
                for t in range(t0, t0 + n):
                    v.tensor_scalar(dst[:, t, :], X[:, t, :], MV[:, t, 0:1], RSTD[:, t:t + 1],
                                    ALU.subtract, ALU.mult).then_inc(h_ready, 1)

            def rope_products(ps4, cos, sin, a4, b4):
                one = v.tensor_tensor(a4, ps4, cos, ALU.mult)
                two = v.tensor_tensor(b4, ps4[:, :, ::-1, :], sin, ALU.mult)
                return one, two

            def piece(p, m):
                what, t = PIECES[m]
                if what == "nv":
                    return
                rows, heads = (KEEP, 2) if what == "sel" else (P, 4)
                ps = full(dve, ("piece", p, m), WORK)
                i = nth(p) * len(ROPED) + ROPED.index(m)
                last = piece_before(p, m, 2, ROPED)
                if last:
                    dve.wait_ge(tok_ready, nth(last[0]) * NPIECE + last[1] + 1)
                a4, b4 = ab(i, rows, heads, 32)
                src = ps[0:rows, 0:heads * D0].rearrange("p (h d) -> p h d", h=heads)[:, :, NOPE:D0]
                src = src.rearrange("p h (j d) -> p h j d", j=2)
                cos = COS0[0:rows, t:t + 1, :].unsqueeze(1).broadcast_to([rows, heads, 2, 32])
                sin = SIN0[0:rows, t:t + 1, :].rearrange("p a (j d) -> p a j d", j=2).broadcast_to([rows, heads, 2, 32])
                one, two = rope_products(src, cos, sin, a4, b4)
                read_work(one, ("piece", p, m))
                read_work(two, ("piece", p, m))

            def low_parts(p, m):
                use = ("piece_tr", p, m)
                k, _, _, r, _ = work.of[use]
                ps = full(dve, use, WORK)
                dve.wait_ge(work_read[k], r - 1)
                src, dst = transposed_heads(p, m, ps)
                read_work(v.tensor_tensor(dst[1], src, dst[0].bitcast(F32), ALU.subtract), use)

            def maxima(layer, p, i):
                u = MAX_UNITS[layer][i]
                ps = full(dve, (layer, "max", p, i), WORK)
                if i == 0 and layer * NPAIR + p >= 2:
                    full(dve, maxima_uses(*((layer, p - 2) if p >= 2 else (0, NPAIR - 2 + p)))[-1], WORK)
                for n, (lo, hi, att, h, qt) in enumerate(u["segs"]):
                    if att is None:
                        dst = NPART[:, h:h + 1]
                    else:
                        c = (att * 2 + h) * NT + qt
                        dst = NMX[:, p % 2, c:c + 1]
                    last = v.tensor_reduce(dst, ps[:, lo:hi], AX.X, ALU.max, negate=True)
                read_work(last, (layer, "max", p, i))
                if layer == 0 and i == len(MAX_UNITS[0]) - 1:
                    was_read(dve, work, work_read, (layer, "max", p, i))
                    c = NT - 1
                    dst = NMX[:, p % 2, c:c + NT + 1:NT]
                    v.tensor_tensor(dst, dst, NPART[:, :], ALU.min).then_inc(max_ready, 1)

            def normalise(layer, n, att):
                use = (layer, "out_tr", n, att)
                ps = full(dve, use, WORK)
                if layer == 0:
                    rows = ps[:, :].rearrange("p (t s h d) -> p t s h d", t=NT, s=2, h=2)
                    outputs, sums, heads, width = rows[:, :, 0, :, :], rows[:, :, 1, :, 0], 2, VD
                    dst = GATED[:, att, :, :, :]
                    if n and att == A1:
                        dve.wait_ge(summed, n)
                else:
                    outputs = ps[:, :].rearrange("p (t h d) -> p t h d", t=NT, d=DP)
                    sums, heads, width = outputs[:, :, :, D1], HG, DP
                    dst = OROWS[1][:, n % 2, :, :].rearrange("p t (h d) -> p t h d", h=HG)
                    if n >= 2:
                        full(dve, (1, "group", n - 2), WORK)
                rs = RSUM[:, att, :, 0:heads]
                then(v.reciprocal(rs, sums))
                if layer == 0:
                    g = 1 if att == A1 else 2 if att == A3 else 0
                    then(v.tensor_scalar(rs, rs, GG[:, g:g + 1], None, ALU.mult))
                read_work(v.tensor_tensor(dst, outputs, rs.unsqueeze(3).broadcast_to([P, NT, heads, width]), ALU.mult), use)

            def attention(layer, seq):
                for s in STEPS[layer]:
                    if s[0] == "piece":
                        piece(s[1], s[2])
                    elif s[0] == "piece_tr":
                        low_parts(s[1], s[2])
                    elif s[0] == "max":
                        maxima(layer, s[1], s[2])
                    elif s[0] == "norm":
                        normalise(layer, s[1], s[2])
                    elif s[0] == "pro":
                        prologue("next", s[1], 16 * seq + 32)
                    elif s[0] == "tail":
                        tail("before", s[1])

            def prologue(tag, j, loads):
                def filled(name):
                    return full(dve, (tag, name), WORK)

                def read(ins, name):
                    read_work(ins, (tag, name))

                def wait_read(name):
                    was_read(dve, work, work_read, (tag, name))

                if j == 0:
                    dve.wait_ge(x_loaded, loads)
                    variances(X0)
                elif j == 1:
                    normalised_rows(POW_AT[tag][0], X0, dst=HN0)
                elif j == 3:
                    wait_read("small0")
                    wait_read("small1")
                    sq = STATE[:, 1, 2, :].rearrange("p (t c) -> p t c", t=NT)
                    then(v.tensor_tensor(sq, SM[:, :, 0:P], SM[:, :, 0:P], ALU.mult))
                    v.tensor_reduce(NA[:, 0:NT], sq[:, :, 0:QL], AX.X, ALU.add)
                    then(v.tensor_reduce(NA[:, NT:2 * NT], sq[:, :, QL:P], AX.X, ALU.add))
                    then(v.tensor_scalar(VAR[:, 0:NT], NA[:, 0:NT], 1.0 / QL, RMS_EPS, ALU.mult, ALU.add))
                    v.tensor_scalar(VAR[:, NT:2 * NT], NA[:, NT:2 * NT], 1.0 / KVL, RMS_EPS, ALU.mult,
                                    ALU.add).then_inc(var_ready, 1)
                    kr_ab = [STATE[:, 1, 1, 256 * k:256 * (k + 1)].rearrange("p (t j d) -> p t j d", t=NT, j=2) for k in range(2)]
                    krs = SM[:, :, P:P + ROPE].rearrange("p t (j d) -> p t j d", j=2)
                    v.tensor_tensor(kr_ab[0], krs, COS0[:, :, :].unsqueeze(2).broadcast_to([P, NT, 2, 32]), ALU.mult)
                    v.tensor_tensor(kr_ab[1], krs[:, :, ::-1, :], SIN0[:, :, :].rearrange("p t (j d) -> p t j d", j=2),
                                    ALU.mult).then_inc(kr_products, 1)
                elif j == 4:
                    ps = filled("score_cols")
                    read(v.tensor_copy(SC[:, :], ps[:, ::P]), "score_cols")
                    ps = filled("gate")
                    read(v.tensor_copy(GS[:, :], ps[:, 0:3]), "gate")
                    rsqrt(POW_AT[tag][1], 2 * NT)
                    then(v.tensor_scalar(RSTD[:, 0:NT], RSTD[:, 0:NT], Q_SCALE, None, ALU.mult))
                    for t in range(NT):
                        v.scalar_tensor_tensor(NCK[:, t, 0:QL], SM[:, t, 0:QL], RSTD[:, t:t + 1], GQ[:, :],
                                               ALU.mult, ALU.mult).then_inc(latents_ready, 1)
                        v.scalar_tensor_tensor(NCK[:, t, QL:P], SM[:, t, QL:P], RSTD[:, NT + t:NT + t + 1], GK[:, :],
                                               ALU.mult, ALU.mult).then_inc(latents_ready, 1)
                elif j == 5:
                    ps = filled("ckvT")
                    read(v.tensor_copy(NQT[QL:P, :], ps[0:KVL, :]), "ckvT")
                    wait_read("gate")
                    v.tensor_reduce(GM[:, :], GS[:, :], AX.X, ALU.max, negate=True).then_inc(gate_in, 1)
                    wait_read("score_cols")
                    wait_read("imp")
                elif 6 <= j <= 9:
                    for t in (j - 6,):
                        then(v.tensor_scalar(AB[:, 0, :], ROW, SC[:, t:t + 1], None, ALU.is_gt, ALU.add,
                                             accum_out=CG[:, t:t + 1]))
                        then(v.scalar_tensor_tensor(AB[:, 0, :], ROW, SC[:, t:t + 1],
                                                    EARLY[:, (3 - t) * P:(3 - t) * P + T], ALU.is_equal, ALU.mult,
                                                    accum_out=CE[:, t:t + 1]))
                if j == 9:
                    then(v.tensor_tensor(CG[:, :], CG[:, :], CE[:, :], ALU.add))
                    then(v.tensor_scalar(MF[:, :], CG[:, :], KEEP - 0.5, None, ALU.is_lt))
                    v.tensor_copy(MB[:, :], MF[:, :]).then_inc(mask_ready, 1)
                elif j == 10:
                    ps = filled("pos")
                    read(v.tensor_copy(POS[:, :], ps[:, 0:NT]), "pos")
                    wait_read("pos")
                    for t in range(NT):
                        last = v.tensor_scalar(OH[:, t, :], RANKS[:, :], POS[:, t:t + 1], MF[:, t:t + 1],
                                               ALU.is_equal, ALU.mult)
                    last.then_inc(onehot_ready, 1)
                elif j == 11:
                    dve.wait_ge(gate_exp, 1)
                    then(v.reciprocal(GD[:, 1:2], GD[:, 0:1]))
                    then(v.tensor_scalar(GG[:, :], GE[:, :], GD[:, 1:2], None, ALU.mult))
                    ps = filled("selT")
                    read(v.tensor_copy(SELT[:, :, :], ps[:, 0:2 * KEEP].rearrange("p (c k) -> p c k", c=NC)), "selT")

            def add_half(use, i, src, dst):
                ps = full(dve, use, WORK)
                half = slice(2 * i, 2 * i + 2)
                read_work(v.tensor_tensor(dst[:, half, :], src[:, half, :],
                                          ps[:, :].rearrange("p (t c) -> p t c", t=2), ALU.add), use)
                was_read(dve, work, work_read, use)
                variances(dst, 2 * i, 2)

            def tail(tag, j):
                for i in range(2):
                    if j == 0:
                        add_half((tag, f"o{i}"), i, X2, X1)
                    elif j == 1:
                        normalised_rows(POW_AT[3][i], X1, 2 * i, 2)
                    elif j == 3:
                        ps = full(dve, (tag, f"sign{i}"), WORK)
                        read_work(v.tensor_tensor(X2[:, 2 * i:2 * i + 2, :], X1[:, 2 * i:2 * i + 2, :],
                                                  ps[:, :].rearrange("p (t c) -> p t c", t=2), ALU.add),
                                  (tag, f"sign{i}"))

            dve.wait_ge(early_loaded, EARLY_LOADED)
            v.tensor_copy(WI[:, :, :], WIMP[:, :].unsqueeze(2).broadcast_to([P, NC, P])).then_inc(set_up, 1)
            v.tensor_copy(IDB[:, :], ID[:, :]).then_inc(set_up, 1)
            v.tensor_copy(CAUSB[:, :], X2[:, 0, 0:P]).then_inc(set_up, 1)
            v.tensor_copy(BEFB[:, :], X2[:, 1, 0:P]).then_inc(set_up, 1)
            v.tensor_copy(CAUTB[:, :], X2[:, 2, 0:P]).then_inc(set_up, 1)
            v.memset(ONEB[:, :], 1.0).then_inc(set_up, 1)
            v.memset(MEANW[:, :], 1.0 / T).then_inc(set_up, 1)
            v.memset(MHALF[:, :], -0.5).then_inc(set_up, 1)
            v.tensor_scalar(WS[:, :, P:P + ROPE], WS[:, :, P:P + ROPE], 1.0 / H, None, ALU.mult).then_inc(set_up, 1)
            v.memset(ONES[:, :], 1.0).then_inc(set_up, 1)
            for h in range(2):
                for n in range(2):
                    v.memset(HEAD[64 * n:64 * n + 64, h:h + 1], float(n == h)).then_inc(set_up, 1)
            dve.wait_ge(set_up, SET_UP)
            v.memset(X2[:, :, :], 0.0)
            v.memset(OT[:, :, :], 0.0)
            for j in range(NPRO):
                prologue("first", j, 16)
            dve.wait_ge(late_loaded, LATE_LOADED)
            v.tensor_scalar(WQKV[:, :, 0:C], WQKV[:, :, 0:C], float(D1) ** -0.5, None, ALU.mult)
            for m in range(NPIECE):
                piece(0, m)
                low_parts(0, m)
            end_pass(dve, 1)
            steps[0] = 0
            with dve.Fori(0, B) as seq:
                attention(0, seq)
                for i in range(2):
                    add_half(("proj", i), i, X0, X1)
                for i in range(2):
                    normalised_rows(POW_AT[1][i], X1, 2 * i, 2)
                for j in range(2):
                    prologue("next", j, 16 * seq + 32)

                def keys_out(t):
                    for n in (2, 3):
                        ps = full(dve, ("heads", t, n), WORK)
                        read_work(v.tensor_copy(KB[:, 4 * (n - 2):4 * (n - 1), t * P:(t + 1) * P],
                                                ps[:, :].rearrange("p (g k) -> p g k", g=4)), ("heads", t, n))

                def rope(t):
                    ps = full(dve, ("qk1", t), WORK)
                    if t:
                        dve.wait_ge(roped1, t)
                    a4, b4 = ab(0, P, 2 * H, 8)
                    cos = COS1[:, t:t + 1, :].unsqueeze(1).broadcast_to([P, 2 * H, 2, 8])
                    sin = SIN1[:, t:t + 1, :].rearrange("p a (j d) -> p a j d", j=2).broadcast_to([P, 2 * H, 2, 8])
                    one, two = rope_products(ps[:, :].rearrange("p (h j d) -> p h j d", j=2, d=8), cos, sin, a4, b4)
                    read_work(one, ("qk1", t))
                    read_work(two, ("qk1", t))

                def spikes(i, between={}):
                    Y, NEGM, DRIVEN, SUM = (STATE[:, i, n, :] for n in range(4))
                    was_read(dve, work, work_read, ("y", i))
                    v.tensor_scalar(SUM, Y, 1.0, None, ALU.is_gt)
                    then(v.scalar_tensor_tensor(DRIVEN, Y, 0.9, Y, ALU.mult, ALU.add))
                    then(v.scalar_tensor_tensor(NEGM, Y, 1.0, DRIVEN, ALU.is_gt, ALU.subtract))
                    for step in range(3):
                        v.scalar_tensor_tensor(SUM, NEGM, -1.0, SUM, ALU.is_lt, ALU.add)
                        then(v.scalar_tensor_tensor(DRIVEN, NEGM, -0.9, Y, ALU.mult, ALU.add))
                        then(v.scalar_tensor_tensor(NEGM, NEGM, -1.0, DRIVEN, ALU.is_lt, ALU.subtract))
                        if step in between:
                            between[step]()
                    then(v.scalar_tensor_tensor(SUM, NEGM, -1.0, SUM, ALU.is_lt, ALU.add))
                    if i == 0:
                        dve.wait_ge(x_stored, 16 * seq + 16)
                    half = slice(2 * i, 2 * i + 2)
                    then(v.scalar_tensor_tensor(X2[:, half, :].rearrange("p t c -> p (t c)"), SUM, 0.2,
                                                X1[:, half, :].rearrange("p t c -> p (t c)"), ALU.mult, ALU.add))
                    variances(X2, 2 * i, 2)

                spikes(0)
                normalised_rows(POW_AT[2][0], X2, 0, 2)
                for j in (3, 4):
                    prologue("next", j, 16 * seq + 32)
                dve.wait_ge(kr_ready, 1)
                spikes(1, {0: lambda: (prologue("next", 5, 0), rope(0)), 1: lambda: rope(1)})
                normalised_rows(POW_AT[2][1], X2, 2, 2)
                keys_out(0)
                rope(2)
                rope(3)
                for t in range(1, NT):
                    keys_out(t)
                attention(1, seq)
                end_pass(dve, seq + 2)
            steps[0] = 0
            for j in range(4):
                tail("last", j)

        @block.scalar
        def _(act):
            a = nc.scalar

            def copy(dst, src):
                return a.activation(dst, src, ACT.Copy)

            def read_work(ins, use):
                ins.then_inc(work_read[work.of[use][0]], 1)

            def selecting_rows(par):
                for row, dst in ((A3, QW[par][0][D0:D0 + 3, 2:4, :]), (A2, K1[par][0][D0:D0 + 3, :, 0:KEEP]),
                                 (A1, K1[par][0][D0:D0 + 3, :, KEEP:])):
                    one = ID[D0:D0 + 3, D0 + row:D0 + row + 1].unsqueeze(2).broadcast_to(list(dst.shape))
                    copy(dst, one)

            def half_out(use, half):
                ps = full(act, use, WORK)
                read_work(copy(HT[:, :, half * 256:(half + 1) * 256], ps[:, :].rearrange("p (c k) -> p c k", c=NC)), use)

            def tail(tag, j):
                if j == 2:
                    for i in range(2):
                        half_out((tag, f"hT{i}"), i)

            def prologue(tag, j):
                copies = {2: [("hT0", HT0[:, 0, :], lambda ps: ps[:, :]), ("hT1", HT0[:, 1, :], lambda ps: ps[:, :])],
                          3: [(f"small{i}", SM[:, 2 * i:2 * i + 2, 0:SM_W],
                               lambda ps: ps[:, :].rearrange("p (t c) -> p t c", t=2)[:, :, 0:SM_W])
                              for i in range(2)] + [("imp", ROW, lambda ps: ps[:, :])],
                          5: [("nqT", NQT[0:QL, :], lambda ps: ps[0:QL, :])]}
                for name, dst, src in copies.get(j, []):
                    ps = full(act, (tag, name), WORK)
                    read_work(copy(dst, src(ps)), (tag, name))
                if j == 6:
                    act.wait_ge(gate_in, 1)
                    a.activation(GE[:, :], GS[:, :], ACT.Exp, bias=GM[:, 0:1], accum_out=GD[:, 0:1]).then_inc(gate_exp, 1)

            def piece(p, m):
                what, t = PIECES[m]
                rows, heads = (KEEP, 2) if what == "sel" else (P, 4)
                use = ("piece", p, m)
                ps = full(act, use, WORK)
                k, _, _, r, _ = work.of[use]
                if what != "nv":
                    act.wait_ge(work_read[k], r - 2)
                i = nth(p) * NPIECE + m
                last = piece_before(p, m, 4)
                if last:
                    full(act, ("piece_tr",) + last, WORK)
                if what == "nv":
                    both = ps[:, 0:2 * P].rearrange("p (t n) -> p t n", t=2)
                    src = both[:, :, 0:64].rearrange("p t (h d) -> p t h d", h=2)
                    dst = TOK[:, i % 4, :, 0:NOPE].rearrange("p (t h) d -> p t h d", t=2)
                    read_work(copy(dst, src), use)
                    read_work(copy(VV[:, p % NPAIR % 3, 2 * t:2 * t + 2, A1, :], both[:, :, 64:P]), use)
                else:
                    src = ps[0:rows, 0:heads * D0].rearrange("p (h d) -> p h d", h=heads)[:, :, 0:NOPE]
                    read_work(copy(TOK[0:rows, i % 4, 0:heads, 0:NOPE], src), use)
                    if what == "qk":
                        read_work(copy(VV[:, p % NPAIR % 3, t, A3, :], ps[:, 384:448]), use)
                    else:
                        read_work(copy(VS[:, p % NPAIR % 3, :], ps[0:KEEP, 192:256]), use)

            def high_parts(p, m):
                ps = full(act, ("piece_tr", p, m), WORK)
                src, dst = transposed_heads(p, m, ps)
                read_work(copy(dst[0], src), ("piece_tr", p, m))

            def maxima_out(layer, p):
                for h in range(2):
                    if layer == 0:
                        ps = full(act, (0, "mt", p, h), WORK)
                        read_work(copy(QW[p % 2][0][D0:D0 + 3, h, :], ps[0:3, :]), (0, "mt", p, h))
                    else:
                        ps = full(act, (1, "mt", p), WORK)
                        read_work(a.activation(QZ[2 * D1:2 * D1 + 2, p, h, :], ps[0:2, :], ACT.Copy,
                                               scale=ID[0:2, h:h + 1]), (1, "mt", p))

            def outputs(layer, n, att):
                if layer == 0:
                    act.wait_ge(pv_done, PV0[0] + n * NPV[0] + (6 if att == A2 else 5))
                    if n:
                        full(act, (0, "out_tr", n - 1, att), WORK)
                    copy(OE[0][:, att, :], OB[att][:, :]).then_inc(evacuated, 1)
                else:
                    act.wait_ge(pv_done, PV0[1] + 2 * (n + 1) * NPV[1])
                    if n >= 2:
                        full(act, (1, "out_tr", n - 2, 0), WORK)
                    copy(OE[1][:, n % 2, :], OB[n % 3][:, :]).then_inc(evacuated, 1)

            def group_out(layer, g):
                ps = full(act, (layer, "group", g), WORK)
                read_work(copy(OT[:, g, :], ps[:, :]), (layer, "group", g))

            def exponentials(layer, p, i):
                j = UNIT0[layer] + p * NU[layer] + i
                ps = full(act, (layer, "unit", p, i), WORK)
                if j >= NP:
                    act.wait_ge(pv_done, products_of(j - NP))
                rows = KEEP if layer == 0 and UNITS[0][i][0][0] == A2 else P
                a.activation(PR[0:rows, j % NP, :], ps[0:rows, :], ACT.Exp).then_inc(exp_ready, 1)

            def attention(layer):
                for s in STEPS[layer]:
                    if s[0] == "piece":
                        piece(s[1], s[2])
                    elif s[0] == "piece_tr":
                        high_parts(s[1], s[2])
                    elif s[0] == "mt_out":
                        maxima_out(layer, s[1])
                    elif s[0] == "unit":
                        exponentials(layer, s[1], s[2])
                    elif s[0] == "out":
                        outputs(layer, s[1], s[2])
                    elif s[0] == "group_out":
                        group_out(layer, s[1])
                    elif s[0] == "pro":
                        prologue("next", s[1])
                    elif s[0] == "tail":
                        tail("before", s[1])
                    elif s[0] == "rows":
                        selecting_rows(s[1])

            act.wait_ge(early_loaded, EARLY_LOADED)
            act.wait_ge(set_up, SET_UP)
            for j in range(NPRO):
                prologue("first", j)
            act.wait_ge(late_loaded, LATE_LOADED)
            a.activation(WSG[:, :, :], WSG[:, :, :], ACT.Sign)
            for m in range(NPIECE):
                piece(0, m)
                high_parts(0, m)
            end_pass(act, 1)
            with act.Fori(0, B) as seq:
                attention(0)
                for i in range(2):
                    half_out(("hT", 1, i), i)
                for s in FFN_STEPS:
                    if s[0] == "fc":
                        ps = full(act, s, WORK)
                        f = NF // 2 * s[1] + s[2]
                        if f >= 2:
                            act.wait_ge(squared, f - 1)
                        read_work(a.activation(AB[:, f % 2, :], ps[:, :], ACT.Relu), s)
                    elif s[0] == "y":
                        ps = full(act, s, WORK)
                        read_work(copy(STATE[:, s[1], 0, :], ps[:, :]), s)
                    elif s[0] == "pro":
                        prologue("next", s[1])

                def values_of_half(i):
                    if i == 0:
                        act.wait_ge(values_set, 1)
                    ps = full(act, ("v", i), WORK)
                    src = ps[:, :].rearrange("p (t h d) -> p t h d", t=2, d=D1)
                    read_work(copy(VP[:, 2 * i:2 * i + 2, :, 0:D1], src), ("v", i))

                def queries_out(t):
                    for n in range(2):
                        ps = full(act, ("heads", t, n), WORK)
                        for h in range(2):
                            read_work(a.activation(QZ[:, 4 * n:4 * n + 4, h, t * P:(t + 1) * P],
                                                   ps[:, :].rearrange("p (g k) -> p g k", g=4), ACT.Copy,
                                                   scale=HEAD[:, h:h + 1]), ("heads", t, n))

                def stack_high(t):
                    act.wait_ge(roped1, t + 1)
                    if t >= 2:
                        for n in range(4):
                            full(act, ("heads", t - 2, n), WORK)
                    q = ROPED1[:, t % 2, 0:H, :].unsqueeze(2).broadcast_to([P, H, 2, D1])
                    k = ROPED1[:, t % 2, H:2 * H, :].unsqueeze(2).broadcast_to([P, H, 2, D1])
                    copy(STACKS[t % 2][0][:, :, 0:4:3, :].bitcast(F32R), q).then_inc(stacked_hi, 1)
                    copy(STACKS[t % 2][1][:, :, 0:2, :].bitcast(F32R), k).then_inc(stacked_hi, 1)

                half_out(("hT", 2, 0), 0)
                stack_high(0)
                values_of_half(0)
                stack_high(1)
                queries_out(0)
                half_out(("hT", 2, 1), 1)
                values_of_half(1)
                for t in range(2, NT):
                    stack_high(t)
                    queries_out(t - 1)
                queries_out(NT - 1)
                attention(1)
                end_pass(act, seq + 2)
            tail("last", 2)

        @block.gpsimd
        def _(pool):
            gp = nc.gpsimd

            def power(i, n, c0=0):
                pool.wait_ge(var_ready, i + 1)
                gp.tensor_tensor(YP[:, c0:c0 + n], VAR[:, c0:c0 + n], MHALF[:, c0:c0 + n], ALU.pow).then_inc(pow_done, 1)

            def piece(p, m):
                what, t = PIECES[m]
                rows, heads = (KEEP, 2) if what == "sel" else (P, 4)
                i = nth(p) * NPIECE + m
                last = piece_before(p, m, 4)
                if last:
                    full(pool, ("piece_tr",) + last, WORK)
                dst = TOK[0:rows, i % 4, 0:heads, NOPE:D0]
                if what == "nv":
                    gp.tensor_copy(dst.rearrange("p (t h) d -> p t h d", t=2),
                                   KR[:, 2 * t:2 * t + 2, :].unsqueeze(2).broadcast_to([P, 2, 2, ROPE])).then_inc(tok_ready, 1)
                    return
                k, _, _, r, _ = work.of[("piece", p, m)]
                pool.wait_ge(work_read[k], r - 2)
                a4, b4 = ab(nth(p) * len(ROPED) + ROPED.index(m), rows, heads, 32)
                merge = "p h j d -> p h (j d)"
                gp.tensor_tensor(dst, a4.rearrange(merge), b4.rearrange(merge), ALU.add).then_inc(tok_ready, 1)

            def sum_attentions(p):
                was_read(pool, work, work_read, (0, "out_tr", p, A2))
                if p >= 4 and p % 2 == 0:
                    full(pool, (0, "group", p // 2 - 2), WORK)
                flat = [GATED[:, a, :, :, :].rearrange("p t h d -> p t (h d)") for a in range(3)]
                gp.tensor_tensor(flat[A1], flat[A1], flat[A3], ALU.add).then_inc(pool_step, 1)
                pool.wait_ge(pool_step, p + 1)
                gp.tensor_tensor(OROWS[0][:, p // 2 % 2, :, 64 * (p % 2):64 * (p % 2) + 64], flat[A1], flat[A2],
                                 ALU.add).then_inc(summed, 1)

            def prologue(tag, j):
                power(POW_AT[tag][j > 0], NT * (2 if j else 1))
                if j:
                    pool.wait_ge(kr_products, 1)
                    a, b = (STATE[:, 1, 1, 256 * k:256 * (k + 1)].rearrange("p (t d) -> p t d", t=NT) for k in range(2))
                    gp.tensor_tensor(KR[:, :, :], a, b, ALU.add).then_inc(kr_ready, 1)

            def tail(j):
                if j == 0:
                    for i in range(2):
                        power(POW_AT[3][i], 2, 2 * i)

            def attention(layer):
                for s in STEPS[layer]:
                    if s[0] == "piece":
                        piece(s[1], s[2])
                    elif s[0] == "norm" and layer == 0 and s[2] == A2:
                        sum_attentions(s[1])
                    elif s[0] == "tail":
                        tail(s[1])

            pool.wait_ge(set_up, SET_UP)
            for j in (0, 3):
                prologue("first", j)
            pool.wait_ge(kr_ready, 1)
            for m in range(NPIECE):
                piece(0, m)
            end_pass(pool, 1)
            with pool.Fori(0, B) as seq:
                attention(0)
                for i in range(2):
                    power(POW_AT[1][i], 2, 2 * i)
                prologue("next", 0)
                for s in FFN_STEPS:
                    if s[0] == "fc":
                        was_read(pool, work, work_read, s)
                        f = NF // 2 * s[1] + s[2]
                        gp.tensor_tensor(R2[:, f, :], AB[:, f % 2, :], AB[:, f % 2, :], ALU.mult).then_inc(squared, 1)
                        if f == 5:
                            power(POW_AT[2][0], 2)
                gp.memset(VP, 1.0).then_inc(values_set, 1)
                prologue("next", 3)
                for n, (q, k) in enumerate(STACKS):
                    for use in ((("next", "nqT"), ("next", "ckvT")), (("y", 1),))[n]:
                        full(pool, use, WORK)
                    gp.memset(q[:, :, 2, :], 0.0)
                    gp.memset(k[:, :, 2, 0:2], 1.0)
                    gp.memset(k[:, :, 2, 2:], 0.0)

                def stack_low(t):
                    pool.wait_ge(stacked_hi, 2 * (t + 1))
                    q, k = STACKS[t % 2]
                    gp.tensor_tensor(q[:, :, 1, :].bitcast(F32R), ROPED1[:, t % 2, 0:H, :], q[:, :, 0, :],
                                     ALU.subtract).then_inc(stacked, 1)
                    gp.tensor_tensor(k[:, :, 3, :].bitcast(F32R), ROPED1[:, t % 2, H:2 * H, :], k[:, :, 0, :],
                                     ALU.subtract).then_inc(stacked, 1)

                for t in range(NT):
                    was_read(pool, work, work_read, ("qk1", t))
                    if t >= 2:
                        pool.wait_ge(stacked, 2 * (t - 1))
                    gp.tensor_tensor(ROPED1[:, t % 2, :, :], AB[:, 0, :].rearrange("p (h d) -> p h d", d=D1),
                                     AB[:, 1, :].rearrange("p (h d) -> p h d", d=D1), ALU.add).then_inc(roped1, 1)
                    if t == 1:
                        power(POW_AT[2][1], 2, 2)
                    stack_low(t)
                pool.wait_ge(kr_ready, 1)
                attention(1)
                end_pass(pool, seq + 2)
            tail(0)


def head_cols(w, perm):
    rows = w.shape[0]
    return w.reshape(rows, H, -1)[:, :, perm].reshape(rows, -1)


def kernel(**inputs):
    import concourse.bacc as bacc
    from concourse.bass_utils import run_bass_kernel_spmd

    a = {k: np.asarray(v) for k, v in inputs.items()}
    L = lambda name: a["L0_attn_" + name]

    def halves(w):
        return np.ascontiguousarray(w.reshape(-1, P, w.shape[1]).transpose(1, 0, 2))

    q = np.concatenate([L("w_dq_nope").reshape(QL, H, NOPE), L("w_dq_rope").reshape(QL, H, ROPE)], 2).reshape(QL, -1)
    nv = np.concatenate([L("w_dk_nope").reshape(KVL, NPAIR, 64), L("w_dv").reshape(KVL, NPAIR, 64)], 2).reshape(KVL, -1)

    def paired(wk, wv):
        both = np.concatenate([wk.reshape(NC, P, NPAIR, 2 * D0), wv.reshape(NC, P, NPAIR, 2 * VD)], 3)
        return np.ascontiguousarray(both.transpose(2, 1, 0, 3))

    even_odd = np.concatenate([np.arange(0, D1, 2), np.arange(1, D1, 2)])
    wqkv = np.ascontiguousarray(a["L1_attn_W_qkv"].T)
    wqkv = np.concatenate([head_cols(wqkv[:, 0:C], even_odd), head_cols(wqkv[:, C:2 * C], even_odd), wqkv[:, 2 * C:]], 1)
    wo = np.zeros((H, DP, C), a["L1_attn_W_o"].dtype)
    wo[:, 0:D1, :] = a["L1_attn_W_o"].T.reshape(H, D1, C)
    arrays = dict(
        x=a["L0_attn_x"].reshape(B * T, C),
        w_small=halves(np.concatenate([L("w_cq"), L("w_ckv"), L("w_krope"), L("w_gate")[:, [1, 0, 2]]], 1)),
        w_imp=halves(L("w_imp"))[:, :, 0],
        w_q=q, w_nv=nv,
        w_kw=paired(L("w_wink"), L("w_winv")), w_sel=paired(L("w_selk"), L("w_selv")),
        w_proj=halves(L("w_proj")), g_q=L("g_qnorm"), g_kv=L("g_kvnorm"),
        w_fc=halves(a["L0_ffn_W_fc"].T), w_ffp=halves(a["L0_ffn_W_proj"].T),
        w_qkv=halves(wqkv), w_o=halves(wo.reshape(H * DP, C)), w_sign=halves(a["L1_ffn_weight"].T),
        **constants(),
    )
    nc = bacc.Bacc("TRN2", target_bir_lowering=False, num_devices=1)
    feed, args = {}, []
    for name in WEIGHT_NAMES + CONST_NAMES:
        arr = np.ascontiguousarray(arrays[name])
        feed[name + "_dram"] = arr
        args.append(nc.dram_tensor(name + "_dram", arr.shape, mybir.dt.from_np(arr.dtype), kind="ExternalInput").ap())
    args.append(nc.dram_tensor("out_dram", (B * T, C), F32, kind="ExternalOutput").ap())
    build_program(nc, *args)
    result = run_bass_kernel_spmd(nc, [feed], core_ids=[0])
    return result.results[0]["out_dram"].reshape(B, T, C)
```
